# Optimizing a Trainium2 kernel written in Bass

```python
import numpy as np
import jax
import jax.numpy as jnp

def _softmax(x, axis=-1):
    return jax.nn.softmax(x, axis=axis)

def _gelu(x):
    return jax.nn.gelu(x, approximate=True)

def _silu(x):
    return jax.nn.silu(x)

def _sigmoid(x):
    return jax.nn.sigmoid(x)

def _layernorm(x, axis=-1, eps=1e-05):
    m = jnp.mean(x, axis=axis, keepdims=True)
    v = jnp.var(x, axis=axis, keepdims=True)
    return (x - m) / jnp.sqrt(v + eps)

def _scatter_add(tgt, idx, src, axis=0):
    return tgt.at[idx].add(src)

def _segment_sum(src, seg, n):
    return jax.ops.segment_sum(src, seg, n)
kernel_name = 'mk_prb_d2_jaxref_r8_e03c52'

def setup_inputs(seed: int=0):
    np.random.seed(seed)
    _w = jnp.asarray

    def _L0_attn_setup():
        import jax, jax.numpy as jnp
        import numpy as np
        D_MODEL = 128
        N_HEADS = 16
        HEAD_DIM = D_MODEL // N_HEADS
        KV_LATENT = 32
        LN_EPS = 1e-05

        def apply_rope(x):
            b, h, t, d = x.shape
            half = d // 2
            pos = jnp.arange(t, dtype=x.dtype)[:, None]
            inv_freq = 1.0 / 10000.0 ** (jnp.arange(half, dtype=x.dtype) / half)
            angles = pos * inv_freq[None, :]
            sin = jnp.sin(angles)[None, None]
            cos = jnp.cos(angles)[None, None]
            x1, x2 = (x[..., :half], x[..., half:])
            return jnp.concatenate([x1 * cos - x2 * sin, x1 * sin + x2 * cos], axis=-1)
        key = jax.random.key(seed)
        ks = jax.random.split(key, 6)
        d, L = (D_MODEL, KV_LATENT)
        s = 1.0 / np.sqrt(d)
        sl = 1.0 / np.sqrt(L)
        return {'x': jax.random.normal(ks[0], (2, 256, d), dtype=jnp.float32), 'W_q': jax.random.uniform(ks[1], (d, d), jnp.float32, -s, s), 'W_dkv': jax.random.uniform(ks[2], (d, L), jnp.float32, -s, s), 'W_uk': jax.random.uniform(ks[3], (L, d), jnp.float32, -sl, sl), 'W_uv': jax.random.uniform(ks[4], (L, d), jnp.float32, -sl, sl), 'W_o': jax.random.uniform(ks[5], (d, d), jnp.float32, -s, s), 'ln_gamma': jnp.ones((L,), jnp.float32), 'ln_beta': jnp.zeros((L,), jnp.float32)}
    _L0_attn_in = _L0_attn_setup()

    def _L0_ffn_setup():
        import jax, jax.numpy as jnp
        import numpy as np
        B, S, D, E, K = (4, 256, 128, 8, 2)
        H = 4 * D
        key = jax.random.key(seed)
        ks = jax.random.split(key, 5)
        x = jax.random.normal(ks[0], (B, S, D), dtype=jnp.float32)
        Wg = jax.random.normal(ks[1], (D, E), dtype=jnp.float32) * (1.0 / np.sqrt(D))
        bg = jnp.zeros((E,), dtype=jnp.float32)
        W1 = jax.random.normal(ks[2], (E, D, H), dtype=jnp.float32) * (1.0 / np.sqrt(D))
        b1 = jnp.zeros((E, H), dtype=jnp.float32)
        W2 = jax.random.normal(ks[3], (E, H, D), dtype=jnp.float32) * (1.0 / np.sqrt(H))
        b2 = jnp.zeros((E, D), dtype=jnp.float32)
        return {'x': x, 'Wg': Wg, 'bg': bg, 'W1': W1, 'b1': b1, 'W2': W2, 'b2': b2}
    _L0_ffn_in = _L0_ffn_setup()

    def _L1_attn_setup():
        import jax, jax.numpy as jnp
        import numpy as np
        B, S, H, NH = (4, 128, 128, 16)
        HD = H // NH
        CAUSAL_HEADS = 4
        META_HEADS = NH // 4
        CAUSAL_W = 0.7
        META_W = (0.9 - 0.8) / 0.2 * 0.3

        def _mha(xq, xkv, Win, bi, Wout, bout, nh):
            b, sq, h = xq.shape
            sk = xkv.shape[1]
            hd = h // nh
            q = (xq @ Win[:, :h] + bi[:h]).reshape(b, sq, nh, hd).transpose(0, 2, 1, 3)
            k = (xkv @ Win[:, h:2 * h] + bi[h:2 * h]).reshape(b, sk, nh, hd).transpose(0, 2, 1, 3)
            v = (xkv @ Win[:, 2 * h:] + bi[2 * h:]).reshape(b, sk, nh, hd).transpose(0, 2, 1, 3)
            scores = jnp.einsum('bhqd,bhkd->bhqk', q, k) / jnp.sqrt(jnp.asarray(hd, q.dtype))
            probs = jax.nn.softmax(scores, axis=-1)
            ctx = jnp.einsum('bhqk,bhkd->bhqd', probs, v)
            return ctx.transpose(0, 2, 1, 3).reshape(b, sq, h) @ Wout + bout

        def _forward(hidden_states, cons_vec, Wq, bq, Wk, bk, Wv, bv, cg_W, cg_b, am_W, am_b, ca_Win, ca_bin, ca_Wout, ca_bout, mc_Win, mc_bin, mc_Wout, mc_bout, Wo, bo):
            b, s, h = hidden_states.shape
            q = (hidden_states @ Wq + bq).reshape(b, s, NH, HD).transpose(0, 2, 1, 3)
            k = (hidden_states @ Wk + bk).reshape(b, s, NH, HD).transpose(0, 2, 1, 3)
            v = (hidden_states @ Wv + bv).reshape(b, s, NH, HD).transpose(0, 2, 1, 3)
            scores = jnp.einsum('bhqd,bhkd->bhqk', q, k) / jnp.sqrt(jnp.asarray(HD, q.dtype))
            mod = jax.nn.sigmoid(hidden_states @ cg_W + cg_b + (cons_vec @ am_W + am_b))
            scores = scores * mod.transpose(0, 2, 1)[..., None]
            probs = jax.nn.softmax(scores, axis=-1)
            ctx = jnp.einsum('bhqk,bhkd->bhqd', probs, v).transpose(0, 2, 1, 3).reshape(b, s, h)
            causal_ctx = _mha(hidden_states, hidden_states, ca_Win, ca_bin, ca_Wout, ca_bout, CAUSAL_HEADS)
            ctx = ctx * (1.0 - CAUSAL_W) + causal_ctx * CAUSAL_W
            meta_ctx = _mha(ctx, ctx, mc_Win, mc_bin, mc_Wout, mc_bout, META_HEADS)
            ctx = ctx * (1.0 - META_W) + meta_ctx * META_W
            return ctx @ Wo + bo
        key = jax.random.key(seed)
        ks = jax.random.split(key, 16)
        sc = 0.02
        d = {'hidden_states': jax.random.normal(ks[0], (B, S, H), jnp.float32), 'cons_vec': jax.random.uniform(ks[1], (16,), jnp.float32), 'Wq': jax.random.normal(ks[2], (H, H), jnp.float32) * sc, 'bq': jnp.zeros((H,), jnp.float32), 'Wk': jax.random.normal(ks[3], (H, H), jnp.float32) * sc, 'bk': jnp.zeros((H,), jnp.float32), 'Wv': jax.random.normal(ks[4], (H, H), jnp.float32) * sc, 'bv': jnp.zeros((H,), jnp.float32), 'cg_W': jax.random.normal(ks[5], (H, NH), jnp.float32) * sc, 'cg_b': jnp.zeros((NH,), jnp.float32), 'am_W': jax.random.normal(ks[6], (16, NH), jnp.float32) * sc, 'am_b': jnp.zeros((NH,), jnp.float32), 'ca_Win': jax.random.normal(ks[7], (H, 3 * H), jnp.float32) * sc, 'ca_bin': jnp.zeros((3 * H,), jnp.float32), 'ca_Wout': jax.random.normal(ks[8], (H, H), jnp.float32) * sc, 'ca_bout': jnp.zeros((H,), jnp.float32), 'mc_Win': jax.random.normal(ks[9], (H, 3 * H), jnp.float32) * sc, 'mc_bin': jnp.zeros((3 * H,), jnp.float32), 'mc_Wout': jax.random.normal(ks[10], (H, H), jnp.float32) * sc, 'mc_bout': jnp.zeros((H,), jnp.float32), 'Wo': jax.random.normal(ks[11], (H, H), jnp.float32) * sc, 'bo': jnp.zeros((H,), jnp.float32)}
        return d
    _L1_attn_in = _L1_attn_setup()

    def _L1_ffn_setup():
        import jax, jax.numpy as jnp
        import numpy as np
        D_IN, D_HID = (128, 512)

        def _ternary(key, shape):
            return jax.random.randint(key, shape, -1, 2).astype(jnp.float32)

        def _tlin(x, w, s):
            return jnp.einsum('bsi,oi->bso', x, w) * s
        key = jax.random.key(seed)
        ks = jax.random.split(key, 12)
        inv = lambda fan: 1.0 / np.sqrt(fan).astype(np.float32)
        return {'x': jax.random.normal(ks[0], (4, 256, D_IN), dtype=jnp.float32), 'w1_w': _ternary(ks[1], (D_HID, D_IN)), 'w1_s': jax.random.uniform(ks[2], (D_HID,), dtype=jnp.float32) * inv(D_IN), 'w2_w': _ternary(ks[3], (D_HID, D_IN)), 'w2_s': jax.random.uniform(ks[4], (D_HID,), dtype=jnp.float32) * inv(D_IN), 'h1_w': _ternary(ks[5], (D_HID, D_HID)), 'h1_s': jax.random.uniform(ks[6], (D_HID,), dtype=jnp.float32) * inv(D_HID), 'h2_w': _ternary(ks[7], (D_HID, D_HID)), 'h2_s': jax.random.uniform(ks[8], (D_HID,), dtype=jnp.float32) * inv(D_HID), 'w3_w': _ternary(ks[9], (D_IN, D_HID)), 'w3_s': jax.random.uniform(ks[10], (D_IN,), dtype=jnp.float32) * inv(D_HID)}
    _L1_ffn_in = _L1_ffn_setup()
    _d = {'L0_attn_x': _L0_attn_in['x'], 'L0_attn_W_q': _L0_attn_in['W_q'], 'L0_attn_W_dkv': _L0_attn_in['W_dkv'], 'L0_attn_W_uk': _L0_attn_in['W_uk'], 'L0_attn_W_uv': _L0_attn_in['W_uv'], 'L0_attn_W_o': _L0_attn_in['W_o'], 'L0_attn_ln_gamma': _L0_attn_in['ln_gamma'], 'L0_attn_ln_beta': _L0_attn_in['ln_beta'], 'L0_ffn_Wg': _L0_ffn_in['Wg'], 'L0_ffn_bg': _L0_ffn_in['bg'], 'L0_ffn_W1': _L0_ffn_in['W1'], 'L0_ffn_b1': _L0_ffn_in['b1'], 'L0_ffn_W2': _L0_ffn_in['W2'], 'L0_ffn_b2': _L0_ffn_in['b2'], 'L1_attn_cons_vec': _L1_attn_in['cons_vec'], 'L1_attn_Wq': _L1_attn_in['Wq'], 'L1_attn_bq': _L1_attn_in['bq'], 'L1_attn_Wk': _L1_attn_in['Wk'], 'L1_attn_bk': _L1_attn_in['bk'], 'L1_attn_Wv': _L1_attn_in['Wv'], 'L1_attn_bv': _L1_attn_in['bv'], 'L1_attn_cg_W': _L1_attn_in['cg_W'], 'L1_attn_cg_b': _L1_attn_in['cg_b'], 'L1_attn_am_W': _L1_attn_in['am_W'], 'L1_attn_am_b': _L1_attn_in['am_b'], 'L1_attn_ca_Win': _L1_attn_in['ca_Win'], 'L1_attn_ca_bin': _L1_attn_in['ca_bin'], 'L1_attn_ca_Wout': _L1_attn_in['ca_Wout'], 'L1_attn_ca_bout': _L1_attn_in['ca_bout'], 'L1_attn_mc_Win': _L1_attn_in['mc_Win'], 'L1_attn_mc_bin': _L1_attn_in['mc_bin'], 'L1_attn_mc_Wout': _L1_attn_in['mc_Wout'], 'L1_attn_mc_bout': _L1_attn_in['mc_bout'], 'L1_attn_Wo': _L1_attn_in['Wo'], 'L1_attn_bo': _L1_attn_in['bo'], 'L1_ffn_w1_w': _L1_ffn_in['w1_w'], 'L1_ffn_w1_s': _L1_ffn_in['w1_s'], 'L1_ffn_w2_w': _L1_ffn_in['w2_w'], 'L1_ffn_w2_s': _L1_ffn_in['w2_s'], 'L1_ffn_h1_w': _L1_ffn_in['h1_w'], 'L1_ffn_h1_s': _L1_ffn_in['h1_s'], 'L1_ffn_h2_w': _L1_ffn_in['h2_w'], 'L1_ffn_h2_s': _L1_ffn_in['h2_s'], 'L1_ffn_w3_w': _L1_ffn_in['w3_w'], 'L1_ffn_w3_s': _L1_ffn_in['w3_s']}
    _x0 = _d['L0_attn_x']
    _d['L0_attn_x'] = jax.random.normal(jax.random.fold_in(jax.random.key(seed), 1), (8, 512, 128), dtype=_x0.dtype)
    del _x0
    return _d

def reference(L0_attn_x, L0_attn_W_q, L0_attn_W_dkv, L0_attn_W_uk, L0_attn_W_uv, L0_attn_W_o, L0_attn_ln_gamma, L0_attn_ln_beta, L0_ffn_Wg, L0_ffn_bg, L0_ffn_W1, L0_ffn_b1, L0_ffn_W2, L0_ffn_b2, L1_attn_cons_vec, L1_attn_Wq, L1_attn_bq, L1_attn_Wk, L1_attn_bk, L1_attn_Wv, L1_attn_bv, L1_attn_cg_W, L1_attn_cg_b, L1_attn_am_W, L1_attn_am_b, L1_attn_ca_Win, L1_attn_ca_bin, L1_attn_ca_Wout, L1_attn_ca_bout, L1_attn_mc_Win, L1_attn_mc_bin, L1_attn_mc_Wout, L1_attn_mc_bout, L1_attn_Wo, L1_attn_bo, L1_ffn_w1_w, L1_ffn_w1_s, L1_ffn_w2_w, L1_ffn_w2_s, L1_ffn_h1_w, L1_ffn_h1_s, L1_ffn_h2_w, L1_ffn_h2_s, L1_ffn_w3_w, L1_ffn_w3_s):

    def _L0_attn_ref(x, W_q, W_dkv, W_uk, W_uv, W_o, ln_gamma, ln_beta):
        import jax, jax.numpy as jnp
        import numpy as np
        D_MODEL = 128
        N_HEADS = 16
        HEAD_DIM = D_MODEL // N_HEADS
        KV_LATENT = 32
        LN_EPS = 1e-05

        def apply_rope(x):
            b, h, t, d = x.shape
            half = d // 2
            pos = jnp.arange(t, dtype=x.dtype)[:, None]
            inv_freq = 1.0 / 10000.0 ** (jnp.arange(half, dtype=x.dtype) / half)
            angles = pos * inv_freq[None, :]
            sin = jnp.sin(angles)[None, None]
            cos = jnp.cos(angles)[None, None]
            x1, x2 = (x[..., :half], x[..., half:])
            return jnp.concatenate([x1 * cos - x2 * sin, x1 * sin + x2 * cos], axis=-1)
        b, t, _ = x.shape
        q = (x @ W_q).reshape(b, t, N_HEADS, HEAD_DIM).transpose(0, 2, 1, 3)
        lat = x @ W_dkv
        mu = jnp.mean(lat, axis=-1, keepdims=True)
        var = jnp.mean(jnp.square(lat - mu), axis=-1, keepdims=True)
        lat = (lat - mu) * jax.lax.rsqrt(var + LN_EPS) * ln_gamma + ln_beta
        k = (lat @ W_uk).reshape(b, t, N_HEADS, HEAD_DIM).transpose(0, 2, 1, 3)
        v = (lat @ W_uv).reshape(b, t, N_HEADS, HEAD_DIM).transpose(0, 2, 1, 3)
        q = apply_rope(q)
        k = apply_rope(k)
        scores = jnp.einsum('bhqd,bhkd->bhqk', q, k) / jnp.sqrt(jnp.float32(HEAD_DIM))
        causal = jnp.tril(jnp.ones((t, t), dtype=bool))
        scores = jnp.where(causal[None, None], scores, -jnp.inf)
        attn = jax.nn.softmax(scores, axis=-1)
        out = jnp.einsum('bhqk,bhkd->bhqd', attn, v)
        out = out.transpose(0, 2, 1, 3).reshape(b, t, D_MODEL)
        return out @ W_o

    def _L0_ffn_ref(x, Wg, bg, W1, b1, W2, b2):
        import jax, jax.numpy as jnp
        import numpy as np
        B, S, D, E, K = (4, 256, 128, 8, 2)
        H = 4 * D
        logits = jnp.einsum('bsd,de->bse', x, Wg) + bg
        _, top_idx = jax.lax.top_k(logits, K)
        sel = jnp.sum(jax.nn.one_hot(top_idx, E, dtype=logits.dtype), axis=-2) > 0
        masked = jnp.where(sel, logits, -jnp.inf)
        gates = jax.nn.softmax(masked, axis=-1)
        out = jnp.zeros_like(x)
        for e in range(E):
            h = jax.nn.relu(jnp.einsum('bsd,dh->bsh', x, W1[e]) + b1[e])
            y = jnp.einsum('bsh,hd->bsd', h, W2[e]) + b2[e]
            out = out + gates[..., e:e + 1] * y
        return out

    def _L1_attn_ref(hidden_states, cons_vec, Wq, bq, Wk, bk, Wv, bv, cg_W, cg_b, am_W, am_b, ca_Win, ca_bin, ca_Wout, ca_bout, mc_Win, mc_bin, mc_Wout, mc_bout, Wo, bo):
        import jax, jax.numpy as jnp
        import numpy as np
        B, S, H, NH = (4, 128, 128, 16)
        HD = H // NH
        CAUSAL_HEADS = 4
        META_HEADS = NH // 4
        CAUSAL_W = 0.7
        META_W = (0.9 - 0.8) / 0.2 * 0.3

        def _mha(xq, xkv, Win, bi, Wout, bout, nh):
            b, sq, h = xq.shape
            sk = xkv.shape[1]
            hd = h // nh
            q = (xq @ Win[:, :h] + bi[:h]).reshape(b, sq, nh, hd).transpose(0, 2, 1, 3)
            k = (xkv @ Win[:, h:2 * h] + bi[h:2 * h]).reshape(b, sk, nh, hd).transpose(0, 2, 1, 3)
            v = (xkv @ Win[:, 2 * h:] + bi[2 * h:]).reshape(b, sk, nh, hd).transpose(0, 2, 1, 3)
            scores = jnp.einsum('bhqd,bhkd->bhqk', q, k) / jnp.sqrt(jnp.asarray(hd, q.dtype))
            probs = jax.nn.softmax(scores, axis=-1)
            ctx = jnp.einsum('bhqk,bhkd->bhqd', probs, v)
            return ctx.transpose(0, 2, 1, 3).reshape(b, sq, h) @ Wout + bout

        def _forward(hidden_states, cons_vec, Wq, bq, Wk, bk, Wv, bv, cg_W, cg_b, am_W, am_b, ca_Win, ca_bin, ca_Wout, ca_bout, mc_Win, mc_bin, mc_Wout, mc_bout, Wo, bo):
            b, s, h = hidden_states.shape
            q = (hidden_states @ Wq + bq).reshape(b, s, NH, HD).transpose(0, 2, 1, 3)
            k = (hidden_states @ Wk + bk).reshape(b, s, NH, HD).transpose(0, 2, 1, 3)
            v = (hidden_states @ Wv + bv).reshape(b, s, NH, HD).transpose(0, 2, 1, 3)
            scores = jnp.einsum('bhqd,bhkd->bhqk', q, k) / jnp.sqrt(jnp.asarray(HD, q.dtype))
            mod = jax.nn.sigmoid(hidden_states @ cg_W + cg_b + (cons_vec @ am_W + am_b))
            scores = scores * mod.transpose(0, 2, 1)[..., None]
            probs = jax.nn.softmax(scores, axis=-1)
            ctx = jnp.einsum('bhqk,bhkd->bhqd', probs, v).transpose(0, 2, 1, 3).reshape(b, s, h)
            causal_ctx = _mha(hidden_states, hidden_states, ca_Win, ca_bin, ca_Wout, ca_bout, CAUSAL_HEADS)
            ctx = ctx * (1.0 - CAUSAL_W) + causal_ctx * CAUSAL_W
            meta_ctx = _mha(ctx, ctx, mc_Win, mc_bin, mc_Wout, mc_bout, META_HEADS)
            ctx = ctx * (1.0 - META_W) + meta_ctx * META_W
            return ctx @ Wo + bo
        return _forward(hidden_states, cons_vec, Wq, bq, Wk, bk, Wv, bv, cg_W, cg_b, am_W, am_b, ca_Win, ca_bin, ca_Wout, ca_bout, mc_Win, mc_bin, mc_Wout, mc_bout, Wo, bo)

    def _L1_ffn_ref(x, w1_w, w1_s, w2_w, w2_s, h1_w, h1_s, h2_w, h2_s, w3_w, w3_s):
        import jax, jax.numpy as jnp
        import numpy as np
        D_IN, D_HID = (128, 512)

        def _ternary(key, shape):
            return jax.random.randint(key, shape, -1, 2).astype(jnp.float32)

        def _tlin(x, w, s):
            return jnp.einsum('bsi,oi->bso', x, w) * s
        h = jax.nn.silu(_tlin(x, w1_w, w1_s)) * _tlin(x, w2_w, w2_s)
        h = jax.nn.gelu(_tlin(h, h1_w, h1_s), approximate=False)
        h = jax.nn.gelu(_tlin(h, h2_w, h2_s), approximate=False)
        return _tlin(h, w3_w, w3_s)
    x = L0_attn_x
    xn = _layernorm(x, axis=-1)
    x = x + _L0_attn_ref(xn, L0_attn_W_q, L0_attn_W_dkv, L0_attn_W_uk, L0_attn_W_uv, L0_attn_W_o, L0_attn_ln_gamma, L0_attn_ln_beta) + _L0_ffn_ref(xn, L0_ffn_Wg, L0_ffn_bg, L0_ffn_W1, L0_ffn_b1, L0_ffn_W2, L0_ffn_b2)
    xn = _layernorm(x, axis=-1)
    x = x + _L1_attn_ref(xn, L1_attn_cons_vec, L1_attn_Wq, L1_attn_bq, L1_attn_Wk, L1_attn_bk, L1_attn_Wv, L1_attn_bv, L1_attn_cg_W, L1_attn_cg_b, L1_attn_am_W, L1_attn_am_b, L1_attn_ca_Win, L1_attn_ca_bin, L1_attn_ca_Wout, L1_attn_ca_bout, L1_attn_mc_Win, L1_attn_mc_bin, L1_attn_mc_Wout, L1_attn_mc_bout, L1_attn_Wo, L1_attn_bo) + _L1_ffn_ref(xn, L1_ffn_w1_w, L1_ffn_w1_s, L1_ffn_w2_w, L1_ffn_w2_s, L1_ffn_h1_w, L1_ffn_h1_s, L1_ffn_h2_w, L1_ffn_h2_s, L1_ffn_w3_w, L1_ffn_w3_s)
    return x

_drawn_inputs = setup_inputs


def setup_inputs(seed=0):
    import zlib

    import numpy as np

    out = dict(_drawn_inputs(seed))
    spreads = {'L0_attn_ln_gamma': (1.0, 0.2),
     'L0_attn_ln_beta': (0.0, 0.1),
     'L0_ffn_bg': (0.0, 0.1),
     'L0_ffn_b1': (0.0, 0.1),
     'L0_ffn_b2': (0.0, 0.1),
     'L1_attn_bq': (0.0, 0.1),
     'L1_attn_bk': (0.0, 0.1),
     'L1_attn_bv': (0.0, 0.1),
     'L1_attn_cg_b': (0.0, 0.1),
     'L1_attn_am_b': (0.0, 0.1),
     'L1_attn_ca_bin': (0.0, 0.1),
     'L1_attn_ca_bout': (0.0, 0.1),
     'L1_attn_mc_bin': (0.0, 0.1),
     'L1_attn_mc_bout': (0.0, 0.1),
     'L1_attn_bo': (0.0, 0.1)}
    factors = {}
    for name, (base, spread) in spreads.items():
        noise = np.random.default_rng([zlib.crc32(name.encode()), seed]).standard_normal(out[name].shape)
        drawn = base * np.exp(spread * noise) if base else spread * noise
        out[name] = jnp.asarray(drawn.astype(out[name].dtype))
    for name, factor in factors.items():
        out[name] = (out[name] * factor).astype(out[name].dtype)
    return out
```

```python
from contextlib import ExitStack

import numpy as np

import concourse.bass as bass
from concourse import mybir

P = 128
F32 = mybir.dt.float32
F16 = mybir.dt.float16
BF16 = mybir.dt.bfloat16
ACT = mybir.ActivationFunctionType
ALU = mybir.AluOpType
AX = mybir.AxisListType

B, T, D = 8, 512, 128
NC = T // P
NH, HD = 16, 8
NG, GH = 4, 4
MH, MD = 4, 32
E, HC = 8, 4
LAT = 32
EPS = 1e-5
CAUSAL_W = 0.7
META_W = (0.9 - 0.8) / 0.2 * 0.3

WIDE = [("l0_q", 128), ("l0_qr", 128), ("l0_o", 128), ("l1_q", 128), ("l1_k", 128), ("l1_v", 128),
        ("cg", 128), ("l1_o", 128), ("ca_q", 128), ("ca_k", 128), ("ca_v", 128), ("ca_o", 128),
        ("mc_q", 128), ("mc_k", 128), ("mc_v", 128), ("mc_o", 128), ("dkv", LAT), ("gate", E)]
COLS = [("bq", 1), ("bk", 1), ("ca_bq", 1), ("ca_bk", 1), ("mc_bq", 1), ("mc_bk", 1),
        ("ca_bo", 1), ("mc_bo", 1), ("cg_b", 1), ("am_b", 1), ("gamma", 1), ("beta", 1),
        ("b1", E * HC), ("s1", HC), ("s2", HC), ("hs1", HC), ("hs2", HC)]
ROWS = [("bv", 128), ("ca_bv", 128), ("mc_bv", 128), ("bo", 128), ("s3", 128), ("bg", E)]
CONST = [("ident", 128), ("mask", 128), ("maskT", 128), ("tri", E * E), ("cos", T), ("sin", T)]
SPLIT = [("W1", E * 512), ("W2", E * 512), ("F1", 512), ("F2", 512), ("G1", 2048), ("G2", 2048),
         ("F3", 512)]


def places(parts):
    at, out = 0, {}
    for name, n in parts:
        out[name] = (at, at + n)
        at += n
    return out, at


def constants():
    ident = np.eye(P, dtype=np.float32)
    q, k = np.arange(P)[:, None], np.arange(P)[None, :]
    mask = np.where(k > q, np.float32(-1e30), np.float32(0))
    e = np.arange(E)
    tri = np.broadcast_to((e[None, :] < e[:, None]).astype(np.float32).reshape(1, E * E), (P, E * E))
    half = HD // 2
    freq = (np.float32(1.0) / np.float32(10000.0) ** (np.arange(half, dtype=np.float32) / np.float32(half))).astype(np.float32)
    angle = (np.arange(T, dtype=np.float32)[:, None] * freq[None, :]).astype(np.float32)
    cos, sin = np.cos(angle).T, np.sin(angle).T
    cos_rows = np.tile(np.concatenate([cos, cos]), (NH, 1))
    sin_rows = np.tile(np.concatenate([-sin, sin]), (NH, 1))
    return np.ascontiguousarray(np.concatenate([ident, mask, mask.T, tri, cos_rows, sin_rows], axis=1), dtype=np.float32)


def build(nc, x_in, wide_in, lat_in, cols_in, rows_in, const_in, split_in, am_in, cons_in, b2_in, out):
    WIDE_AT, n_wide = places(WIDE)
    COLS_AT, n_cols = places(COLS)
    ROWS_AT, n_rows = places(ROWS)
    CONST_AT, n_const = places(CONST)
    SPLIT_AT, n_split = places(SPLIT)
    ctx = ExitStack()
    with ctx:
        def sb(name, shape, dt=F32):
            return ctx.enter_context(nc.sbuf_tensor(name, shape, dt))

        wide = sb("wide", [P, n_wide])
        latw = sb("latw", [LAT, 3 * 128])
        cols = sb("cols", [P, n_cols])
        rows = sb("rows", [P, n_rows])
        const = sb("const", [P, n_const])
        w_hi = sb("w_hi", [P, n_split], F16)
        w_lo = sb("w_lo", [P, n_split], F16)
        b2 = sb("b2", [E, 128])
        am = sb("am", [16, 128])
        cons = sb("cons", [16, 1])
        ident16 = sb("ident16", [P, P], F16)
        identb = sb("identb", [P, P], BF16)
        maskb = sb("maskb", [P, P], BF16)
        maskTb = sb("maskTb", [P, P], BF16)
        ones = sb("ones", [P, 32])
        neghalf = sb("neghalf", [P, NC])
        mod_bias = sb("mod_bias", [P, 1])
        neg_s1 = sb("neg_s1", [P, HC])
        ca_bo7 = sb("ca_bo7", [P, 1])
        mc_bo15 = sb("mc_bo15", [P, 1])

        def W(name):
            a, b = WIDE_AT[name]
            return wide[:, a:b]

        def V(name, i=0, n=P):
            a, _ = COLS_AT[name]
            return cols[0:n, a + i:a + i + 1]

        def R(name):
            a, b = ROWS_AT[name]
            return rows[:, a:b]

        def C(name):
            a, b = CONST_AT[name]
            return const[:, a:b]

        def part(w, name, i, n):
            a, _ = SPLIT_AT[name]
            return w[:, a + i * n:a + (i + 1) * n]

        x = sb("x", [P, NC, D])
        xn = sb("xn", [P, NC, D])
        xT = sb("xT", [P, T])
        xh = sb("xh", [P, T], F16)
        xl = sb("xl", [P, T], F16)
        stats = sb("stats", [P, NC, 6])
        mv = sb("mv", [P, NC, 2])
        ve = sb("ve", [P, NC])
        rstd = sb("rstd", [P, NC])
        latn = sb("latn", [P, NC, LAT])
        latT = sb("latT", [LAT, T])
        t_a = sb("t_a", [P, T])
        t_b = sb("t_b", [P, T])
        q32 = sb("q32", [P, T])
        k32 = sb("k32", [P, T])
        q_hi = sb("q_hi", [P, T], F16)
        q_lo = sb("q_lo", [P, T], F16)
        k_hi = sb("k_hi", [P, T], F16)
        k_lo = sb("k_lo", [P, T], F16)
        qs = sb("qs", [P, NG, T], F16)
        qm = sb("qm", [P, NG, T], F16)
        kp = sb("kp", [P, NH, T], F16)
        vp = sb("vp", [P, NC, NH, 32])
        qc = sb("qc", [P, MH, T], F16)
        kc = sb("kc", [P, MH, T], F16)
        vc = sb("vc", [P, NC, D])
        negmax = sb("negmax", [P, NG + 2, NC, GH], F16)
        mrow = sb("mrow", [GH, 2, T], F16)
        probs = sb("probs", [P, 2, GH, T])
        osb = sb("osb", [P, NG, T])
        rden = sb("rden", [P, NC, NH])
        onorm = sb("onorm", [P, NC, NH, HD])
        oT = sb("oT", [P, T])
        oc = sb("oc", [P, T])
        ctxT = sb("ctxT", [P, T])
        h_hi = sb("h_hi", [P, 2, HC, T], F16)
        h_lo = sb("h_lo", [P, 2, HC, T], F16)
        h32 = sb("h32", [P, HC, T])
        lg = sb("lg", [P, NC, E])
        gex = sb("gex", [P, NC, E])
        gmax = sb("gmax", [P, NC])
        gsum = sb("gsum", [P, NC])
        gates = sb("gates", [P, NC, E])
        cmp1 = sb("cmp1", [P, NC, E, E])
        cmp2 = sb("cmp2", [P, NC, E, E])
        gT = sb("gT", [E, T])

        psum = ctx.enter_context(nc.psum_tensor("banks", [P, 8, 512], F32))
        SCO, TRA, OUT, MIS, UP, DN = 0, 2, 4, 5, 6, 7

        sems = {}

        def sem(name):
            if name not in sems:
                sems[name] = ctx.enter_context(nc.semaphore(name))
            return sems[name]

        stage = probs[:, :, :, :].rearrange("p a g t -> p (a g t)")
        s_in, s_stage, s_split, s_free, s_set, s_am, s_one, s_zero, s_rows = (
            ctx.enter_context(nc.semaphore(n)) for n in ("s_in", "s_stage", "s_split", "s_free", "s_set", "s_am", "s_one", "s_zero", "s_rows"))

        LOADS = [(SPLIT_AT["W1"][0], 4096), (SPLIT_AT["W2"][0], 4096), (SPLIT_AT["F1"][0], 3072), (SPLIT_AT["G2"][0], 2560)]

        with nc.Block() as block:
            @block.sync
            def _(sp):
                for dst, src in ((const, const_in), (wide, wide_in), (cols, cols_in), (latw, lat_in),
                                 (b2, b2_in), (am, am_in), (cons, cons_in)):
                    sp.dma_start(dst[:, :], src).then_inc(s_in, 16)
                sp.dma_start(rows[:, :], rows_in.broadcast_to([P, n_rows])).then_inc(s_in, 16)
                for n, (a, w) in enumerate(LOADS):
                    if n:
                        sp.wait_ge(s_free, n)
                    sp.dma_start(stage[:, 0:w], split_in[:, a:a + w]).then_inc(s_stage, 16)
                    if n == 0:
                        sp.wait_ge(s_one, 1)
                        sp.wait_ge(s_zero, 1)
                        for h in range(NH):
                            r = 32 * (h % GH) + 3
                            sp.dma_start(kp[r:r + 1, h, :], kc[0:1, 0, :]).then_inc(s_rows, 16)
                sp.wait_ge(s_rows, 16 * NH)

            @block.scalar
            def _(act):
                for n, (a, w) in enumerate(LOADS):
                    act.wait_ge(s_stage, 16 * (n + 1))
                    nc.scalar.activation(w_hi[:, a:a + w], stage[:, 0:w], ACT.Copy).then_inc(s_split, 1)

            @block.vector
            def _(dve):
                nc.vector.memset(ones[:, :], 1.0)
                nc.vector.memset(neghalf[:, :], -0.5)
                nc.vector.memset(qs[:, :, :], 0.0)
                nc.vector.memset(kc[:, :, :], 1.0).then_inc(s_one, 1)
                dve.wait_ge(s_in, 8 * 16)
                nc.vector.tensor_copy(ident16[:, :], C("ident"))
                nc.vector.tensor_copy(identb[:, :], C("ident"))
                nc.vector.tensor_copy(maskb[:, :], C("mask"))
                nc.vector.tensor_copy(maskTb[:, :], C("maskT"))
                nc.vector.tensor_scalar(ca_bo7[:, :], V("ca_bo"), CAUSAL_W, None, ALU.mult)
                nc.vector.tensor_scalar(neg_s1[:, :], cols[:, COLS_AT["s1"][0]:COLS_AT["s1"][1]], -1.0, None, ALU.mult)
                nc.vector.tensor_scalar(mc_bo15[:, :], V("mc_bo"), META_W, None, ALU.mult)
                nc.vector.tensor_tensor(out=t_a[:, 0:1], in0=V("cg_b"), in1=V("am_b"), op=ALU.add).then_inc(s_set, 1)
                dve.wait_ge(s_set, 1)
                dve.wait_ge(s_am, 1)
                nc.vector.tensor_tensor(out=t_b[:, 0:1], in0=psum[:, 0, 0:1], in1=t_a[:, 0:1], op=ALU.add).then_inc(s_set, 1)
                dve.wait_ge(s_set, 2)
                nc.vector.tensor_scalar(mod_bias[:, :], t_b[:, 0:1], -1.0, None, ALU.mult)
                for n, (a, w) in enumerate(LOADS):
                    dve.wait_ge(s_split, n + 1)
                    nc.vector.tensor_tensor(out=w_lo[:, a:a + w], in0=stage[:, 0:w], in1=w_hi[:, a:a + w],
                                            op=ALU.subtract).then_inc(s_free, 1)

            @block.tensor
            def _(pe):
                pe.wait_ge(s_in, 8 * 16)
                nc.tensor.matmul(psum[:, 0, 0:1], am[:, :], cons[:, :], start=True, stop=True).then_inc(s_am, 1)

            @block.gpsimd
            def _(pool):
                nc.gpsimd.memset(kp[:, :, :], 0.0).then_inc(s_zero, 1)
                nc.gpsimd.memset(vp[:, :, :, :], 0.0).then_inc(s_zero, 1)
                nc.gpsimd.memset(qm[:, :, :], 0.0)
                pool.wait_ge(s_zero, 2)
                nc.gpsimd.memset(vp[:, :, :, HD:HD + 1], 1.0)

        LAG = 12
        NS = {0: 32, 1: 40, 2: 8}
        SCALE = {True: float(HD) ** -0.5, False: float(MD) ** -0.5}
        U = 8

        def main(st, gr):
            return st < 2 and gr < NG

        def width(st, c):
            return (P * (c + 1), P * c) if st == 0 else (T, 0)

        with nc.Fori(0, B) as i:
            with nc.Block() as block:
                @block.tensor
                def _(pe):
                    def mm(bank, cols_, lhsT, rhs, start, stop, rows_=slice(0, P), skip=False):
                        return nc.tensor.matmul(psum[rows_, bank, cols_], lhsT, rhs, start=start, stop=stop,
                                                skip_group_check=skip)

                    def transpose_x(L):
                        pe.wait_ge(sem(f"xn{L}"), 1)
                        for c in range(NC):
                            last = nc.tensor.transpose(psum[:, MIS, c * P:(c + 1) * P], xn[:, c, :], C("ident"))
                        last.then_inc(sem(f"xT_ps{L}"), 1)
                        pe.wait_ge(sem(f"xT{L}"), 1)

                    def project(bank, w, rhs, name):
                        mm(bank, slice(0, T), w, rhs, True, True).then_inc(sem(name), 1)

                    def values(bank, lhs, w, name, k=P):
                        for c in range(NC):
                            last = mm(bank, slice(c * P, (c + 1) * P), lhs[0:k, c * P:(c + 1) * P], w, True, True)
                        last.then_inc(sem(name), 1)

                    def three(bank, cols_, parts):
                        n = 3 * len(parts)
                        j = 0
                        for (a_hi, a_lo, b_hi, b_lo) in parts:
                            for a, b in ((a_hi, b_hi), (a_hi, b_lo), (a_lo, b_hi)):
                                last = mm(bank, cols_, a, b, j == 0, j == n - 1)
                                j += 1
                        return last

                    def score_unit(st, u):
                        gr, c, pair = u // U, (u % U) // 2, u % 2
                        if u:
                            pe.wait_ge(sem(f"max{st}"), u)
                        if st == 1 and u == U * NG:
                            pe.wait_ge(sem("spread3"), 16 * 24)
                        kw, _ = width(st, c)
                        for s in range(2):
                            g = 2 * pair + s
                            if main(st, gr):
                                lhsT, rhs = qs[:, gr, c * P:(c + 1) * P], kp[:, GH * gr + g, 0:kw]
                            else:
                                lhsT, rhs = qc[0:96, g, c * P:(c + 1) * P], kc[0:96, g, 0:kw]
                            last = mm(SCO + s, slice(0, kw), lhsT, rhs, True, st != 0)
                            if st == 0:
                                last = mm(SCO + s, slice(kw - P, kw), identb[:, :], maskb[:, :], False, True)
                        last.then_inc(sem(f"score{st}"), 1)

                    def max_rows(st, gr):
                        pe.wait_ge(sem(f"max{st}"), U * (gr + 1))
                        if gr:
                            pe.wait_ge(sem(f"mrow{st}"), gr)
                        for c in range(NC):
                            last = mm(MIS, slice(c * P, (c + 1) * P), negmax[:, gr, c, :], ident16[:, :], True, True,
                                      rows_=slice(0, GH))
                        last.then_inc(sem(f"mrow_ps{st}"), 1)

                    def trans_unit(st, u):
                        gr, c, pair = u // U, (u % U) // 2, u % 2
                        if u % U == 0:
                            pe.wait_ge(sem(f"qm{st}_{gr}"), 16 * (1 if main(st, gr) else MH))
                        if u:
                            pe.wait_ge(sem(f"exp{st}"), u)
                        _, q0 = width(st, c)
                        for s in range(2):
                            g = 2 * pair + s
                            if main(st, gr):
                                lhsT, rhs = kp[:, GH * gr + g, c * P:(c + 1) * P], qm[:, gr, q0:T]
                            else:
                                lhsT, rhs = kc[0:97, g, c * P:(c + 1) * P], qc[0:97, g, q0:T]
                            last = mm(TRA + s, slice(q0, T), lhsT, rhs, True, st != 0)
                            if st == 0:
                                last = mm(TRA + s, slice(q0, q0 + P), identb[:, :], maskTb[:, :], False, True)
                        last.then_inc(sem(f"trans{st}"), 1)

                    def value_step(st, kk):
                        gr, c = kk // NC, kk % NC
                        pe.wait_ge(sem(f"exp{st}"), 2 * kk + 2)
                        if c == 0:
                            if gr:
                                pe.wait_ge(sem(f"osb{st}"), gr)
                            if st == 1 and gr == NG:
                                pe.wait_ge(sem("h32_1"), HC)
                        _, q0 = width(st, c)
                        for g in range(GH):
                            r = slice(32 * g, 32 * g + 32)
                            if main(st, gr):
                                lhsT = vp[:, c, GH * gr + g, :]
                            else:
                                lhsT = vc[:, c, MD * g:MD * (g + 1)]
                            last = mm(OUT, slice(q0, T), lhsT, probs[:, kk % 2, g, q0:T], c == 0, c == NC - 1, rows_=r)
                        if not main(st, gr):
                            for g in range(GH):
                                r = slice(32 * g, 32 * g + 32)
                                last = mm(DN, slice(q0, T), ones[:, :], probs[:, kk % 2, g, q0:T], c == 0, c == NC - 1, rows_=r)
                        last.then_inc(sem(f"pv{st}"), 1)

                    def attention(st, pieces):
                        n = NS[st]
                        slots = n + LAG + 3
                        done = 0
                        for s in range(slots):
                            if s < n:
                                score_unit(st, s)
                            want = -(-len(pieces) * (s + 1) // slots)
                            while done < (done + want + 1) // 2:
                                pieces[done][0](*pieces[done][1])
                                done += 1
                            if s % U == 1 and 0 < s <= n + 1:
                                max_rows(st, s // U - 1) if s >= U else None
                            if LAG <= s < n + LAG:
                                trans_unit(st, s - LAG)
                            while done < want:
                                pieces[done][0](*pieces[done][1])
                                done += 1
                            k = s - LAG - 2
                            if k > 0 and k % 2 == 1 and k // 2 < n // 2:
                                value_step(st, k // 2)

                    transpose_x(0)
                    for c in range(NC):
                        last = mm(DN, slice(LAT * c, LAT * c + LAT), xT[:, c * P:(c + 1) * P], W("dkv"), True, True)
                    last.then_inc(sem("lat_ps"), 1)
                    project(0, W("l0_q"), xT[:, :], "q_ps0")
                    project(1, W("l0_qr"), xT[:, :], "q_ps0")
                    for c in range(NC):
                        last = mm(2, slice(E * c, E * c + E), xT[:, c * P:(c + 1) * P], W("gate"), True, True)
                    last.then_inc(sem("lg_ps"), 1)

                    def up0(e, hc):
                        n = e * HC + hc
                        if n == 0:
                            pe.wait_ge(sem("xsplit0"), 1)
                        else:
                            pe.wait_ge(sem("relu"), n)
                        three(UP, slice(0, T), [(part(w_hi, "W1", n, P), part(w_lo, "W1", n, P), xh[:, :], xl[:, :])]) \
                            .then_inc(sem("up0"), 1)

                    def down0(e, c):
                        if c == 0:
                            pe.wait_ge(sem("h_lo0"), HC * (e + 1))
                            if e:
                                pe.wait_ge(sem("acc0"), e)
                            else:
                                pe.wait_ge(sem("latn"), 1)
                        t = slice(c * P, (c + 1) * P)
                        last = three(DN, t, [(h_hi[:, e % 2, hc, t], h_lo[:, e % 2, hc, t],
                                              part(w_hi, "W2", e * HC + hc, P), part(w_lo, "W2", e * HC + hc, P))
                                             for hc in range(HC)])
                        if c == NC - 1:
                            last.then_inc(sem("down0"), 1)

                    pieces = []
                    for e in range(E + 1):
                        for hc in range(HC):
                            if e < E:
                                pieces.append((up0, (e, hc)))
                            if e:
                                pieces.append((down0, (e - 1, hc)))
                    for f, a in pieces[:2]:
                        f(*a)
                    pe.wait_ge(sem("latn"), 1)
                    for c in range(NC):
                        last = nc.tensor.transpose(psum[0:LAT, 3, c * P:(c + 1) * P], latn[:, c, :], C("ident"))
                    last.then_inc(sem("latT_ps"), 1)
                    for f, a in pieces[2:4]:
                        f(*a)
                    pe.wait_ge(sem("latT"), 1)
                    pe.wait_ge(sem("rope_q"), 1)
                    project(0, latw[:, 0:128], latT[:, :], "k_ps0")
                    project(1, latw[:, 128:256], latT[:, :], "k_ps0")
                    values(MIS, latT, latw[:, 256:384], "v_ps0", k=LAT)
                    for f, a in pieces[4:12]:
                        f(*a)
                    pe.wait_ge(sem("spread0"), 16 * (24 + 48))
                    pe.wait_ge(sem("rope_k"), 1)
                    pe.wait_ge(sem("lg"), 1)
                    pe.wait_ge(sem("vp0"), 1)
                    attention(0, pieces[12:])

                    def finish_heads(L):
                        pe.wait_ge(sem(f"osb{L}"), NG)
                        for c in range(NC):
                            for gr in range(NG):
                                last = nc.tensor.transpose(psum[:, c, gr * P:(gr + 1) * P],
                                                           osb[:, gr, c * P:(c + 1) * P], C("ident"))
                            last.then_inc(sem(f"oq_ps{L}"), 1)
                        for c in range(NC):
                            pe.wait_ge(sem(f"onorm{L}"), c + 1)
                            last = nc.tensor.transpose(psum[:, MIS, c * P:(c + 1) * P],
                                                       onorm[:, c, :, :].rearrange("p h d -> p (h d)"), C("ident"))
                        last.then_inc(sem(f"oT_ps{L}"), 1)
                        pe.wait_ge(sem(f"oT{L}"), 1)

                    finish_heads(0)
                    pe.wait_ge(sem("gates"), 1)
                    for c in range(NC):
                        last = nc.tensor.transpose(psum[0:E, UP, c * P:(c + 1) * P], gates[:, c, :], C("ident"))
                    last.then_inc(sem("gT_ps"), 1)
                    pe.wait_ge(sem("gT"), 1)
                    for c in range(NC):
                        t = slice(c * P, (c + 1) * P)
                        mm(0, t, oT[:, t], W("l0_o"), True, False)
                        last = mm(0, t, gT[:, t], b2[:, :], False, True)
                    last.then_inc(sem("attn0"), 1)

                    transpose_x(1)
                    pe.wait_ge(sem("xin1"), 1)
                    project(0, W("l1_q"), xT[:, :], "q_ps1")
                    project(1, W("cg"), xT[:, :], "mod_ps")
                    project(2, W("l1_k"), xT[:, :], "k_ps1")
                    project(3, W("ca_q"), xT[:, :], "caq_ps")
                    project(4, W("ca_k"), xT[:, :], "cak_ps")
                    values(5, xT, W("l1_v"), "v_ps1")
                    values(7, xT, W("ca_v"), "cav_ps")

                    def gate1(o):
                        if o == 0:
                            pe.wait_ge(sem("xsplit1"), 1)
                            pe.wait_ge(sem("vc1"), 1)
                        else:
                            pe.wait_ge(sem("h32_1"), o)
                        three(UP, slice(0, T), [(part(w_hi, "F1", o, P), part(w_lo, "F1", o, P), xh[:, :], xl[:, :])]) \
                            .then_inc(sem("g1a"), 1)
                        three(DN, slice(0, T), [(part(w_hi, "F2", o, P), part(w_lo, "F2", o, P), xh[:, :], xl[:, :])]) \
                            .then_inc(sem("g1b"), 1)

                    def hidden(n, o, ic, name, src):
                        if ic == 0:
                            if o == 0:
                                pe.wait_ge(sem(f"hsplit{n}"), 1)
                            if n == 1 and o == 0:
                                pe.wait_ge(sem("h32_1"), HC)
                            else:
                                pe.wait_ge(sem("up_free"), HC * (n - 1) + o)
                        for j, (a, b) in enumerate(((w_hi, h_hi), (w_hi, h_lo), (w_lo, h_hi))):
                            wa, _ = SPLIT_AT[name]
                            last = mm(UP, slice(0, T), a[:, wa + ic * 512 + o * P:wa + ic * 512 + (o + 1) * P],
                                      b[:, src, ic, :], ic == 0 and j == 0, ic == HC - 1 and j == 2)
                        if ic == HC - 1:
                            last.then_inc(sem(f"hid{n}"), 1)

                    gate1(0)
                    pe.wait_ge(sem("spread1"), 16 * (24 + 48))
                    for name in ("q_out1", "mod_e", "k32_1", "caq32", "cak32", "vp1"):
                        pe.wait_ge(sem(name), 1)
                    attention(1, [(gate1, (o,)) for o in range(1, HC)]
                              + [(hidden, (1, o, ic, "G1", 0)) for o in range(HC) for ic in range(HC)])
                    finish_heads(1)
                    pe.wait_ge(sem("oc1"), 1)
                    project(OUT, W("ca_o"), oc[:, :], "mix_ps1")
                    pe.wait_ge(sem("ctx"), 1)
                    pe.wait_ge(sem("onorm1"), NC)
                    project(0, W("mc_q"), ctxT[:, :], "mcq_ps")
                    project(1, W("mc_k"), ctxT[:, :], "mck_ps")
                    values(2, ctxT, W("mc_v"), "mcv_ps")
                    hid2 = [(hidden, (2, o, ic, "G2", 1)) for o in range(HC) for ic in range(HC)]
                    for f, a in hid2[:4]:
                        f(*a)
                    pe.wait_ge(sem("spread2"), 16 * 24)
                    for name in ("mcq32", "mck32", "vc2"):
                        pe.wait_ge(sem(name), 1)
                    attention(2, hid2[4:])
                    pe.wait_ge(sem("oc2"), 1)
                    project(0, W("mc_o"), oc[:, :], "mix_ps2")
                    pe.wait_ge(sem("hsplit3"), 1)
                    pe.wait_ge(sem("up_free"), 8)
                    for c in range(NC):
                        t = slice(c * P, (c + 1) * P)
                        last = three(UP, t, [(h_hi[:, 0, hc, t], h_lo[:, 0, hc, t], part(w_hi, "F3", hc, P),
                                              part(w_lo, "F3", hc, P)) for hc in range(HC)])
                    last.then_inc(sem("y3"), 1)
                    pe.wait_ge(sem("ctx2"), 1)
                    for c in range(NC):
                        t = slice(c * P, (c + 1) * P)
                        last = mm(1, t, ctxT[:, t], W("l1_o"), True, True)
                    last.then_inc(sem("attn1"), 1)

                @block.vector
                def _(dve):
                    count = [0]

                    def link(ins):
                        count[0] += 1
                        ins.then_inc(sem("dve_chain"), 1)
                        dve.wait_ge(sem("dve_chain"), count[0])

                    v = nc.vector

                    def norm_stats(src, n, tag):
                        for c in range(NC):
                            ins = v.bn_stats(stats[:, c, :], src(c))
                        link(ins)
                        for c in range(NC):
                            ins = v.bn_aggr(mv[:, c, :], stats[:, c, :])
                        link(ins)
                        v.tensor_scalar(ve[:, :], mv[:, :, 1], EPS, None, ALU.add).then_inc(sem(f"ve{tag}"), 1)
                        dve.wait_ge(sem(f"rstd{tag}"), 1)

                    def layer_norm(L):
                        norm_stats(lambda c: x[:, c, :], D, f"x{L}")
                        for c in range(NC):
                            ins = v.tensor_scalar(xn[:, c, :], x[:, c, :], mv[:, c, 0:1], rstd[:, c:c + 1],
                                                  ALU.subtract, ALU.mult)
                        ins.then_inc(sem(f"xn{L}"), 1)
                        dve.wait_ge(sem(f"xT{L}"), 1)
                        link(v.tensor_copy(xh[:, :], xT[:, :]))
                        v.tensor_tensor(out=xl[:, :], in0=xT[:, :], in1=xh[:, :], op=ALU.subtract) \
                            .then_inc(sem(f"xsplit{L}"), 1)

                    def halves(src, hi, lo, name):
                        link(v.tensor_copy(hi[:, :], src[:, :]))
                        v.tensor_tensor(out=lo[:, :], in0=src[:, :], in1=hi[:, :], op=ALU.subtract) \
                            .then_inc(sem(name), 1)

                    def reduce_unit(st, u):
                        gr, c, pair = u // U, (u % U) // 2, u % 2
                        kw, _ = width(st, c)
                        dve.wait_ge(sem(f"score{st}"), u + 1)
                        v.tensor_reduce(negmax[:, gr, c, 2 * pair:2 * pair + 2], psum[:, SCO:SCO + 2, 0:kw],
                                        AX.X, ALU.max, negate=True).then_inc(sem(f"max{st}"), 1)

                    def max_out(st, gr):
                        dve.wait_ge(sem(f"mrow_ps{st}"), gr + 1)
                        if gr >= 2:
                            dve.wait_ge(sem(f"qm{st}_{gr - 2}"), 16)
                        v.tensor_copy(mrow[:, gr % 2, :], psum[0:GH, MIS, :]).then_inc(sem(f"mrow{st}"), 1)

                    def mixing_out(st):
                        dve.wait_ge(sem(f"pv{st}"), NS[st] // 2)
                        link(v.reciprocal(t_b[:, :], psum[:, DN, :]))
                        v.tensor_tensor(out=oc[:, :], in0=psum[:, OUT, :], in1=t_b[:, :], op=ALU.mult) \
                            .then_inc(sem(f"oc{st}"), 1)

                    def finish_heads(L):
                        for c in range(NC):
                            dve.wait_ge(sem(f"oq_ps{L}"), c + 1)
                            bank = psum[:, c, :].rearrange("p (h r) -> p h r", r=32)
                            link(v.reciprocal(rden[:, c, :], bank[:, :, HD]))
                            v.tensor_tensor(out=onorm[:, c, :, :], in0=bank[:, :, 0:HD],
                                            in1=rden[:, c, :].unsqueeze(2).broadcast_to([P, NH, HD]),
                                            op=ALU.mult).then_inc(sem(f"onorm{L}"), 1)

                    dve.wait_ge(sem("x_in"), 16)
                    layer_norm(0)
                    dve.wait_ge(sem("lat_ps"), 1)
                    norm_stats(lambda c: psum[:, DN, LAT * c:LAT * c + LAT], LAT, "lat")
                    for c in range(NC):
                        ins = v.tensor_scalar(latn[:, c, :], psum[:, DN, LAT * c:LAT * c + LAT], mv[:, c, 0:1],
                                              rstd[:, c:c + 1], ALU.subtract, ALU.mult)
                    ins.then_inc(sem("latn"), 1)
                    dve.wait_ge(sem("q_ps0"), 2)
                    v.tensor_tensor(out=t_a[:, :], in0=psum[:, 0, :], in1=C("cos"), op=ALU.mult)
                    link(v.tensor_tensor(out=t_b[:, :], in0=psum[:, 1, :], in1=C("sin"), op=ALU.mult))
                    ins = v.tensor_tensor(out=q32[:, :], in0=t_a[:, :], in1=t_b[:, :], op=ALU.add)
                    ins.then_inc(sem("rope_q"), 1)
                    dve.wait_ge(sem("rope_q"), 1)
                    halves(q32, q_hi, q_lo, "qsplit0")
                    dve.wait_ge(sem("latT_ps"), 1)
                    v.tensor_scalar(latT[:, :], psum[0:LAT, 3, :], V("gamma", n=LAT), V("beta", n=LAT),
                                    ALU.mult, ALU.add).then_inc(sem("latT"), 1)
                    dve.wait_ge(sem("k_ps0"), 2)
                    v.tensor_tensor(out=t_a[:, :], in0=psum[:, 0, :], in1=C("cos"), op=ALU.mult)
                    link(v.tensor_tensor(out=t_b[:, :], in0=psum[:, 1, :], in1=C("sin"), op=ALU.mult))
                    v.tensor_tensor(out=k32[:, :], in0=t_a[:, :], in1=t_b[:, :], op=ALU.add).then_inc(sem("rope_k"), 1)
                    dve.wait_ge(sem("rope_k"), 1)
                    halves(k32, k_hi, k_lo, "ksplit0")
                    dve.wait_ge(sem("lg_ps"), 1)
                    link(v.tensor_tensor(out=lg[:, :, :], in0=psum[:, 2, 0:NC * E].rearrange("p (c e) -> p c e", e=E),
                                         in1=R("bg").unsqueeze(1).broadcast_to([P, NC, E]), op=ALU.add))
                    mine = lg[:, :, :].unsqueeze(3).broadcast_to([P, NC, E, E])
                    other = lg[:, :, :].unsqueeze(2).broadcast_to([P, NC, E, E])
                    tri = C("tri").rearrange("p (e f) -> p e f", f=E)
                    v.tensor_tensor(out=cmp1[:, :, :, :], in0=other, in1=mine, op=ALU.is_gt)
                    link(v.tensor_tensor(out=cmp2[:, :, :, :], in0=other, in1=mine, op=ALU.is_equal))
                    for c in range(NC):
                        ins = v.tensor_tensor(out=cmp2[:, c, :, :], in0=cmp2[:, c, :, :], in1=tri, op=ALU.mult)
                    link(ins)
                    link(v.tensor_tensor(out=cmp1[:, :, :, :], in0=cmp1[:, :, :, :], in1=cmp2[:, :, :, :], op=ALU.add))
                    link(v.tensor_reduce(gates[:, :, :], cmp1[:, :, :, :], AX.X, ALU.add))
                    v.tensor_scalar(gates[:, :, :], gates[:, :, :], 1.5, None, ALU.is_lt)
                    link(v.tensor_reduce(gmax[:, :], lg[:, :, :], AX.X, ALU.max))
                    v.tensor_tensor(out=lg[:, :, :], in0=lg[:, :, :], in1=gmax[:, :].unsqueeze(2).broadcast_to([P, NC, E]),
                                    op=ALU.subtract).then_inc(sem("lg"), 1)
                    dve.wait_ge(sem("gex"), 1)
                    link(v.tensor_tensor(out=gates[:, :, :], in0=gates[:, :, :], in1=gex[:, :, :], op=ALU.mult))
                    link(v.tensor_reduce(gsum[:, :], gates[:, :, :], AX.X, ALU.add))
                    link(v.reciprocal(gsum[:, :], gsum[:, :]))
                    v.tensor_tensor(out=gates[:, :, :], in0=gates[:, :, :], in1=gsum[:, :].unsqueeze(2).broadcast_to([P, NC, E]),
                                    op=ALU.mult).then_inc(sem("gates"), 1)
                    dve.wait_ge(sem("gates"), 1)

                    hid = [0]

                    def hidden_hi(e, hc):
                        dve.wait_ge(sem("relu"), e * HC + hc + 1)
                        if hc == 0 and e >= 2:
                            dve.wait_ge(sem("down0"), e - 1)
                        v.tensor_copy(h_hi[:, e % 2, hc, :], h32[:, hc, :]).then_inc(sem("h_hi0"), 1)

                    def add_expert(e):
                        dve.wait_ge(sem("down0"), e + 1)
                        for c in range(NC):
                            ins = v.scalar_tensor_tensor(out=x[:, c, :], in0=psum[:, DN, c * P:(c + 1) * P],
                                                         scalar=gates[:, c, e:e + 1], in1=x[:, c, :],
                                                         op0=ALU.mult, op1=ALU.add)
                        ins.then_inc(sem("acc0"), 1)
                        dve.wait_ge(sem("acc0"), e + 1)

                    pieces = []
                    for e in range(E + 1):
                        for hc in range(HC):
                            if e < E:
                                pieces.append((hidden_hi, (e, hc)))
                            if e:
                                pieces.append((add_expert, (e - 1,)) if hc == HC - 1 else None)

                    def attention(st, pieces):
                        n = NS[st]
                        slots = n + LAG + 3
                        done = 0
                        for s in range(slots):
                            if s < n:
                                reduce_unit(st, s)
                            want = -(-len(pieces) * (s + 1) // slots)
                            if s % U == 1 and U <= s <= n + 1:
                                max_out(st, s // U - 1)
                            while done < want:
                                if pieces[done] is not None:
                                    pieces[done][0](*pieces[done][1])
                                done += 1

                    for piece in pieces[:12]:
                        if piece is not None:
                            piece[0](*piece[1])
                    attention(0, pieces[12:])
                    finish_heads(0)
                    dve.wait_ge(sem("attn0"), 1)
                    xf = x[:, :, :].rearrange("p c d -> p (c d)")
                    v.tensor_tensor(out=xf, in0=xf, in1=psum[:, 0, :], op=ALU.add).then_inc(sem("xin1"), 1)
                    dve.wait_ge(sem("xin1"), 1)

                    layer_norm(1)
                    dve.wait_ge(sem("mod_e"), 1)
                    link(v.tensor_scalar(t_a[:, :], t_a[:, :], 1.0, None, ALU.add))
                    link(v.reciprocal(t_a[:, :], t_a[:, :]))
                    dve.wait_ge(sem("q_ps1"), 1)
                    v.scalar_tensor_tensor(out=q32[:, :], in0=psum[:, 0, :], scalar=V("bq"), in1=t_a[:, :],
                                           op0=ALU.add, op1=ALU.mult).then_inc(sem("q_out1"), 1)
                    dve.wait_ge(sem("q_out1"), 1)
                    halves(q32, q_hi, q_lo, "qsplit1")
                    dve.wait_ge(sem("k32_1"), 1)
                    halves(k32, k_hi, k_lo, "ksplit1")
                    dve.wait_ge(sem("v_ps1"), 1)
                    for c in range(NC):
                        ins = v.tensor_tensor(out=vp[:, c, :, 0:HD],
                                              in0=psum[:, 5, c * P:(c + 1) * P].rearrange("p (h d) -> p h d", d=HD),
                                              in1=R("bv").rearrange("p (h d) -> p h d", d=HD), op=ALU.add)
                    ins.then_inc(sem("vp1"), 1)
                    dve.wait_ge(sem("cav_ps"), 1)
                    v.tensor_tensor(out=vc[:, :, :], in0=psum[:, 7, :].rearrange("p (c d) -> p c d", d=D),
                                    in1=R("ca_bv").unsqueeze(1).broadcast_to([P, NC, D]), op=ALU.add) \
                        .then_inc(sem("vc1"), 1)
                    dve.wait_ge(sem("spread1"), 16 * (24 + 48))
                    dve.wait_ge(sem("caq32"), 1)
                    halves(q32, q_hi, q_lo, "qsplit3")
                    dve.wait_ge(sem("cak32"), 1)
                    halves(k32, k_hi, k_lo, "ksplit3")

                    def gate_out(o):
                        dve.wait_ge(sem("silu_e"), o + 1)
                        link(v.tensor_scalar(t_b[:, :], t_b[:, :], 1.0, None, ALU.add))
                        link(v.reciprocal(t_b[:, :], t_b[:, :]))
                        link(v.scalar_tensor_tensor(out=t_b[:, :], in0=psum[:, UP, :], scalar=V("s1", o), in1=t_b[:, :],
                                                    op0=ALU.mult, op1=ALU.mult))
                        dve.wait_ge(sem("g1b"), o + 1)
                        v.scalar_tensor_tensor(out=h32[:, o, :], in0=psum[:, DN, :], scalar=V("s2", o), in1=t_b[:, :],
                                               op0=ALU.mult, op1=ALU.mult).then_inc(sem("h32_1"), 1)
                        dve.wait_ge(sem("h32_1"), o + 1)
                        link(v.tensor_copy(h_hi[:, 0, o, :], h32[:, o, :]))
                        ins = v.tensor_tensor(out=h_lo[:, 0, o, :], in0=h32[:, o, :], in1=h_hi[:, 0, o, :], op=ALU.subtract)
                        if o == HC - 1:
                            ins.then_inc(sem("hsplit1"), 1)
                            ins = None

                    def hidden_out(n, o):
                        dve.wait_ge(sem(f"hid{n}"), o + 1)
                        if n == 1 and o == 0:
                            dve.wait_ge(sem("hsplit1"), 1)
                        if n == 2 and o == 0:
                            dve.wait_ge(sem("hsplit2"), 1)
                        v.tensor_scalar(h32[:, o, :], psum[:, UP, :], V(f"hs{n}", o), None, ALU.mult) \
                            .then_inc(sem("up_free"), 1)

                    def gelu_parts(n, dst):
                        dve.wait_ge(sem(f"gelu{n}"), 1)
                        for o in range(HC):
                            ins = v.tensor_copy(h_hi[:, dst, o, :], h32[:, o, :])
                        link(ins)
                        for o in range(HC):
                            ins = v.tensor_tensor(out=h_lo[:, dst, o, :], in0=h32[:, o, :], in1=h_hi[:, dst, o, :],
                                                  op=ALU.subtract)
                        ins.then_inc(sem(f"hsplit{n + 1}"), 1)

                    gate_out(0)
                    attention(1, [(gate_out, (o,)) for o in range(1, HC)]
                              + [((hidden_out, (1, o)) if ic == HC - 1 else None) for o in range(HC) for ic in range(HC)])
                    mixing_out(1)
                    finish_heads(1)
                    dve.wait_ge(sem("mix1"), 1)
                    dve.wait_ge(sem("oT1"), 1)
                    v.scalar_tensor_tensor(out=ctxT[:, :], in0=oT[:, :], scalar=1.0 - CAUSAL_W, in1=t_a[:, :],
                                           op0=ALU.mult, op1=ALU.add).then_inc(sem("ctx"), 1)
                    dve.wait_ge(sem("mcq32"), 1)
                    halves(q32, q_hi, q_lo, "qsplit2")
                    dve.wait_ge(sem("mck32"), 1)
                    halves(k32, k_hi, k_lo, "ksplit2")
                    dve.wait_ge(sem("mcv_ps"), 1)
                    v.tensor_tensor(out=vc[:, :, :], in0=psum[:, 2, :].rearrange("p (c d) -> p c d", d=D),
                                    in1=R("mc_bv").unsqueeze(1).broadcast_to([P, NC, D]), op=ALU.add) \
                        .then_inc(sem("vc2"), 1)
                    gelu_parts(1, 1)
                    hid2 = [((hidden_out, (2, o)) if ic == HC - 1 else None) for o in range(HC) for ic in range(HC)]
                    hid2[3][0](*hid2[3][1])
                    attention(2, hid2[4:])
                    mixing_out(2)
                    gelu_parts(2, 0)
                    dve.wait_ge(sem("mix2"), 1)
                    v.scalar_tensor_tensor(out=ctxT[:, :], in0=ctxT[:, :], scalar=1.0 - META_W, in1=t_a[:, :],
                                           op0=ALU.mult, op1=ALU.add).then_inc(sem("ctx2"), 1)
                    dve.wait_ge(sem("y3"), 1)
                    t4 = t_b[:, :].rearrange("p (c d) -> p c d", d=D)
                    link(v.tensor_tensor(out=t4, in0=psum[:, UP, :].rearrange("p (c d) -> p c d", d=D),
                                         in1=R("s3").unsqueeze(1).broadcast_to([P, NC, D]), op=ALU.mult))
                    link(v.tensor_tensor(out=xf, in0=xf, in1=t_b[:, :], op=ALU.add))
                    link(v.tensor_tensor(out=x[:, :, :], in0=x[:, :, :], in1=R("bo").unsqueeze(1).broadcast_to([P, NC, D]),
                                         op=ALU.add))
                    dve.wait_ge(sem("attn1"), 1)
                    v.tensor_tensor(out=xf, in0=xf, in1=psum[:, 1, :], op=ALU.add).then_inc(sem("x_out"), 1)

                @block.scalar
                def _(act):
                    a = nc.scalar

                    def exp_unit(st, u):
                        gr, c, pair = u // U, (u % U) // 2, u % 2
                        _, q0 = width(st, c)
                        act.wait_ge(sem(f"trans{st}"), u + 1)
                        kk = u // 2
                        if kk >= 2 and pair == 0:
                            act.wait_ge(sem(f"pv{st}"), kk - 1)
                        a.activation(probs[:, kk % 2, 2 * pair:2 * pair + 2, q0:T], psum[:, TRA:TRA + 2, q0:T],
                                     ACT.Exp, scale=SCALE[main(st, gr)]).then_inc(sem(f"exp{st}"), 1)

                    def out_group(st, gr):
                        act.wait_ge(sem(f"pv{st}"), NC * (gr + 1))
                        a.activation(osb[:, gr, :], psum[:, OUT, :], ACT.Copy).then_inc(sem(f"osb{st}"), 1)

                    def relu(e, hc):
                        act.wait_ge(sem("up0"), e * HC + hc + 1)
                        if e:
                            act.wait_ge(sem("h_lo0"), HC * (e - 1) + hc + 1)
                        a.activation(h32[:, hc, :], psum[:, UP, :], ACT.Relu, bias=V("b1", e * HC + hc)) \
                            .then_inc(sem("relu"), 1)

                    def attention(st, pieces):
                        n = NS[st]
                        slots = n + LAG + 3
                        done = 0
                        for s in range(slots):
                            want = -(-len(pieces) * (s + 1) // slots)
                            while done < (done + want + 1) // 2:
                                if pieces[done] is not None:
                                    pieces[done][0](*pieces[done][1])
                                done += 1
                            if LAG <= s < n + LAG:
                                exp_unit(st, s - LAG)
                            while done < want:
                                if pieces[done] is not None:
                                    pieces[done][0](*pieces[done][1])
                                done += 1
                            k = s - LAG - 2
                            if k > 0 and k % U == 7 and main(st, k // U) and k // U < n // U:
                                out_group(st, k // U)

                    def move(dst, bank, name, rows_=P, wait=None):
                        act.wait_ge(sem(wait), 1)
                        a.activation(dst, psum[0:rows_, bank, :], ACT.Copy).then_inc(sem(name), 1)

                    move(xT[:, :], MIS, "xT0", wait="xT_ps0")
                    pieces = []
                    for e in range(E + 1):
                        for hc in range(HC):
                            if e < E:
                                pieces.append((relu, (e, hc)))
                            if e:
                                pieces.append(None)
                    for f, ar in pieces[:4]:
                        f(*ar)
                    act.wait_ge(sem("v_ps0"), 1)
                    for c in range(NC):
                        ins = a.activation(vp[:, c, :, 0:HD], psum[:, MIS, c * P:(c + 1) * P]
                                           .rearrange("p (h d) -> p h d", d=HD), ACT.Copy)
                    ins.then_inc(sem("vp0"), 1)
                    act.wait_ge(sem("lg"), 1)
                    a.activation(gex[:, :, :], lg[:, :, :], ACT.Exp).then_inc(sem("gex"), 1)
                    for piece in pieces[4:12]:
                        if piece is not None:
                            piece[0](*piece[1])
                    attention(0, pieces[12:])
                    move(oT[:, :], MIS, "oT0", wait="oT_ps0")
                    move(gT[:, :], UP, "gT", rows_=E, wait="gT_ps")

                    move(xT[:, :], MIS, "xT1", wait="xT_ps1")
                    act.wait_ge(sem("mod_ps"), 1)
                    act.wait_ge(sem("rope_k"), 1)
                    a.activation(t_a[:, :], psum[:, 1, :], ACT.Exp, scale=-1.0, bias=mod_bias[:, :]).then_inc(sem("mod_e"), 1)
                    act.wait_ge(sem("mod_e"), 1)
                    act.wait_ge(sem("k_ps1"), 1)
                    a.activation(k32[:, :], psum[:, 2, :], ACT.Identity, bias=V("bk")).then_inc(sem("k32_1"), 1)
                    act.wait_ge(sem("caq_ps"), 1)
                    act.wait_ge(sem("qsplit1"), 1)
                    a.activation(q32[:, :], psum[:, 3, :], ACT.Identity, bias=V("ca_bq")).then_inc(sem("caq32"), 1)
                    act.wait_ge(sem("cak_ps"), 1)
                    act.wait_ge(sem("ksplit1"), 1)
                    a.activation(k32[:, :], psum[:, 4, :], ACT.Identity, bias=V("ca_bk")).then_inc(sem("cak32"), 1)

                    def silu_e(o):
                        act.wait_ge(sem("g1a"), o + 1)
                        if o:
                            act.wait_ge(sem("h32_1"), o)
                        a.activation(t_b[:, :], psum[:, UP, :], ACT.Exp, scale=neg_s1[:, o:o + 1]).then_inc(sem("silu_e"), 1)

                    silu_e(0)
                    attention(1, [(silu_e, (o,)) for o in range(1, HC)] + [None] * 16)
                    move(oT[:, :], MIS, "oT1", wait="oT_ps1")
                    act.wait_ge(sem("mix_ps1"), 1)
                    a.activation(t_a[:, :], psum[:, OUT, :], ACT.Identity, scale=CAUSAL_W, bias=ca_bo7[:, :]).then_inc(sem("mix1"), 1)
                    act.wait_ge(sem("mcq_ps"), 1)
                    a.activation(q32[:, :], psum[:, 0, :], ACT.Identity, bias=V("mc_bq")).then_inc(sem("mcq32"), 1)
                    act.wait_ge(sem("mck_ps"), 1)
                    a.activation(k32[:, :], psum[:, 1, :], ACT.Identity, bias=V("mc_bk")).then_inc(sem("mck32"), 1)
                    act.wait_ge(sem("up_free"), HC)
                    a.activation(h32[:, :, :], h32[:, :, :], ACT.Gelu).then_inc(sem("gelu1"), 1)
                    attention(2, [])
                    act.wait_ge(sem("up_free"), 2 * HC)
                    a.activation(h32[:, :, :], h32[:, :, :], ACT.Gelu).then_inc(sem("gelu2"), 1)
                    act.wait_ge(sem("mix_ps2"), 1)
                    a.activation(t_a[:, :], psum[:, 0, :], ACT.Identity, scale=META_W, bias=mc_bo15[:, :]).then_inc(sem("mix2"), 1)

                @block.gpsimd
                def _(pool):
                    def inverse_root(tag):
                        pool.wait_ge(sem(f"ve{tag}"), 1)
                        nc.gpsimd.tensor_tensor(out=rstd[:, :], in0=ve[:, :], in1=neghalf[:, :], op=ALU.pow) \
                            .then_inc(sem(f"rstd{tag}"), 1)

                    inverse_root("x0")
                    inverse_root("lat")
                    for n in range(E * HC):
                        e, hc = n // HC, n % HC
                        pool.wait_ge(sem("h_hi0"), n + 1)
                        nc.gpsimd.tensor_tensor(out=h_lo[:, e % 2, hc, :], in0=h32[:, hc, :], in1=h_hi[:, e % 2, hc, :],
                                                op=ALU.subtract).then_inc(sem("h_lo0"), 1)
                    inverse_root("x1")

                @block.sync
                def _(sp):
                    def spread_main(L):
                        sp.wait_ge(sem(f"qsplit{L}"), 1)
                        for gr in range(NG):
                            for j, part_ in enumerate((q_hi, q_hi, q_lo)):
                                for dst in (qs, qm):
                                    sp.dma_start(dst[j:P:4, gr, :], part_[32 * gr:32 * gr + 32, :]).then_inc(sem(f"spread{L}"), 16)
                        sp.wait_ge(sem(f"ksplit{L}"), 1)
                        for h in range(NH):
                            r = 32 * (h % GH)
                            for j, part_ in enumerate((k_hi, k_lo, k_hi)):
                                sp.dma_start(kp[r + j:r + 32:4, h, :], part_[HD * h:HD * (h + 1), :]).then_inc(sem(f"spread{L}"), 16)

                    def spread_mixing(n, st):
                        sp.wait_ge(sem(f"qsplit{n}"), 1)
                        sp.wait_ge(sem(f"ksplit{n}"), 1)
                        if st == 2:
                            sp.wait_ge(sem("trans1"), NS[1])
                        for h in range(MH):
                            for j, (a, b) in enumerate(((q_hi, k_hi), (q_hi, k_lo), (q_lo, k_hi))):
                                sp.dma_start(qc[32 * j:32 * j + 32, h, :], a[MD * h:MD * (h + 1), :]).then_inc(sem(f"spread{n}"), 16)
                                sp.dma_start(kc[32 * j:32 * j + 32, h, :], b[MD * h:MD * (h + 1), :]).then_inc(sem(f"spread{n}"), 16)

                    def max_rows(st, gr):
                        sp.wait_ge(sem(f"mrow{st}"), gr + 1)
                        if main(st, gr):
                            sp.dma_start(qm[3:P:32, gr, :], mrow[:, gr % 2, :]).then_inc(sem(f"qm{st}_{gr}"), 16)
                        else:
                            for h in range(MH):
                                sp.dma_start(qc[96:97, h, :], mrow[h:h + 1, gr % 2, :]).then_inc(sem(f"qm{st}_{gr}"), 16)

                    sp.dma_start(x[:, :, :], x_in[bass.ds(i, 1)].rearrange("b (c p) d -> p (b c) d", p=P)).then_inc(sem("x_in"), 16)
                    spread_main(0)
                    for gr in range(NG):
                        max_rows(0, gr)
                    spread_main(1)
                    spread_mixing(3, 1)
                    for gr in range(NG + 1):
                        max_rows(1, gr)
                    spread_mixing(2, 2)
                    max_rows(2, 0)
                    sp.wait_ge(sem("x_out"), 1)
                    sp.dma_start(out[bass.ds(i, 1)].rearrange("b (c p) d -> p (b c) d", p=P), x[:, :, :]).then_inc(sem("stored"), 16)
                    sp.wait_ge(sem("stored"), 16)

            numbers = sorted(s.num for s in sems.values())
            assert numbers == list(range(numbers[0], numbers[0] + len(numbers)))
            nc.sync.sem_clear(range(numbers[0], numbers[-1] + 1))
            nc.all_engine_barrier()


def kernel(**inputs):
    import numpy as _np
    import concourse.bacc as _bacc
    from concourse import mybir as _mybir
    from concourse.bass_utils import run_bass_kernel_spmd as _run

    a = {n: _np.asarray(v) for n, v in inputs.items()}
    f32 = _np.float32

    def swapped(w):
        return w.reshape(w.shape[0], NH, 2, HD // 2)[:, :, ::-1].reshape(w.shape[0], 128)

    ca, mc = a["L1_attn_ca_Win"], a["L1_attn_mc_Win"]
    cab, mcb = a["L1_attn_ca_bin"], a["L1_attn_mc_bin"]
    wide = _np.concatenate([
        a["L0_attn_W_q"], swapped(a["L0_attn_W_q"]), a["L0_attn_W_o"], a["L1_attn_Wq"], a["L1_attn_Wk"], a["L1_attn_Wv"],
        _np.repeat(a["L1_attn_cg_W"], HD, axis=1), a["L1_attn_Wo"], ca, a["L1_attn_ca_Wout"], mc, a["L1_attn_mc_Wout"],
        a["L0_attn_W_dkv"], a["L0_ffn_Wg"]], axis=1)
    latw = _np.concatenate([a["L0_attn_W_uk"], swapped(a["L0_attn_W_uk"]), a["L0_attn_W_uv"]], axis=1)

    def column(v):
        return v.reshape(-1, 128).T

    def padded(v):
        z = _np.zeros((128, 1), f32)
        z[:v.shape[0], 0] = v
        return z

    cols = _np.concatenate([
        column(a["L1_attn_bq"]), column(a["L1_attn_bk"]), column(cab[:128]), column(cab[128:256]),
        column(mcb[:128]), column(mcb[128:256]), column(a["L1_attn_ca_bout"]), column(a["L1_attn_mc_bout"]),
        column(_np.repeat(a["L1_attn_cg_b"], HD)), column(_np.repeat(a["L1_attn_am_b"], HD)),
        padded(a["L0_attn_ln_gamma"]), padded(a["L0_attn_ln_beta"]), column(a["L0_ffn_b1"]),
        column(a["L1_ffn_w1_s"]), column(a["L1_ffn_w2_s"]), column(a["L1_ffn_h1_s"]), column(a["L1_ffn_h2_s"])], axis=1)
    rows = _np.concatenate([a["L1_attn_bv"], cab[256:], mcb[256:], a["L1_attn_bo"], a["L1_ffn_w3_s"], a["L0_ffn_bg"]])[None]

    def chunks(w):
        return w.reshape(-1, 128, w.shape[-1]).transpose(1, 0, 2).reshape(128, -1)

    split = _np.concatenate([
        a["L0_ffn_W1"].transpose(1, 0, 2).reshape(128, -1), chunks(a["L0_ffn_W2"].reshape(-1, 128)),
        a["L1_ffn_w1_w"].T, a["L1_ffn_w2_w"].T, chunks(a["L1_ffn_h1_w"].T), chunks(a["L1_ffn_h2_w"].T),
        chunks(a["L1_ffn_w3_w"].T)], axis=1)
    arrays = dict(x_in=a["L0_attn_x"], wide_in=wide, lat_in=latw, cols_in=cols, rows_in=rows, const_in=constants(),
                  split_in=split, am_in=_np.repeat(a["L1_attn_am_W"], HD, axis=1), cons_in=a["L1_attn_cons_vec"][:, None],
                  b2_in=a["L0_ffn_b2"])
    arrays = {n: _np.ascontiguousarray(v) for n, v in arrays.items()}
    nc = _bacc.Bacc("TRN2", target_bir_lowering=False, num_devices=1)
    args = {n: nc.dram_tensor(n, v.shape, _mybir.dt.from_np(v.dtype), kind="ExternalInput").ap() for n, v in arrays.items()}
    out = nc.dram_tensor("out", (B, T, D), F32, kind="ExternalOutput").ap()
    build(nc, out=out, **args)
    r = _run(nc, [arrays], core_ids=[0])
    return r.results[0]["out"]
```

```python
from contextlib import ExitStack

import numpy as np

import concourse.bass as bass
from concourse import mybir

P = 128
F32 = mybir.dt.float32
F16 = mybir.dt.float16
BF16 = mybir.dt.bfloat16
ACT = mybir.ActivationFunctionType
ALU = mybir.AluOpType
AX = mybir.AxisListType

B, T, D = 8, 512, 128
NC = T // P
NH, HD = 16, 8
NG, GH = 4, 4
MH, MD = 4, 32
E, HC = 8, 4
LAT = 32
EPS = 1e-5
CAUSAL_W = 0.7
META_W = (0.9 - 0.8) / 0.2 * 0.3

WIDE = [("l0_q", 128), ("l0_qr", 128), ("l0_o", 128), ("l1_q", 128), ("l1_k", 128), ("l1_v", 128),
        ("cg", 128), ("l1_o", 128), ("ca_q", 128), ("ca_k", 128), ("ca_v", 128), ("ca_o", 128),
        ("mc_q", 128), ("mc_k", 128), ("mc_v", 128), ("mc_o", 128), ("dkv", LAT), ("gate", E)]
COLS = [("bq", 1), ("bk", 1), ("ca_bq", 1), ("ca_bk", 1), ("mc_bq", 1), ("mc_bk", 1),
        ("ca_bo", 1), ("mc_bo", 1), ("cg_b", 1), ("am_b", 1), ("gamma", 1), ("beta", 1),
        ("b1", E * HC), ("s1", HC), ("s2", HC), ("hs1", HC), ("hs2", HC)]
ROWS = [("bv", 128), ("ca_bv", 128), ("mc_bv", 128), ("bo", 128), ("s3", 128), ("bg", E)]
CONST = [("ident", 128), ("mask", 128), ("maskT", 128), ("tri", E * E), ("cos", T), ("sin", T)]
SPLIT = [("W1", E * 512), ("W2", E * 512), ("F1", 512), ("F2", 512), ("G1", 2048), ("G2", 2048),
         ("F3", 512)]


def places(parts):
    at, out = 0, {}
    for name, n in parts:
        out[name] = (at, at + n)
        at += n
    return out, at


def constants():
    ident = np.eye(P, dtype=np.float32)
    q, k = np.arange(P)[:, None], np.arange(P)[None, :]
    mask = np.where(k > q, np.float32(-1e30), np.float32(0))
    e = np.arange(E)
    tri = np.broadcast_to((e[None, :] < e[:, None]).astype(np.float32).reshape(1, E * E), (P, E * E))
    half = HD // 2
    freq = (np.float32(1.0) / np.float32(10000.0) ** (np.arange(half, dtype=np.float32) / np.float32(half))).astype(np.float32)
    angle = (np.arange(T, dtype=np.float32)[:, None] * freq[None, :]).astype(np.float32)
    cos, sin = np.cos(angle).T, np.sin(angle).T
    cos_rows = np.tile(np.concatenate([cos, cos]), (NH, 1))
    sin_rows = np.tile(np.concatenate([-sin, sin]), (NH, 1))
    return np.ascontiguousarray(np.concatenate([ident, mask, mask.T, tri, cos_rows, sin_rows], axis=1), dtype=np.float32)


def build(nc, x_in, wide_in, lat_in, cols_in, rows_in, const_in, split_in, am_in, cons_in, b2_in, out):
    WIDE_AT, n_wide = places(WIDE)
    COLS_AT, n_cols = places(COLS)
    ROWS_AT, n_rows = places(ROWS)
    CONST_AT, n_const = places(CONST)
    SPLIT_AT, n_split = places(SPLIT)
    ctx = ExitStack()
    with ctx:
        def sb(name, shape, dt=F32):
            return ctx.enter_context(nc.sbuf_tensor(name, shape, dt))

        wide = sb("wide", [P, n_wide])
        latw = sb("latw", [LAT, 3 * 128])
        cols = sb("cols", [P, n_cols])
        rows = sb("rows", [P, n_rows])
        const = sb("const", [P, n_const])
        w_hi = sb("w_hi", [P, n_split], F16)
        w_lo = sb("w_lo", [P, n_split], F16)
        b2 = sb("b2", [E, 128])
        am = sb("am", [16, 128])
        cons = sb("cons", [16, 1])
        ident16 = sb("ident16", [P, P], F16)
        identb = sb("identb", [P, P], BF16)
        maskb = sb("maskb", [P, P], BF16)
        maskTb = sb("maskTb", [P, P], BF16)
        ones = sb("ones", [P, 32])
        neghalf = sb("neghalf", [P, NC])
        mod_bias = sb("mod_bias", [P, 1])
        half_s1 = sb("half_s1", [P, HC])
        s12 = sb("s12", [P, HC])
        ca_bo7 = sb("ca_bo7", [P, 1])
        mc_bo15 = sb("mc_bo15", [P, 1])

        def W(name):
            a, b = WIDE_AT[name]
            return wide[:, a:b]

        def V(name, i=0, n=P):
            a, _ = COLS_AT[name]
            return cols[0:n, a + i:a + i + 1]

        def R(name):
            a, b = ROWS_AT[name]
            return rows[:, a:b]

        def C(name):
            a, b = CONST_AT[name]
            return const[:, a:b]

        def part(w, name, i, n):
            a, _ = SPLIT_AT[name]
            return w[:, a + i * n:a + (i + 1) * n]

        x = sb("x", [P, NC, D])
        xn = sb("xn", [P, NC, D])
        xT = sb("xT", [P, T])
        xh = sb("xh", [P, T], F16)
        xl = sb("xl", [P, T], F16)
        stats = sb("stats", [P, NC, 6])
        mv = sb("mv", [P, NC, 2])
        ve = sb("ve", [P, NC])
        rstd = sb("rstd", [P, NC])
        latn = sb("latn", [P, NC, LAT])
        latT = sb("latT", [LAT, T])
        t_a = sb("t_a", [P, T])
        t_b = sb("t_b", [P, T])
        q32 = sb("q32", [P, T])
        k32 = sb("k32", [P, T])
        parts = sb("parts", [P, 2, 4, T], F16)
        qsm = sb("qsm", [P, 2, NG, T], F16)
        qs, qm = qsm[:, 0, :, :], qsm[:, 1, :, :]
        kp = sb("kp", [P, NH, T], F16)
        vp = sb("vp", [P, NC, NH, 32])
        qkc = sb("qkc", [P, 2, MH, T], F16)
        qc, kc = qkc[:, 0, :, :], qkc[:, 1, :, :]
        vc = sb("vc", [P, NC, D])
        negmax = sb("negmax", [P, NG + 2, NC, GH], F16)
        mrow = sb("mrow", [GH, 2, T], F16)
        probs = sb("probs", [P, 2, GH, T])
        osb = sb("osb", [P, NG, T])
        rden = sb("rden", [P, NC, NH])
        onorm = sb("onorm", [P, NC, NH, HD])
        oT = sb("oT", [P, T])
        oc = sb("oc", [P, T])
        ctxT = sb("ctxT", [P, T])
        h_hi = sb("h_hi", [P, 2, HC, T], F16)
        h_lo = sb("h_lo", [P, 2, HC, T], F16)
        h32 = sb("h32", [P, HC, T])
        lg = sb("lg", [P, NC, E])
        gex = sb("gex", [P, NC, E])
        gmax = sb("gmax", [P, NC])
        gsum = sb("gsum", [P, NC])
        gates = sb("gates", [P, NC, E])
        cmp1 = sb("cmp1", [P, NC, E, E])
        cmp2 = sb("cmp2", [P, NC, E, E])
        gT = sb("gT", [E, T])

        relay = nc.dram_tensor("relay", (2, 4, P, T), F16, kind="Internal").ap()

        psum = ctx.enter_context(nc.psum_tensor("banks", [P, 8, 512], F32))
        SCO, TRA, OUT, MIS, UP, DN = 0, 2, 4, 5, 6, 7

        sems = {}

        def sem(name):
            if name not in sems:
                sems[name] = ctx.enter_context(nc.semaphore(name))
            return sems[name]

        stage = probs[:, :, :, :].rearrange("p a g t -> p (a g t)")
        s_in, s_stage, s_split, s_free, s_set, s_am, s_one, s_zero, s_rows = (
            ctx.enter_context(nc.semaphore(n)) for n in ("s_in", "s_stage", "s_split", "s_free", "s_set", "s_am", "s_one", "s_zero", "s_rows"))

        LOADS = [(SPLIT_AT["W1"][0], 4096), (SPLIT_AT["W2"][0], 4096), (SPLIT_AT["F1"][0], 3072), (SPLIT_AT["G2"][0], 2560)]

        with nc.Block() as block:
            @block.sync
            def _(sp):
                for dst, src in ((const, const_in), (wide, wide_in), (cols, cols_in), (latw, lat_in),
                                 (b2, b2_in), (am, am_in), (cons, cons_in)):
                    sp.dma_start(dst[:, :], src).then_inc(s_in, 16)
                sp.dma_start(rows[:, :], rows_in.broadcast_to([P, n_rows])).then_inc(s_in, 16)
                for n, (a, w) in enumerate(LOADS):
                    if n:
                        sp.wait_ge(s_free, n)
                    sp.dma_start(stage[:, 0:w], split_in[:, a:a + w]).then_inc(s_stage, 16)
                    if n == 0:
                        sp.wait_ge(s_one, 1)
                        sp.wait_ge(s_zero, 1)
                        for h in range(NH):
                            r = 32 * (h % GH) + 3
                            sp.dma_start(kp[r:r + 1, h, :], kc[0:1, 0, :]).then_inc(s_rows, 16)
                sp.wait_ge(s_rows, 16 * NH)

            @block.scalar
            def _(act):
                for n, (a, w) in enumerate(LOADS):
                    act.wait_ge(s_stage, 16 * (n + 1))
                    nc.scalar.activation(w_hi[:, a:a + w], stage[:, 0:w], ACT.Copy).then_inc(s_split, 1)

            @block.vector
            def _(dve):
                nc.vector.memset(ones[:, :], 1.0)
                nc.vector.memset(neghalf[:, :], -0.5)
                nc.vector.memset(qs, 0.0)
                nc.vector.memset(kc, 1.0).then_inc(s_one, 1)
                dve.wait_ge(s_in, 8 * 16)
                nc.vector.tensor_copy(ident16[:, :], C("ident"))
                nc.vector.tensor_copy(identb[:, :], C("ident"))
                nc.vector.tensor_copy(maskb[:, :], C("mask"))
                nc.vector.tensor_copy(maskTb[:, :], C("maskT"))
                nc.vector.tensor_scalar(ca_bo7[:, :], V("ca_bo"), CAUSAL_W, None, ALU.mult)
                nc.vector.tensor_scalar(half_s1[:, :], cols[:, COLS_AT["s1"][0]:COLS_AT["s1"][1]], 0.5, None, ALU.mult)
                nc.vector.scalar_tensor_tensor(out=s12[:, :], in0=cols[:, COLS_AT["s1"][0]:COLS_AT["s1"][1]], scalar=0.5,
                                               in1=cols[:, COLS_AT["s2"][0]:COLS_AT["s2"][1]], op0=ALU.mult, op1=ALU.mult)
                nc.vector.tensor_scalar(mc_bo15[:, :], V("mc_bo"), META_W, None, ALU.mult)
                nc.vector.tensor_tensor(out=t_a[:, 0:1], in0=V("cg_b"), in1=V("am_b"), op=ALU.add).then_inc(s_set, 1)
                dve.wait_ge(s_set, 1)
                dve.wait_ge(s_am, 1)
                nc.vector.tensor_tensor(out=t_b[:, 0:1], in0=psum[:, 0, 0:1], in1=t_a[:, 0:1], op=ALU.add).then_inc(s_set, 1)
                dve.wait_ge(s_set, 2)
                nc.vector.tensor_scalar(mod_bias[:, :], t_b[:, 0:1], 0.5, None, ALU.mult)
                for n, (a, w) in enumerate(LOADS):
                    dve.wait_ge(s_split, n + 1)
                    nc.vector.tensor_tensor(out=w_lo[:, a:a + w], in0=stage[:, 0:w], in1=w_hi[:, a:a + w],
                                            op=ALU.subtract).then_inc(s_free, 1)

            @block.tensor
            def _(pe):
                pe.wait_ge(s_in, 8 * 16)
                nc.tensor.matmul(psum[:, 0, 0:1], am[:, :], cons[:, :], start=True, stop=True).then_inc(s_am, 1)

            @block.gpsimd
            def _(pool):
                nc.gpsimd.memset(kp[:, :, :], 0.0).then_inc(s_zero, 1)
                nc.gpsimd.memset(vp[:, :, :, :], 0.0).then_inc(s_zero, 1)
                nc.gpsimd.memset(qm, 0.0)
                pool.wait_ge(s_zero, 2)
                nc.gpsimd.memset(vp[:, :, :, HD:HD + 1], 1.0)

        TAIL = {48: [(1, 0)], 49: [(1, 1)], 50: [(1, 2), (0, 0)], 51: [(1, 3), (0, 1)], 52: [(0, 2)], 53: [(0, 3)]}
        PRO, POST = 28, 8
        NSPREAD, NMIX = 12 + 6, 6
        LAG = 12
        NS = {0: 32, 1: 40, 2: 8}
        SCALE = {True: float(HD) ** -0.5, False: float(MD) ** -0.5}
        U = 8

        def main(st, gr):
            return st < 2 and gr < NG

        def width(st, c):
            return (P * (c + 1), P * c) if st == 0 else (T, 0)

        with nc.Fori(0, B) as i:
            with nc.Block() as block:
                @block.tensor
                def _(pe):
                    def mm(bank, cols_, lhsT, rhs, start, stop, rows_=slice(0, P), skip=False):
                        return nc.tensor.matmul(psum[rows_, bank, cols_], lhsT, rhs, start=start, stop=stop,
                                                skip_group_check=skip)

                    def transpose_x(L):
                        pe.wait_ge(sem(f"xn{L}"), 1)
                        for c in range(NC):
                            last = nc.tensor.transpose(psum[:, MIS, c * P:(c + 1) * P], xn[:, c, :], C("ident"))
                        last.then_inc(sem(f"xT_ps{L}"), 1)
                        pe.wait_ge(sem(f"xT{L}"), 1)

                    def project(bank, w, rhs, name):
                        mm(bank, slice(0, T), w, rhs, True, True).then_inc(sem(name), 1)

                    def values(bank, lhs, w, name, k=P):
                        for c in range(NC):
                            last = mm(bank, slice(c * P, (c + 1) * P), lhs[0:k, c * P:(c + 1) * P], w, True, True)
                        last.then_inc(sem(name), 1)

                    def three(bank, cols_, parts):
                        n = 3 * len(parts)
                        j = 0
                        for (a_hi, a_lo, b_hi, b_lo) in parts:
                            for a, b in ((a_hi, b_hi), (a_hi, b_lo), (a_lo, b_hi)):
                                last = mm(bank, cols_, a, b, j == 0, j == n - 1)
                                j += 1
                        return last

                    def score_unit(st, u):
                        gr, c, pair = u // U, (u % U) // 2, u % 2
                        if st == 1 and u == U * NG:
                            pe.wait_ge(sem("spread3"), 16 * NMIX)
                        kw, _ = width(st, c)
                        for s in range(2):
                            g = 2 * pair + s
                            if u:
                                pe.wait_ge(sem(f"max{st}"), 2 * u + s - 1)
                            if main(st, gr):
                                lhsT, rhs = qs[:, gr, c * P:(c + 1) * P], kp[:, GH * gr + g, 0:kw]
                            else:
                                lhsT, rhs = qc[0:96, g, c * P:(c + 1) * P], kc[0:96, g, 0:kw]
                            last = mm(SCO + s, slice(0, kw), lhsT, rhs, True, st != 0)
                            if st == 0:
                                last = mm(SCO + s, slice(kw - P, kw), identb[:, :], maskb[:, :], False, True)
                            last.then_inc(sem(f"score{st}"), 1)

                    def max_rows(st, gr):
                        pe.wait_ge(sem(f"max{st}"), 2 * U * (gr + 1))
                        if gr:
                            pe.wait_ge(sem(f"mrow{st}"), gr)
                        for c in range(NC):
                            last = mm(MIS, slice(c * P, (c + 1) * P), negmax[:, gr, c, :], ident16[:, :], True, True,
                                      rows_=slice(0, GH))
                        last.then_inc(sem(f"mrow_ps{st}"), 1)

                    def trans_unit(st, u):
                        gr, c, pair = u // U, (u % U) // 2, u % 2
                        if u % U == 0:
                            pe.wait_ge(sem(f"qm{st}_{gr}"), 16 * (1 if main(st, gr) else MH))
                        _, q0 = width(st, c)
                        for s in range(2):
                            g = 2 * pair + s
                            if u:
                                pe.wait_ge(sem(f"exp{st}"), 2 * u + s - 1)
                            if main(st, gr):
                                lhsT, rhs = kp[:, GH * gr + g, c * P:(c + 1) * P], qm[:, gr, q0:T]
                            else:
                                lhsT, rhs = kc[0:97, g, c * P:(c + 1) * P], qc[0:97, g, q0:T]
                            last = mm(TRA + s, slice(q0, T), lhsT, rhs, True, st != 0)
                            if st == 0:
                                last = mm(TRA + s, slice(q0, q0 + P), identb[:, :], maskTb[:, :], False, True)
                            last.then_inc(sem(f"trans{st}"), 1)

                    def value_step(st, kk):
                        gr, c = kk // NC, kk % NC
                        pe.wait_ge(sem(f"exp{st}"), GH * (kk + 1))
                        if c == 0:
                            if gr:
                                pe.wait_ge(sem(f"osb{st}"), gr)
                            if st == 1 and gr == NG:
                                pe.wait_ge(sem("h32_1"), HC)
                        _, q0 = width(st, c)
                        for g in range(GH):
                            r = slice(32 * g, 32 * g + 32)
                            if main(st, gr):
                                lhsT = vp[:, c, GH * gr + g, :]
                            else:
                                lhsT = vc[:, c, MD * g:MD * (g + 1)]
                            last = mm(OUT, slice(q0, T), lhsT, probs[:, kk % 2, g, q0:T], c == 0, c == NC - 1, rows_=r)
                        if not main(st, gr):
                            for g in range(GH):
                                r = slice(32 * g, 32 * g + 32)
                                last = mm(DN, slice(q0, T), ones[:, :], probs[:, kk % 2, g, q0:T], c == 0, c == NC - 1, rows_=r)
                        last.then_inc(sem(f"pv{st}"), 1)

                    def attention(st, pieces):
                        n = NS[st]
                        slots = n + LAG + 3
                        done = 0
                        for s in range(slots):
                            if st == 1 and s in TAIL:
                                for what, c in TAIL[s]:
                                    (heads_out if what else heads_back)(1, c)
                            if s < n:
                                score_unit(st, s)
                            want = -(-len(pieces) * (s + 1) // slots)
                            while done < (done + want + 1) // 2:
                                pieces[done][0](*pieces[done][1])
                                done += 1
                            if s % U == 1 and 0 < s <= n + 1:
                                max_rows(st, s // U - 1) if s >= U else None
                            if LAG <= s < n + LAG:
                                trans_unit(st, s - LAG)
                            while done < want:
                                pieces[done][0](*pieces[done][1])
                                done += 1
                            k = s - LAG - 2
                            if k > 0 and k % 2 == 1 and k // 2 < n // 2:
                                value_step(st, k // 2)

                    transpose_x(0)
                    for c in range(NC):
                        last = mm(DN, slice(LAT * c, LAT * c + LAT), xT[:, c * P:(c + 1) * P], W("dkv"), True, True)
                    last.then_inc(sem("lat_ps"), 1)
                    project(0, W("l0_q"), xT[:, :], "q_ps0")
                    project(1, W("l0_qr"), xT[:, :], "q_ps0")
                    for c in range(NC):
                        last = mm(2, slice(E * c, E * c + E), xT[:, c * P:(c + 1) * P], W("gate"), True, True)
                    last.then_inc(sem("lg_ps"), 1)

                    def up0(e, hc):
                        n = e * HC + hc
                        if n == 0:
                            pe.wait_ge(sem("xsplit0"), 1)
                        else:
                            pe.wait_ge(sem("relu"), n)
                        three(UP, slice(0, T), [(part(w_hi, "W1", n, P), part(w_lo, "W1", n, P), xh[:, :], xl[:, :])]) \
                            .then_inc(sem("up0"), 1)

                    def down0(e, c):
                        if c == 0:
                            pe.wait_ge(sem("h_lo0"), HC * (e + 1))
                            if e:
                                pe.wait_ge(sem("acc0"), e)
                            else:
                                pe.wait_ge(sem("latn"), 1)
                        t = slice(c * P, (c + 1) * P)
                        last = three(DN, t, [(h_hi[:, e % 2, hc, t], h_lo[:, e % 2, hc, t],
                                              part(w_hi, "W2", e * HC + hc, P), part(w_lo, "W2", e * HC + hc, P))
                                             for hc in range(HC)])
                        if c == NC - 1:
                            last.then_inc(sem("down0"), 1)

                    pieces = []
                    for e in range(E + 1):
                        for hc in range(HC):
                            if e < E:
                                pieces.append((up0, (e, hc)))
                            if e:
                                pieces.append((down0, (e - 1, hc)))
                    for f, a in pieces[:2]:
                        f(*a)
                    pe.wait_ge(sem("latn"), 1)
                    for c in range(NC):
                        last = nc.tensor.transpose(psum[0:LAT, 3, c * P:(c + 1) * P], latn[:, c, :], C("ident"))
                    last.then_inc(sem("latT_ps"), 1)
                    for f, a in pieces[2:4]:
                        f(*a)
                    pe.wait_ge(sem("latT"), 1)
                    pe.wait_ge(sem("rope_q"), 1)
                    project(0, latw[:, 0:128], latT[:, :], "k_ps0")
                    project(1, latw[:, 128:256], latT[:, :], "k_ps0")
                    values(MIS, latT, latw[:, 256:384], "v_ps0", k=LAT)
                    for f, a in pieces[4:PRO]:
                        f(*a)
                    pe.wait_ge(sem("spread0"), 16 * NSPREAD)
                    pe.wait_ge(sem("rope_k"), 1)
                    pe.wait_ge(sem("lg"), 1)
                    pe.wait_ge(sem("vp0"), 1)
                    attention(0, pieces[PRO:-POST])

                    def heads_out(L, c):
                        pe.wait_ge(sem(f"osb{L}"), NG)
                        pe.wait_ge(sem(f"max{L}"), 2 * NS[L])
                        if c >= 2:
                            pe.wait_ge(sem(f"onorm{L}"), c - 1)
                        for gr in range(NG):
                            last = nc.tensor.transpose(psum[:, SCO + c % 2, gr * P:(gr + 1) * P],
                                                       osb[:, gr, c * P:(c + 1) * P], C("ident"))
                        last.then_inc(sem(f"oq_ps{L}"), 1)

                    def heads_back(L, c):
                        pe.wait_ge(sem(f"onorm{L}"), c + 1)
                        if c == 0:
                            pe.wait_ge(sem(f"mrow{L}"), NS[L] // U)
                        last = nc.tensor.transpose(psum[:, MIS, c * P:(c + 1) * P],
                                                   onorm[:, c, :, :].rearrange("p h d -> p (h d)"), C("ident"))
                        if c == NC - 1:
                            last.then_inc(sem(f"oT_ps{L}"), 1)

                    post = pieces[-POST:]
                    for c in range(NC):
                        heads_out(0, c)
                        if c:
                            post[c - 1][0](*post[c - 1][1])
                            heads_back(0, c - 1)
                    for f, a in post[3:5]:
                        f(*a)
                    heads_back(0, NC - 1)
                    for f, a in post[5:]:
                        f(*a)
                    pe.wait_ge(sem("oT0"), 1)
                    pe.wait_ge(sem("gates"), 1)
                    for c in range(NC):
                        last = nc.tensor.transpose(psum[0:E, UP, c * P:(c + 1) * P], gates[:, c, :], C("ident"))
                    last.then_inc(sem("gT_ps"), 1)
                    pe.wait_ge(sem("gT"), 1)
                    pe.wait_ge(sem("onorm0"), NC)
                    for c in range(NC):
                        t = slice(c * P, (c + 1) * P)
                        mm(0, t, oT[:, t], W("l0_o"), True, False)
                        last = mm(0, t, gT[:, t], b2[:, :], False, True)
                    last.then_inc(sem("attn0"), 1)

                    transpose_x(1)
                    pe.wait_ge(sem("xin1"), 1)
                    project(0, W("l1_q"), xT[:, :], "q_ps1")
                    project(1, W("cg"), xT[:, :], "mod_ps")
                    project(2, W("l1_k"), xT[:, :], "k_ps1")
                    project(3, W("ca_q"), xT[:, :], "caq_ps")
                    project(4, W("ca_k"), xT[:, :], "cak_ps")
                    values(5, xT, W("l1_v"), "v_ps1")
                    values(7, xT, W("ca_v"), "cav_ps")

                    def gate1(o):
                        if o == 0:
                            pe.wait_ge(sem("xsplit1"), 1)
                            pe.wait_ge(sem("vc1"), 1)
                        else:
                            pe.wait_ge(sem("h32_1"), o)
                        three(UP, slice(0, T), [(part(w_hi, "F1", o, P), part(w_lo, "F1", o, P), xh[:, :], xl[:, :])]) \
                            .then_inc(sem("g1a"), 1)
                        three(DN, slice(0, T), [(part(w_hi, "F2", o, P), part(w_lo, "F2", o, P), xh[:, :], xl[:, :])]) \
                            .then_inc(sem("g1b"), 1)

                    def hidden(n, o, ic, name, src):
                        if ic == 0:
                            if o == 0:
                                pe.wait_ge(sem(f"hsplit{n}"), 1)
                            if n == 1 and o == 0:
                                pe.wait_ge(sem("h32_1"), HC)
                            else:
                                pe.wait_ge(sem("up_free"), HC * (n - 1) + o)
                        for j, (a, b) in enumerate(((w_hi, h_hi), (w_hi, h_lo), (w_lo, h_hi))):
                            wa, _ = SPLIT_AT[name]
                            last = mm(UP, slice(0, T), a[:, wa + ic * 512 + o * P:wa + ic * 512 + (o + 1) * P],
                                      b[:, src, ic, :], ic == 0 and j == 0, ic == HC - 1 and j == 2)
                        if ic == HC - 1:
                            last.then_inc(sem(f"hid{n}"), 1)

                    for o in range(HC):
                        gate1(o)
                    pe.wait_ge(sem("spread1"), 16 * NSPREAD)
                    for name in ("q_out1", "mod_e", "k32_1", "caq32", "cak32", "vp1"):
                        pe.wait_ge(sem(name), 1)
                    attention(1, [(hidden, (1, o, ic, "G1", 0)) for o in range(HC) for ic in range(HC)])
                    pe.wait_ge(sem("oc1"), 1)
                    project(OUT, W("ca_o"), oc[:, :], "mix_ps1")
                    pe.wait_ge(sem("ctx"), 1)
                    pe.wait_ge(sem("onorm1"), NC)
                    project(0, W("mc_q"), ctxT[:, :], "mcq_ps")
                    project(1, W("mc_k"), ctxT[:, :], "mck_ps")
                    values(2, ctxT, W("mc_v"), "mcv_ps")
                    hid2 = [(hidden, (2, o, ic, "G2", 1)) for o in range(HC) for ic in range(HC)]
                    for f, a in hid2[:4]:
                        f(*a)
                    pe.wait_ge(sem("spread2"), 16 * NMIX)
                    for name in ("mcq32", "mck32", "vc2"):
                        pe.wait_ge(sem(name), 1)
                    attention(2, hid2[4:])
                    pe.wait_ge(sem("oc2"), 1)
                    project(0, W("mc_o"), oc[:, :], "mix_ps2")
                    pe.wait_ge(sem("hsplit3"), 1)
                    pe.wait_ge(sem("up_free"), 8)
                    for c in range(NC):
                        t = slice(c * P, (c + 1) * P)
                        last = three(UP, t, [(h_hi[:, 0, hc, t], h_lo[:, 0, hc, t], part(w_hi, "F3", hc, P),
                                              part(w_lo, "F3", hc, P)) for hc in range(HC)])
                    last.then_inc(sem("y3"), 1)
                    pe.wait_ge(sem("ctx2"), 1)
                    for c in range(NC):
                        t = slice(c * P, (c + 1) * P)
                        last = mm(1, t, ctxT[:, t], W("l1_o"), True, True)
                    last.then_inc(sem("attn1"), 1)

                @block.vector
                def _(dve):
                    count = [0]

                    def link(ins):
                        count[0] += 1
                        ins.then_inc(sem("dve_chain"), 1)
                        dve.wait_ge(sem("dve_chain"), count[0])

                    v = nc.vector

                    def norm_stats(src, n, tag):
                        for c in range(NC):
                            ins = v.bn_stats(stats[:, c, :], src(c))
                        link(ins)
                        for c in range(NC):
                            ins = v.bn_aggr(mv[:, c, :], stats[:, c, :])
                        link(ins)
                        v.tensor_scalar(ve[:, :], mv[:, :, 1], EPS, None, ALU.add).then_inc(sem(f"ve{tag}"), 1)
                        dve.wait_ge(sem(f"rstd{tag}"), 1)

                    def layer_norm(L):
                        norm_stats(lambda c: x[:, c, :], D, f"x{L}")
                        for c in range(NC):
                            ins = v.tensor_scalar(xn[:, c, :], x[:, c, :], mv[:, c, 0:1], rstd[:, c:c + 1],
                                                  ALU.subtract, ALU.mult)
                        ins.then_inc(sem(f"xn{L}"), 1)
                        dve.wait_ge(sem(f"xT{L}"), 1)
                        link(v.tensor_copy(xh[:, :], xT[:, :]))
                        v.tensor_tensor(out=xl[:, :], in0=xT[:, :], in1=xh[:, :], op=ALU.subtract) \
                            .then_inc(sem(f"xsplit{L}"), 1)

                    def halves(src, w, at, name):
                        link(v.tensor_copy(parts[:, w, at, :], src[:, :]))
                        v.tensor_tensor(out=parts[:, w, at + 1, :], in0=src[:, :], in1=parts[:, w, at, :], op=ALU.subtract) \
                            .then_inc(sem(name), 1)

                    def reduce_unit(st, u):
                        gr, c, pair = u // U, (u % U) // 2, u % 2
                        kw, _ = width(st, c)
                        for s in range(2):
                            dve.wait_ge(sem(f"score{st}"), 2 * u + s + 1)
                            g = 2 * pair + s
                            v.tensor_reduce(negmax[:, gr, c, g:g + 1], psum[:, SCO + s, 0:kw],
                                            AX.X, ALU.max, negate=True).then_inc(sem(f"max{st}"), 1)

                    def max_out(st, gr):
                        dve.wait_ge(sem(f"mrow_ps{st}"), gr + 1)
                        if gr >= 2:
                            dve.wait_ge(sem(f"qm{st}_{gr - 2}"), 16)
                        v.tensor_copy(mrow[:, gr % 2, :], psum[0:GH, MIS, :]).then_inc(sem(f"mrow{st}"), 1)

                    def mixing_out(st):
                        dve.wait_ge(sem(f"pv{st}"), NS[st] // 2)
                        link(v.reciprocal(t_b[:, :], psum[:, DN, :]))
                        v.tensor_tensor(out=oc[:, :], in0=psum[:, OUT, :], in1=t_b[:, :], op=ALU.mult) \
                            .then_inc(sem(f"oc{st}"), 1)

                    def heads_norm(L, c):
                        dve.wait_ge(sem(f"oq_ps{L}"), c + 1)
                        bank = psum[:, SCO + c % 2, :].rearrange("p (h r) -> p h r", r=32)
                        link(v.reciprocal(rden[:, c, :], bank[:, :, HD]))
                        v.tensor_tensor(out=onorm[:, c, :, :], in0=bank[:, :, 0:HD],
                                        in1=rden[:, c, :].unsqueeze(2).broadcast_to([P, NH, HD]),
                                        op=ALU.mult).then_inc(sem(f"onorm{L}"), 1)

                    dve.wait_ge(sem("x_in"), 16)
                    layer_norm(0)
                    dve.wait_ge(sem("lat_ps"), 1)
                    norm_stats(lambda c: psum[:, DN, LAT * c:LAT * c + LAT], LAT, "lat")
                    for c in range(NC):
                        ins = v.tensor_scalar(latn[:, c, :], psum[:, DN, LAT * c:LAT * c + LAT], mv[:, c, 0:1],
                                              rstd[:, c:c + 1], ALU.subtract, ALU.mult)
                    ins.then_inc(sem("latn"), 1)
                    dve.wait_ge(sem("q_ps0"), 2)
                    v.tensor_tensor(out=t_a[:, :], in0=psum[:, 0, :], in1=C("cos"), op=ALU.mult)
                    link(v.tensor_tensor(out=t_b[:, :], in0=psum[:, 1, :], in1=C("sin"), op=ALU.mult))
                    ins = v.tensor_tensor(out=q32[:, :], in0=t_a[:, :], in1=t_b[:, :], op=ALU.add)
                    ins.then_inc(sem("rope_q"), 1)
                    dve.wait_ge(sem("rope_q"), 1)
                    halves(q32, 0, 0, "qsplit0")
                    dve.wait_ge(sem("latT_ps"), 1)
                    v.tensor_scalar(latT[:, :], psum[0:LAT, 3, :], V("gamma", n=LAT), V("beta", n=LAT),
                                    ALU.mult, ALU.add).then_inc(sem("latT"), 1)
                    dve.wait_ge(sem("k_ps0"), 2)
                    v.tensor_tensor(out=t_a[:, :], in0=psum[:, 0, :], in1=C("cos"), op=ALU.mult)
                    link(v.tensor_tensor(out=t_b[:, :], in0=psum[:, 1, :], in1=C("sin"), op=ALU.mult))
                    v.tensor_tensor(out=k32[:, :], in0=t_a[:, :], in1=t_b[:, :], op=ALU.add).then_inc(sem("rope_k"), 1)
                    dve.wait_ge(sem("rope_k"), 1)
                    halves(k32, 0, 2, "ksplit0")
                    dve.wait_ge(sem("lg_ps"), 1)
                    link(v.tensor_tensor(out=lg[:, :, :], in0=psum[:, 2, 0:NC * E].rearrange("p (c e) -> p c e", e=E),
                                         in1=R("bg").unsqueeze(1).broadcast_to([P, NC, E]), op=ALU.add))
                    mine = lg[:, :, :].unsqueeze(3).broadcast_to([P, NC, E, E])
                    other = lg[:, :, :].unsqueeze(2).broadcast_to([P, NC, E, E])
                    tri = C("tri").rearrange("p (e f) -> p e f", f=E)
                    v.tensor_tensor(out=cmp1[:, :, :, :], in0=other, in1=mine, op=ALU.is_gt)
                    link(v.tensor_tensor(out=cmp2[:, :, :, :], in0=other, in1=mine, op=ALU.is_equal))
                    for c in range(NC):
                        ins = v.tensor_tensor(out=cmp2[:, c, :, :], in0=cmp2[:, c, :, :], in1=tri, op=ALU.mult)
                    link(ins)
                    link(v.tensor_tensor(out=cmp1[:, :, :, :], in0=cmp1[:, :, :, :], in1=cmp2[:, :, :, :], op=ALU.add))
                    link(v.tensor_reduce(gates[:, :, :], cmp1[:, :, :, :], AX.X, ALU.add))
                    v.tensor_scalar(gates[:, :, :], gates[:, :, :], 1.5, None, ALU.is_lt)
                    link(v.tensor_reduce(gmax[:, :], lg[:, :, :], AX.X, ALU.max))
                    v.tensor_tensor(out=lg[:, :, :], in0=lg[:, :, :], in1=gmax[:, :].unsqueeze(2).broadcast_to([P, NC, E]),
                                    op=ALU.subtract).then_inc(sem("lg"), 1)
                    dve.wait_ge(sem("gex"), 1)
                    link(v.tensor_tensor(out=gates[:, :, :], in0=gates[:, :, :], in1=gex[:, :, :], op=ALU.mult))
                    link(v.tensor_reduce(gsum[:, :], gates[:, :, :], AX.X, ALU.add))
                    link(v.reciprocal(gsum[:, :], gsum[:, :]))
                    v.tensor_tensor(out=gates[:, :, :], in0=gates[:, :, :], in1=gsum[:, :].unsqueeze(2).broadcast_to([P, NC, E]),
                                    op=ALU.mult).then_inc(sem("gates"), 1)
                    dve.wait_ge(sem("gates"), 1)

                    hid = [0]

                    def hidden_hi(e, hc):
                        dve.wait_ge(sem("relu"), e * HC + hc + 1)
                        if hc == 0 and e >= 2:
                            dve.wait_ge(sem("down0"), e - 1)
                        v.tensor_copy(h_hi[:, e % 2, hc, :], h32[:, hc, :]).then_inc(sem("h_hi0"), 1)

                    def add_expert(e):
                        dve.wait_ge(sem("down0"), e + 1)
                        for c in range(NC):
                            ins = v.scalar_tensor_tensor(out=x[:, c, :], in0=psum[:, DN, c * P:(c + 1) * P],
                                                         scalar=gates[:, c, e:e + 1], in1=x[:, c, :],
                                                         op0=ALU.mult, op1=ALU.add)
                        ins.then_inc(sem("acc0"), 1)
                        dve.wait_ge(sem("acc0"), e + 1)

                    pieces = []
                    for e in range(E + 1):
                        for hc in range(HC):
                            if e < E:
                                pieces.append((hidden_hi, (e, hc)))
                            if e:
                                pieces.append((add_expert, (e - 1,)) if hc == HC - 1 else None)

                    def attention(st, pieces):
                        n = NS[st]
                        slots = n + LAG + 3
                        done = 0
                        for s in range(slots):
                            if st == 1 and s in TAIL:
                                for what, c in TAIL[s]:
                                    if what:
                                        heads_norm(1, c)
                            if s < n:
                                reduce_unit(st, s)
                            want = -(-len(pieces) * (s + 1) // slots)
                            if s % U == 1 and U <= s <= n + 1:
                                max_out(st, s // U - 1)
                            while done < want:
                                if pieces[done] is not None:
                                    pieces[done][0](*pieces[done][1])
                                done += 1

                    for piece in pieces[:PRO]:
                        if piece is not None:
                            piece[0](*piece[1])
                    attention(0, pieces[PRO:-POST])
                    post = pieces[-POST:]
                    for c in range(NC):
                        heads_norm(0, c)
                        if c and post[c - 1] is not None:
                            post[c - 1][0](*post[c - 1][1])
                    for piece in post[3:]:
                        if piece is not None:
                            piece[0](*piece[1])
                    dve.wait_ge(sem("attn0"), 1)
                    xf = x[:, :, :].rearrange("p c d -> p (c d)")
                    v.tensor_tensor(out=xf, in0=xf, in1=psum[:, 0, :], op=ALU.add).then_inc(sem("xin1"), 1)
                    dve.wait_ge(sem("xin1"), 1)

                    layer_norm(1)
                    dve.wait_ge(sem("mod_e"), 1)
                    link(v.tensor_scalar(t_a[:, :], t_a[:, :], 0.5, 0.5, ALU.mult, ALU.add))
                    dve.wait_ge(sem("q_ps1"), 1)
                    v.scalar_tensor_tensor(out=q32[:, :], in0=psum[:, 0, :], scalar=V("bq"), in1=t_a[:, :],
                                           op0=ALU.add, op1=ALU.mult).then_inc(sem("q_out1"), 1)
                    dve.wait_ge(sem("q_out1"), 1)
                    halves(q32, 0, 0, "qsplit1")
                    dve.wait_ge(sem("k32_1"), 1)
                    halves(k32, 0, 2, "ksplit1")
                    dve.wait_ge(sem("v_ps1"), 1)
                    for c in range(NC):
                        ins = v.tensor_tensor(out=vp[:, c, :, 0:HD],
                                              in0=psum[:, 5, c * P:(c + 1) * P].rearrange("p (h d) -> p h d", d=HD),
                                              in1=R("bv").rearrange("p (h d) -> p h d", d=HD), op=ALU.add)
                    ins.then_inc(sem("vp1"), 1)
                    dve.wait_ge(sem("cav_ps"), 1)
                    v.tensor_tensor(out=vc[:, :, :], in0=psum[:, 7, :].rearrange("p (c d) -> p c d", d=D),
                                    in1=R("ca_bv").unsqueeze(1).broadcast_to([P, NC, D]), op=ALU.add) \
                        .then_inc(sem("vc1"), 1)
                    dve.wait_ge(sem("caq32"), 1)
                    halves(q32, 1, 0, "qsplit3")
                    dve.wait_ge(sem("cak32"), 1)
                    halves(k32, 1, 2, "ksplit3")

                    def gate_out(o):
                        dve.wait_ge(sem("silu_e"), o + 1)
                        link(v.scalar_tensor_tensor(out=t_b[:, :], in0=t_b[:, :], scalar=1.0, in1=psum[:, UP, :],
                                                    op0=ALU.add, op1=ALU.mult))
                        dve.wait_ge(sem("g1b"), o + 1)
                        v.scalar_tensor_tensor(out=h32[:, o, :], in0=psum[:, DN, :], scalar=s12[:, o:o + 1], in1=t_b[:, :],
                                               op0=ALU.mult, op1=ALU.mult).then_inc(sem("h32_1"), 1)
                        dve.wait_ge(sem("h32_1"), o + 1)
                        link(v.tensor_copy(h_hi[:, 0, o, :], h32[:, o, :]))
                        ins = v.tensor_tensor(out=h_lo[:, 0, o, :], in0=h32[:, o, :], in1=h_hi[:, 0, o, :], op=ALU.subtract)
                        if o == HC - 1:
                            ins.then_inc(sem("hsplit1"), 1)
                            ins = None

                    def hidden_out(n, o):
                        dve.wait_ge(sem(f"hid{n}"), o + 1)
                        if n == 1 and o == 0:
                            dve.wait_ge(sem("hsplit1"), 1)
                        if n == 2 and o == 0:
                            dve.wait_ge(sem("hsplit2"), 1)
                        v.tensor_scalar(h32[:, o, :], psum[:, UP, :], V(f"hs{n}", o), None, ALU.mult) \
                            .then_inc(sem("up_free"), 1)

                    def gelu_parts(n, dst):
                        dve.wait_ge(sem(f"gelu{n}"), 1)
                        for o in range(HC):
                            ins = v.tensor_copy(h_hi[:, dst, o, :], h32[:, o, :])
                        link(ins)
                        for o in range(HC):
                            ins = v.tensor_tensor(out=h_lo[:, dst, o, :], in0=h32[:, o, :], in1=h_hi[:, dst, o, :],
                                                  op=ALU.subtract)
                        ins.then_inc(sem(f"hsplit{n + 1}"), 1)

                    for o in range(HC):
                        gate_out(o)
                    attention(1, [((hidden_out, (1, o)) if ic == HC - 1 else None) for o in range(HC) for ic in range(HC)])
                    mixing_out(1)
                    dve.wait_ge(sem("mix1"), 1)
                    dve.wait_ge(sem("oT1"), 1)
                    v.scalar_tensor_tensor(out=ctxT[:, :], in0=oT[:, :], scalar=1.0 - CAUSAL_W, in1=t_a[:, :],
                                           op0=ALU.mult, op1=ALU.add).then_inc(sem("ctx"), 1)
                    dve.wait_ge(sem("mcq32"), 1)
                    halves(q32, 1, 0, "qsplit2")
                    dve.wait_ge(sem("mck32"), 1)
                    halves(k32, 1, 2, "ksplit2")
                    dve.wait_ge(sem("mcv_ps"), 1)
                    v.tensor_tensor(out=vc[:, :, :], in0=psum[:, 2, :].rearrange("p (c d) -> p c d", d=D),
                                    in1=R("mc_bv").unsqueeze(1).broadcast_to([P, NC, D]), op=ALU.add) \
                        .then_inc(sem("vc2"), 1)
                    gelu_parts(1, 1)
                    hid2 = [((hidden_out, (2, o)) if ic == HC - 1 else None) for o in range(HC) for ic in range(HC)]
                    hid2[3][0](*hid2[3][1])
                    attention(2, hid2[4:])
                    mixing_out(2)
                    gelu_parts(2, 0)
                    dve.wait_ge(sem("mix2"), 1)
                    v.scalar_tensor_tensor(out=ctxT[:, :], in0=ctxT[:, :], scalar=1.0 - META_W, in1=t_a[:, :],
                                           op0=ALU.mult, op1=ALU.add).then_inc(sem("ctx2"), 1)
                    dve.wait_ge(sem("y3"), 1)
                    t4 = t_b[:, :].rearrange("p (c d) -> p c d", d=D)
                    link(v.tensor_tensor(out=t4, in0=psum[:, UP, :].rearrange("p (c d) -> p c d", d=D),
                                         in1=R("s3").unsqueeze(1).broadcast_to([P, NC, D]), op=ALU.mult))
                    link(v.tensor_tensor(out=xf, in0=xf, in1=t_b[:, :], op=ALU.add))
                    link(v.tensor_tensor(out=x[:, :, :], in0=x[:, :, :], in1=R("bo").unsqueeze(1).broadcast_to([P, NC, D]),
                                         op=ALU.add))
                    dve.wait_ge(sem("attn1"), 1)
                    v.tensor_tensor(out=xf, in0=xf, in1=psum[:, 1, :], op=ALU.add).then_inc(sem("x_out"), 1)

                @block.scalar
                def _(act):
                    a = nc.scalar

                    def exp_unit(st, u):
                        gr, c, pair = u // U, (u % U) // 2, u % 2
                        _, q0 = width(st, c)
                        kk = u // 2
                        if kk >= 2 and pair == 0:
                            act.wait_ge(sem(f"pv{st}"), kk - 1)
                        for s in range(2):
                            act.wait_ge(sem(f"trans{st}"), 2 * u + s + 1)
                            a.activation(probs[:, kk % 2, 2 * pair + s, q0:T], psum[:, TRA + s, q0:T],
                                         ACT.Exp, scale=SCALE[main(st, gr)]).then_inc(sem(f"exp{st}"), 1)

                    def out_group(st, gr):
                        act.wait_ge(sem(f"pv{st}"), NC * (gr + 1))
                        a.activation(osb[:, gr, :], psum[:, OUT, :], ACT.Copy).then_inc(sem(f"osb{st}"), 1)

                    def relu(e, hc):
                        act.wait_ge(sem("up0"), e * HC + hc + 1)
                        if e:
                            act.wait_ge(sem("h_lo0"), HC * (e - 1) + hc + 1)
                        a.activation(h32[:, hc, :], psum[:, UP, :], ACT.Relu, bias=V("b1", e * HC + hc)) \
                            .then_inc(sem("relu"), 1)

                    def attention(st, pieces):
                        n = NS[st]
                        slots = n + LAG + 3
                        done = 0
                        for s in range(slots):
                            want = -(-len(pieces) * (s + 1) // slots)
                            while done < (done + want + 1) // 2:
                                if pieces[done] is not None:
                                    pieces[done][0](*pieces[done][1])
                                done += 1
                            if LAG <= s < n + LAG:
                                exp_unit(st, s - LAG)
                            while done < want:
                                if pieces[done] is not None:
                                    pieces[done][0](*pieces[done][1])
                                done += 1
                            k = s - LAG - 2
                            if k > 0 and k % U == 7 and main(st, k // U) and k // U < n // U:
                                out_group(st, k // U)

                    def move(dst, bank, name, rows_=P, wait=None):
                        act.wait_ge(sem(wait), 1)
                        a.activation(dst, psum[0:rows_, bank, :], ACT.Copy).then_inc(sem(name), 1)

                    move(xT[:, :], MIS, "xT0", wait="xT_ps0")
                    pieces = []
                    for e in range(E + 1):
                        for hc in range(HC):
                            if e < E:
                                pieces.append((relu, (e, hc)))
                            if e:
                                pieces.append(None)
                    for f, ar in pieces[:4]:
                        f(*ar)
                    act.wait_ge(sem("v_ps0"), 1)
                    for c in range(NC):
                        ins = a.activation(vp[:, c, :, 0:HD], psum[:, MIS, c * P:(c + 1) * P]
                                           .rearrange("p (h d) -> p h d", d=HD), ACT.Copy)
                    ins.then_inc(sem("vp0"), 1)
                    act.wait_ge(sem("lg"), 1)
                    a.activation(gex[:, :, :], lg[:, :, :], ACT.Exp).then_inc(sem("gex"), 1)
                    for piece in pieces[4:PRO]:
                        if piece is not None:
                            piece[0](*piece[1])
                    attention(0, pieces[PRO:-POST])
                    for piece in pieces[-POST:]:
                        if piece is not None:
                            piece[0](*piece[1])
                    move(oT[:, :], MIS, "oT0", wait="oT_ps0")
                    move(gT[:, :], UP, "gT", rows_=E, wait="gT_ps")

                    move(xT[:, :], MIS, "xT1", wait="xT_ps1")
                    act.wait_ge(sem("mod_ps"), 1)
                    a.activation(t_a[:, :], psum[:, 1, :], ACT.Tanh, scale=0.5, bias=mod_bias[:, :]).then_inc(sem("mod_e"), 1)
                    act.wait_ge(sem("mod_e"), 1)
                    act.wait_ge(sem("k_ps1"), 1)
                    a.activation(k32[:, :], psum[:, 2, :], ACT.Identity, bias=V("bk")).then_inc(sem("k32_1"), 1)
                    act.wait_ge(sem("caq_ps"), 1)
                    act.wait_ge(sem("qsplit1"), 1)
                    a.activation(q32[:, :], psum[:, 3, :], ACT.Identity, bias=V("ca_bq")).then_inc(sem("caq32"), 1)
                    act.wait_ge(sem("cak_ps"), 1)
                    act.wait_ge(sem("ksplit1"), 1)
                    a.activation(k32[:, :], psum[:, 4, :], ACT.Identity, bias=V("ca_bk")).then_inc(sem("cak32"), 1)

                    def silu_e(o):
                        act.wait_ge(sem("g1a"), o + 1)
                        if o:
                            act.wait_ge(sem("h32_1"), o)
                        a.activation(t_b[:, :], psum[:, UP, :], ACT.Tanh, scale=half_s1[:, o:o + 1]).then_inc(sem("silu_e"), 1)

                    for o in range(HC):
                        silu_e(o)
                    attention(1, [])
                    move(oT[:, :], MIS, "oT1", wait="oT_ps1")
                    act.wait_ge(sem("mix_ps1"), 1)
                    a.activation(t_a[:, :], psum[:, OUT, :], ACT.Identity, scale=CAUSAL_W, bias=ca_bo7[:, :]).then_inc(sem("mix1"), 1)
                    act.wait_ge(sem("mcq_ps"), 1)
                    a.activation(q32[:, :], psum[:, 0, :], ACT.Identity, bias=V("mc_bq")).then_inc(sem("mcq32"), 1)
                    act.wait_ge(sem("mck_ps"), 1)
                    a.activation(k32[:, :], psum[:, 1, :], ACT.Identity, bias=V("mc_bk")).then_inc(sem("mck32"), 1)
                    act.wait_ge(sem("up_free"), HC)
                    a.activation(h32[:, :, :], h32[:, :, :], ACT.Gelu).then_inc(sem("gelu1"), 1)
                    attention(2, [])
                    act.wait_ge(sem("up_free"), 2 * HC)
                    a.activation(h32[:, :, :], h32[:, :, :], ACT.Gelu).then_inc(sem("gelu2"), 1)
                    act.wait_ge(sem("mix_ps2"), 1)
                    a.activation(t_a[:, :], psum[:, 0, :], ACT.Identity, scale=META_W, bias=mc_bo15[:, :]).then_inc(sem("mix2"), 1)

                @block.gpsimd
                def _(pool):
                    def inverse_root(tag):
                        pool.wait_ge(sem(f"ve{tag}"), 1)
                        nc.gpsimd.tensor_tensor(out=rstd[:, :], in0=ve[:, :], in1=neghalf[:, :], op=ALU.pow) \
                            .then_inc(sem(f"rstd{tag}"), 1)

                    inverse_root("x0")
                    inverse_root("lat")
                    for n in range(E * HC):
                        e, hc = n // HC, n % HC
                        pool.wait_ge(sem("h_hi0"), n + 1)
                        nc.gpsimd.tensor_tensor(out=h_lo[:, e % 2, hc, :], in0=h32[:, hc, :], in1=h_hi[:, e % 2, hc, :],
                                                op=ALU.subtract).then_inc(sem("h_lo0"), 1)
                    inverse_root("x1")

                @block.sync
                def _(sp):
                    def relayed(w, first, n):
                        sp.dma_start(relay[w, first:first + 2].rearrange("a p t -> p a t"), parts[:, w, first:first + 2, :]) \
                            .then_inc(sem(f"relay{w}_{first}"), 16)

                    def spread_main(L):
                        k = "p (g d) t"
                        sp.wait_ge(sem(f"ksplit{L}"), 1)
                        relayed(0, 2, L)
                        sp.wait_ge(sem(f"qsplit{L}"), 1)
                        relayed(0, 0, L)
                        sp.wait_ge(sem("relay0_2"), 16 * (L + 1))
                        for g in range(GH):
                            for j, a in enumerate((2, 3, 2)):
                                src = relay[0, a].rearrange("(m g d) t -> g d m t", g=GH, d=HD)[g]
                                dst = kp[32 * g + j:32 * g + 32:4, g:NH:GH, :]
                                sp.dma_start(dst, src).then_inc(sem(f"spread{L}"), 16)
                        sp.wait_ge(sem("relay0_0"), 16 * (L + 1))
                        for j, a in enumerate((0, 0, 1)):
                            src = relay[0, a].rearrange("(m r) t -> r m t", r=32)
                            for w in range(2):
                                sp.dma_start(qsm[j:P:4, w, :, :], src).then_inc(sem(f"spread{L}"), 16)

                    def spread_mixing(n, st):
                        sp.wait_ge(sem(f"qsplit{n}"), 1)
                        sp.wait_ge(sem(f"ksplit{n}"), 1)
                        relayed(1, 0, 0)
                        relayed(1, 2, 0)
                        if st == 2:
                            sp.wait_ge(sem("trans1"), 2 * NS[1])
                        sp.wait_ge(sem("relay1_0"), 16 * st)
                        sp.wait_ge(sem("relay1_2"), 16 * st)
                        for j, (a, b) in enumerate(((0, 2), (0, 3), (1, 2))):
                            for w, part_ in ((0, a), (1, b)):
                                sp.dma_start(qkc[32 * j:32 * j + 32, w, :, :],
                                             relay[1, part_].rearrange("(h d) t -> d h t", d=MD)).then_inc(sem(f"spread{n}"), 16)

                    def max_rows(st, gr):
                        sp.wait_ge(sem(f"mrow{st}"), gr + 1)
                        if main(st, gr):
                            sp.dma_start(qm[3:P:32, gr, :], mrow[:, gr % 2, :]).then_inc(sem(f"qm{st}_{gr}"), 16)
                        else:
                            for h in range(MH):
                                sp.dma_start(qc[96:97, h, :], mrow[h:h + 1, gr % 2, :]).then_inc(sem(f"qm{st}_{gr}"), 16)

                    sp.dma_start(x[:, :, :], x_in[bass.ds(i, 1)].rearrange("b (c p) d -> p (b c) d", p=P)).then_inc(sem("x_in"), 16)
                    spread_main(0)
                    for gr in range(NG):
                        max_rows(0, gr)
                    spread_main(1)
                    spread_mixing(3, 1)
                    for gr in range(NG + 1):
                        max_rows(1, gr)
                    spread_mixing(2, 2)
                    max_rows(2, 0)
                    sp.wait_ge(sem("x_out"), 1)
                    sp.dma_start(out[bass.ds(i, 1)].rearrange("b (c p) d -> p (b c) d", p=P), x[:, :, :]).then_inc(sem("stored"), 16)
                    sp.wait_ge(sem("stored"), 16)

            numbers = sorted(s.num for s in sems.values())
            assert numbers == list(range(numbers[0], numbers[0] + len(numbers)))
            nc.sync.sem_clear(range(numbers[0], numbers[-1] + 1))
            nc.all_engine_barrier()


def kernel(**inputs):
    import numpy as _np
    import concourse.bacc as _bacc
    from concourse import mybir as _mybir
    from concourse.bass_utils import run_bass_kernel_spmd as _run

    a = {n: _np.asarray(v) for n, v in inputs.items()}
    f32 = _np.float32

    def swapped(w):
        return w.reshape(w.shape[0], NH, 2, HD // 2)[:, :, ::-1].reshape(w.shape[0], 128)

    ca, mc = a["L1_attn_ca_Win"], a["L1_attn_mc_Win"]
    cab, mcb = a["L1_attn_ca_bin"], a["L1_attn_mc_bin"]
    wide = _np.concatenate([
        a["L0_attn_W_q"], swapped(a["L0_attn_W_q"]), a["L0_attn_W_o"], a["L1_attn_Wq"], a["L1_attn_Wk"], a["L1_attn_Wv"],
        _np.repeat(a["L1_attn_cg_W"], HD, axis=1), a["L1_attn_Wo"], ca, a["L1_attn_ca_Wout"], mc, a["L1_attn_mc_Wout"],
        a["L0_attn_W_dkv"], a["L0_ffn_Wg"]], axis=1)
    latw = _np.concatenate([a["L0_attn_W_uk"], swapped(a["L0_attn_W_uk"]), a["L0_attn_W_uv"]], axis=1)

    def column(v):
        return v.reshape(-1, 128).T

    def padded(v):
        z = _np.zeros((128, 1), f32)
        z[:v.shape[0], 0] = v
        return z

    cols = _np.concatenate([
        column(a["L1_attn_bq"]), column(a["L1_attn_bk"]), column(cab[:128]), column(cab[128:256]),
        column(mcb[:128]), column(mcb[128:256]), column(a["L1_attn_ca_bout"]), column(a["L1_attn_mc_bout"]),
        column(_np.repeat(a["L1_attn_cg_b"], HD)), column(_np.repeat(a["L1_attn_am_b"], HD)),
        padded(a["L0_attn_ln_gamma"]), padded(a["L0_attn_ln_beta"]), column(a["L0_ffn_b1"]),
        column(a["L1_ffn_w1_s"]), column(a["L1_ffn_w2_s"]), column(a["L1_ffn_h1_s"]), column(a["L1_ffn_h2_s"])], axis=1)
    rows = _np.concatenate([a["L1_attn_bv"], cab[256:], mcb[256:], a["L1_attn_bo"], a["L1_ffn_w3_s"], a["L0_ffn_bg"]])[None]

    def chunks(w):
        return w.reshape(-1, 128, w.shape[-1]).transpose(1, 0, 2).reshape(128, -1)

    split = _np.concatenate([
        a["L0_ffn_W1"].transpose(1, 0, 2).reshape(128, -1), chunks(a["L0_ffn_W2"].reshape(-1, 128)),
        a["L1_ffn_w1_w"].T, a["L1_ffn_w2_w"].T, chunks(a["L1_ffn_h1_w"].T), chunks(a["L1_ffn_h2_w"].T),
        chunks(a["L1_ffn_w3_w"].T)], axis=1)
    arrays = dict(x_in=a["L0_attn_x"], wide_in=wide, lat_in=latw, cols_in=cols, rows_in=rows, const_in=constants(),
                  split_in=split, am_in=_np.repeat(a["L1_attn_am_W"], HD, axis=1), cons_in=a["L1_attn_cons_vec"][:, None],
                  b2_in=a["L0_ffn_b2"])
    arrays = {n: _np.ascontiguousarray(v) for n, v in arrays.items()}
    nc = _bacc.Bacc("TRN2", target_bir_lowering=False, num_devices=1)
    args = {n: nc.dram_tensor(n, v.shape, _mybir.dt.from_np(v.dtype), kind="ExternalInput").ap() for n, v in arrays.items()}
    out = nc.dram_tensor("out", (B, T, D), F32, kind="ExternalOutput").ap()
    build(nc, out=out, **args)
    r = _run(nc, [arrays], core_ids=[0])
    return r.results[0]["out"]
```

```python
from contextlib import ExitStack

import numpy as np

import concourse.bass as bass
from concourse import mybir

P = 128
F32 = mybir.dt.float32
F16 = mybir.dt.float16
BF16 = mybir.dt.bfloat16
ACT = mybir.ActivationFunctionType
ALU = mybir.AluOpType
AX = mybir.AxisListType

B, T, D = 8, 512, 128
NC = T // P
NH, HD = 16, 8
NG, GH = 4, 4
MH, MD = 4, 32
E, HC = 8, 4
LAT = 32
EPS = 1e-5
CAUSAL_W = 0.7
META_W = (0.9 - 0.8) / 0.2 * 0.3

WIDE = [("l0_q", 128), ("l0_qr", 128), ("l0_o", 128), ("l1_q", 128), ("l1_k", 128), ("l1_v", 128),
        ("cg", 128), ("l1_o", 128), ("ca_q", 128), ("ca_k", 128), ("ca_v", 128), ("ca_o", 128),
        ("mc_q", 128), ("mc_k", 128), ("mc_v", 128), ("mc_o", 128), ("dkv", LAT), ("gate", E)]
COLS = [("bq", 1), ("bk", 1), ("ca_bq", 1), ("ca_bk", 1), ("mc_bq", 1), ("mc_bk", 1),
        ("ca_bo", 1), ("mc_bo", 1), ("cg_b", 1), ("am_b", 1), ("gamma", 1), ("beta", 1),
        ("b1", E * HC), ("s1", HC), ("s2", HC), ("hs1", HC), ("hs2", HC)]
ROWS = [("bv", 128), ("ca_bv", 128), ("mc_bv", 128), ("bo", 128), ("s3", 128), ("bg", E)]
CONST = [("ident", 128), ("mask", 128), ("maskT", 128), ("tri", E * E), ("cos", T), ("sin", T)]
SPLIT = [("W1", E * 512), ("W2", E * 512), ("F1", 512), ("F2", 512), ("G1", 2048), ("G2", 2048),
         ("F3", 512)]


def places(parts):
    at, out = 0, {}
    for name, n in parts:
        out[name] = (at, at + n)
        at += n
    return out, at


def constants():
    ident = np.eye(P, dtype=np.float32)
    q, k = np.arange(P)[:, None], np.arange(P)[None, :]
    mask = np.where(k > q, np.float32(-1e30), np.float32(0))
    e = np.arange(E)
    tri = np.broadcast_to((e[None, :] < e[:, None]).astype(np.float32).reshape(1, E * E), (P, E * E))
    half = HD // 2
    freq = (np.float32(1.0) / np.float32(10000.0) ** (np.arange(half, dtype=np.float32) / np.float32(half))).astype(np.float32)
    angle = (np.arange(T, dtype=np.float32)[:, None] * freq[None, :]).astype(np.float32)
    cos, sin = np.cos(angle).T, np.sin(angle).T
    cos_rows = np.tile(np.concatenate([cos, cos]), (NH, 1))
    sin_rows = np.tile(np.concatenate([-sin, sin]), (NH, 1))
    return np.ascontiguousarray(np.concatenate([ident, mask, mask.T, tri, cos_rows, sin_rows], axis=1), dtype=np.float32)


def build(nc, x_in, wide_in, lat_in, cols_in, rows_in, const_in, split_in, am_in, cons_in, b2_in, out):
    WIDE_AT, n_wide = places(WIDE)
    COLS_AT, n_cols = places(COLS)
    ROWS_AT, n_rows = places(ROWS)
    CONST_AT, n_const = places(CONST)
    SPLIT_AT, n_split = places(SPLIT)
    ctx = ExitStack()
    with ctx:
        def sb(name, shape, dt=F32):
            return ctx.enter_context(nc.sbuf_tensor(name, shape, dt))

        wide = sb("wide", [P, n_wide])
        latw = sb("latw", [LAT, 3 * 128])
        cols = sb("cols", [P, n_cols])
        rows = sb("rows", [P, n_rows])
        const = sb("const", [P, n_const])
        w_hi = sb("w_hi", [P, n_split], F16)
        w_lo = sb("w_lo", [P, n_split], F16)
        b2 = sb("b2", [E, 128])
        am = sb("am", [16, 128])
        cons = sb("cons", [16, 1])
        ident16 = sb("ident16", [P, P], F16)
        identb = sb("identb", [P, P], BF16)
        maskb = sb("maskb", [P, P], BF16)
        maskTb = sb("maskTb", [P, P], BF16)
        ones = sb("ones", [P, 32])
        neghalf = sb("neghalf", [P, NC])
        mod_bias = sb("mod_bias", [P, 1])
        half_s1 = sb("half_s1", [P, HC])
        s12 = sb("s12", [P, HC])
        ca_bo7 = sb("ca_bo7", [P, 1])
        mc_bo15 = sb("mc_bo15", [P, 1])

        def W(name):
            a, b = WIDE_AT[name]
            return wide[:, a:b]

        def V(name, i=0, n=P):
            a, _ = COLS_AT[name]
            return cols[0:n, a + i:a + i + 1]

        def R(name):
            a, b = ROWS_AT[name]
            return rows[:, a:b]

        def C(name):
            a, b = CONST_AT[name]
            return const[:, a:b]

        def part(w, name, i, n):
            a, _ = SPLIT_AT[name]
            return w[:, a + i * n:a + (i + 1) * n]

        x = sb("x", [P, NC, D])
        x_next = sb("x_next", [P, NC, D])
        xn = sb("xn", [P, NC, D])
        xT = sb("xT", [P, T])
        xh = sb("xh", [P, T], F16)
        xl = sb("xl", [P, T], F16)
        stats = sb("stats", [P, NC, 6])
        mv = sb("mv", [P, NC, 2])
        ve = sb("ve", [P, NC])
        rstd = sb("rstd", [P, NC])
        latn = sb("latn", [P, NC, LAT])
        latT = sb("latT", [LAT, T])
        t_a = sb("t_a", [P, T])
        t_b = sb("t_b", [P, T])
        q32 = sb("q32", [P, T])
        k32 = sb("k32", [P, T])
        parts = sb("parts", [P, 2, 4, T], F16)
        qsm = sb("qsm", [P, 2, NG, T], F16)
        qs, qm = qsm[:, 0, :, :], qsm[:, 1, :, :]
        kp = sb("kp", [P, NH, T], F16)
        vp = sb("vp", [P, NC, NH, 32])
        qkc = sb("qkc", [P, 2, MH, T], F16)
        qc, kc = qkc[:, 0, :, :], qkc[:, 1, :, :]
        vc = sb("vc", [P, NC, D])
        negmax = sb("negmax", [P, NG + 2, NC, GH], F16)
        mrow = sb("mrow", [GH, 2, T], F16)
        probs = sb("probs", [P, 2, GH, T])
        osb = sb("osb", [P, NG, T])
        rden = sb("rden", [P, NC, NH])
        onorm = sb("onorm", [P, NC, NH, HD])
        oT = sb("oT", [P, T])
        oc = sb("oc", [P, T])
        ctxT = sb("ctxT", [P, T])
        h_hi = sb("h_hi", [P, 2, HC, T], F16)
        h_lo = sb("h_lo", [P, 2, HC, T], F16)
        h32 = sb("h32", [P, HC, T])
        lg = sb("lg", [P, NC, E])
        gex = sb("gex", [P, NC, E])
        gmax = sb("gmax", [P, NC])
        gsum = sb("gsum", [P, NC])
        gates = sb("gates", [P, NC, E])
        cmp1 = sb("cmp1", [P, NC, E, E])
        cmp2 = sb("cmp2", [P, NC, E, E])
        gT = oc[0:E, :]

        relay = nc.dram_tensor("relay", (2, 4, P, T), F16, kind="Internal").ap()

        psum = ctx.enter_context(nc.psum_tensor("banks", [P, 8, 512], F32))
        SCO, TRA, OUT, MIS, UP, DN = 0, 2, 4, 5, 6, 7

        TAIL = {48: [(1, 0)], 49: [(1, 1)], 50: [(1, 2), (0, 0)], 51: [(1, 3), (0, 1)], 52: [(0, 2)], 53: [(0, 3)]}
        PRO, POST = 0, 4
        NSPREAD, NMIX = 12 + 6, 6
        PRO1, SPAN = 4, {1: 10}
        LAG = 12
        NS = {0: 32, 1: 40, 2: 8}
        SCALE = {True: float(HD) ** -0.5, False: float(MD) ** -0.5}
        U = 8

        sems = {}

        def sem(name):
            if name not in sems:
                sems[name] = ctx.enter_context(nc.semaphore(name))
            return sems[name]

        stage = probs[:, :, :, :].rearrange("p a g t -> p a (g t)")
        s_stage = [ctx.enter_context(nc.semaphore(f"s_stage{n}")) for n in range(2)]
        s_in, s_split, s_free, s_set, s_am, s_one, s_zero, s_rows, s_half = (
            ctx.enter_context(nc.semaphore(n)) for n in ("s_in", "s_split", "s_free", "s_set", "s_am", "s_one", "s_zero", "s_rows", "s_half"))

        LOADS = [(at, min(GH * T, n_split - at)) for at in range(0, n_split, GH * T)]

        FIRST = 2 * HC
        REST = E * HC - FIRST

        def mm(bank, cols_, lhsT, rhs, start, stop, rows_=slice(0, P)):
            return nc.tensor.matmul(psum[rows_, bank, cols_], lhsT, rhs, start=start, stop=stop)

        def three(bank, cols_, parts):
            n = 3 * len(parts)
            j = 0
            for (a_hi, a_lo, b_hi, b_lo) in parts:
                for a, b in ((a_hi, b_hi), (a_hi, b_lo), (a_lo, b_hi)):
                    last = mm(bank, cols_, a, b, j == 0, j == n - 1)
                    j += 1
            return last

        def transpose_x(pe, L):
            pe.wait_ge(sem(f"xn{L}"), 1)
            for c in range(NC):
                last = nc.tensor.transpose(psum[:, MIS, c * P:(c + 1) * P], xn[:, c, :], C("ident"))
            last.then_inc(sem(f"xT_ps{L}"), 1)
            pe.wait_ge(sem(f"xT{L}"), 1)

        def project(bank, w, rhs, name):
            mm(bank, slice(0, T), w, rhs, True, True).then_inc(sem(name), 1)

        def values(bank, lhs, w, name, k=P):
            for c in range(NC):
                last = mm(bank, slice(c * P, (c + 1) * P), lhs[0:k, c * P:(c + 1) * P], w, True, True)
            last.then_inc(sem(name), 1)

        def chain_of(dve):
            count = [0]

            def link(ins):
                count[0] += 1
                ins.then_inc(sem("dve_chain"), 1)
                dve.wait_ge(sem("dve_chain"), count[0])
            return link

        def norm_stats(dve, link, src, n, tag):
            v = nc.vector
            for c in range(NC):
                ins = v.bn_stats(stats[:, c, :], src(c))
            link(ins)
            for c in range(NC):
                ins = v.bn_aggr(mv[:, c, :], stats[:, c, :])
            link(ins)
            v.tensor_scalar(ve[:, :], mv[:, :, 1], EPS, None, ALU.add).then_inc(sem(f"ve{tag}"), 1)
            dve.wait_ge(sem(f"rstd{tag}"), 1)

        def normalise(dve, link, src, L):
            norm_stats(dve, link, lambda c: src[:, c, :], D, f"x{L}")
            for c in range(NC):
                ins = nc.vector.tensor_scalar(xn[:, c, :], src[:, c, :], mv[:, c, 0:1], rstd[:, c:c + 1],
                                              ALU.subtract, ALU.mult)
            ins.then_inc(sem(f"xn{L}"), 1)

        def split_x(dve, L):
            dve.wait_ge(sem(f"xh{L}"), 1)
            nc.vector.tensor_tensor(out=xl[:, :], in0=xT[:, :], in1=xh[:, :], op=ALU.subtract) \
                .then_inc(sem(f"xsplit{L}"), 1)

        def halves(link, src, w, at, name):
            link(nc.vector.tensor_copy(parts[:, w, at, :], src[:, :]))
            nc.vector.tensor_tensor(out=parts[:, w, at + 1, :], in0=src[:, :], in1=parts[:, w, at, :], op=ALU.subtract) \
                .then_inc(sem(name), 1)

        def open_pe_x(pe):
            transpose_x(pe, 0)
            for c in range(NC):
                mm(DN, slice(LAT * c, LAT * c + LAT), xT[:, c * P:(c + 1) * P], W("dkv"), True, True)
            for c in range(NC):
                last = mm(DN, slice(P + E * c, P + E * c + E), xT[:, c * P:(c + 1) * P], W("gate"), True, True)
            last.then_inc(sem("lat_ps"), 1)
            project(3, W("l0_q"), xT[:, :], "q_ps0")
            project(4, W("l0_qr"), xT[:, :], "q_ps0")

        def open_pe_lat(pe):
            pe.wait_ge(sem("latn"), 1)
            for c in range(NC):
                last = nc.tensor.transpose(psum[0:LAT, MIS, c * P:(c + 1) * P], latn[:, c, :], C("ident"))
            last.then_inc(sem("latT_ps"), 1)

        def open_pe_kv(pe):
            pe.wait_ge(sem("latT"), 1)
            pe.wait_ge(sem("rope_q"), 1)
            project(3, latw[:, 0:128], latT[:, :], "k_ps0")
            project(4, latw[:, 128:256], latT[:, :], "k_ps0")
            values(MIS, latT, latw[:, 256:384], "v_ps0", k=LAT)

        def open_dve_x(dve, link):
            dve.wait_ge(sem("x_in"), 16)
            normalise(dve, link, x_next, 0)

        def rope(dve, link, dst, ps, name):
            v = nc.vector
            dve.wait_ge(sem(ps), 2)
            v.tensor_tensor(out=t_a[:, :], in0=psum[:, 3, :], in1=C("cos"), op=ALU.mult)
            link(v.tensor_tensor(out=t_b[:, :], in0=psum[:, 4, :], in1=C("sin"), op=ALU.mult))
            v.tensor_tensor(out=dst[:, :], in0=t_a[:, :], in1=t_b[:, :], op=ALU.add).then_inc(sem(name), 1)
            dve.wait_ge(sem(name), 1)

        def open_dve_lat(dve, link):
            v = nc.vector
            split_x(dve, 0)
            dve.wait_ge(sem("lat_ps"), 1)
            v.tensor_tensor(out=lg[:, :, :], in0=psum[:, DN, P:P + NC * E].rearrange("p (c e) -> p c e", e=E),
                            in1=R("bg").unsqueeze(1).broadcast_to([P, NC, E]), op=ALU.add)
            norm_stats(dve, link, lambda c: psum[:, DN, LAT * c:LAT * c + LAT], LAT, "lat")
            for c in range(NC):
                ins = v.tensor_scalar(latn[:, c, :], psum[:, DN, LAT * c:LAT * c + LAT], mv[:, c, 0:1],
                                      rstd[:, c:c + 1], ALU.subtract, ALU.mult)
            ins.then_inc(sem("latn"), 1)
            rope(dve, link, q32, "q_ps0", "rope_q")
            halves(link, q32, 0, 0, "qsplit0")

        def open_dve_k(dve, link):
            rope(dve, link, k32, "k_ps0", "rope_k")
            halves(link, k32, 0, 2, "ksplit0")

        def open_dve_rank(dve, link):
            v = nc.vector
            mine = lg[:, :, :].unsqueeze(3).broadcast_to([P, NC, E, E])
            other = lg[:, :, :].unsqueeze(2).broadcast_to([P, NC, E, E])
            tri = C("tri").rearrange("p (e f) -> p e f", f=E)
            v.tensor_tensor(out=cmp1[:, :, :, :], in0=other, in1=mine, op=ALU.is_gt)
            link(v.tensor_tensor(out=cmp2[:, :, :, :], in0=other, in1=mine, op=ALU.is_equal))
            for c in range(NC):
                ins = v.tensor_tensor(out=cmp2[:, c, :, :], in0=cmp2[:, c, :, :], in1=tri, op=ALU.mult)
            link(ins)
            link(v.tensor_tensor(out=cmp1[:, :, :, :], in0=cmp1[:, :, :, :], in1=cmp2[:, :, :, :], op=ALU.add))
            link(v.tensor_reduce(gates[:, :, :], cmp1[:, :, :, :], AX.X, ALU.add))
            v.tensor_scalar(gates[:, :, :], gates[:, :, :], 1.5, None, ALU.is_lt)
            link(v.tensor_reduce(gmax[:, :], lg[:, :, :], AX.X, ALU.max))
            v.tensor_tensor(out=lg[:, :, :], in0=lg[:, :, :], in1=gmax[:, :].unsqueeze(2).broadcast_to([P, NC, E]),
                            op=ALU.subtract).then_inc(sem("lg"), 1)

        def open_dve_gates(dve, link):
            v = nc.vector
            dve.wait_ge(sem("gex"), 1)
            link(v.tensor_tensor(out=gates[:, :, :], in0=gates[:, :, :], in1=gex[:, :, :], op=ALU.mult))
            link(v.tensor_reduce(gsum[:, :], gates[:, :, :], AX.X, ALU.add))
            link(v.reciprocal(gsum[:, :], gsum[:, :]))
            link(v.tensor_tensor(out=gates[:, :, :], in0=gates[:, :, :],
                                 in1=gsum[:, :].unsqueeze(2).broadcast_to([P, NC, E]), op=ALU.mult))

        def move(act, dst, bank, name, rows_=P, wait=None):
            act.wait_ge(sem(wait), 1)
            nc.scalar.activation(dst, psum[0:rows_, bank, :], ACT.Copy).then_inc(sem(name), 1)

        def take_x(act, L):
            move(act, xT[:, :], MIS, f"xT{L}", wait=f"xT_ps{L}")
            nc.scalar.activation(xh[:, :], psum[:, MIS, :], ACT.Copy).then_inc(sem(f"xh{L}"), 1)

        def open_act_lat(act):
            act.wait_ge(sem("latT_ps"), 1)
            nc.scalar.activation(latT[:, :], psum[0:LAT, MIS, :], ACT.Identity, scale=V("gamma", n=LAT),
                                 bias=V("beta", n=LAT)).then_inc(sem("latT"), 1)

        def open_act_v(act):
            act.wait_ge(sem("v_ps0"), 1)
            for c in range(NC):
                ins = nc.scalar.activation(vp[:, c, :, 0:HD], psum[:, MIS, c * P:(c + 1) * P]
                                           .rearrange("p (h d) -> p h d", d=HD), ACT.Copy)
            ins.then_inc(sem("vp0"), 1)

        def open_act_gates(act):
            act.wait_ge(sem("lg"), 1)
            nc.scalar.activation(gex[:, :, :], lg[:, :, :], ACT.Exp).then_inc(sem("gex"), 1)

        def first_up(pe, n, done):
            if n:
                pe.wait_ge(sem("relu"), done + n)
            three(UP, slice(0, T), [(part(w_hi, "W1", n, P), part(w_lo, "W1", n, P), xh[:, :], xl[:, :])]) \
                .then_inc(sem("up0"), 1)

        def first_relu(act, n, done):
            act.wait_ge(sem("up0"), done + n + 1)
            if n >= HC:
                act.wait_ge(sem("h_lo0"), done + n - HC + 1)
            nc.scalar.activation(h32[:, n % HC, :], psum[:, UP, :], ACT.Relu, bias=V("b1", n)).then_inc(sem("relu"), 1)

        def first_hi(dve, n, done):
            dve.wait_ge(sem("relu"), done + n + 1)
            nc.vector.tensor_copy(h_hi[:, n // HC, n % HC, :], h32[:, n % HC, :]).then_inc(sem("h_hi0"), 1)

        def first_lo(pool, n, done):
            pool.wait_ge(sem("h_hi0"), done + n + 1)
            nc.gpsimd.tensor_tensor(out=h_lo[:, n // HC, n % HC, :], in0=h32[:, n % HC, :], in1=h_hi[:, n // HC, n % HC, :],
                                    op=ALU.subtract).then_inc(sem("h_lo0"), 1)

        def inverse_root(pool, tag):
            pool.wait_ge(sem(f"ve{tag}"), 1)
            nc.gpsimd.tensor_tensor(out=rstd[:, :], in0=ve[:, :], in1=neghalf[:, :], op=ALU.pow) \
                .then_inc(sem(f"rstd{tag}"), 1)

        def load_x(sp, at):
            sp.dma_start(x_next[:, :, :], x_in[at].rearrange("b (c p) d -> p (b c) d", p=P)).then_inc(sem("x_in"), 16)

        def relayed(sp, w, first):
            sp.dma_start(relay[w, first:first + 2].rearrange("a p t -> p a t"), parts[:, w, first:first + 2, :]) \
                .then_inc(sem("relay1" if w else f"relay0_{first}"), 16)

        def spread_main(sp, L, n):
            sp.wait_ge(sem(f"qsplit{L}"), 1)
            relayed(sp, 0, 0)
            sp.wait_ge(sem(f"ksplit{L}"), 1)
            relayed(sp, 0, 2)
            sp.wait_ge(sem("relay0_0"), 16 * (n + 1))
            for j, a in enumerate((0, 0, 1)):
                src = relay[0, a].rearrange("(m r) t -> r m t", r=32)
                for w in range(2):
                    sp.dma_start(qsm[j:P:4, w, :, :], src).then_inc(sem(f"spread{L}"), 16)
            sp.wait_ge(sem("relay0_2"), 16 * (n + 1))
            for g in range(GH):
                for j, a in enumerate((2, 3, 2)):
                    src = relay[0, a].rearrange("(m g d) t -> g d m t", g=GH, d=HD)[g]
                    sp.dma_start(kp[32 * g + j:32 * g + 32:4, g:NH:GH, :], src).then_inc(sem(f"spread{L}"), 16)

        def restart():
            numbers = sorted(s.num for s in sems.values())
            assert numbers == list(range(numbers[0], numbers[0] + len(numbers)))
            nc.sync.sem_clear(range(numbers[0], numbers[-1] + 1))
            nc.all_engine_barrier()

        with nc.Block() as block:
            @block.sync
            def _(sp):
                load_x(sp, slice(0, 1))
                for dst, src in ((const, const_in), (wide, wide_in), (cols, cols_in), (latw, lat_in),
                                 (b2, b2_in), (am, am_in), (cons, cons_in)):
                    sp.dma_start(dst[:, :], src).then_inc(s_in, 16)
                sp.dma_start(rows[:, :], rows_in.broadcast_to([P, n_rows])).then_inc(s_in, 16)
                for n, (a, w) in enumerate(LOADS):
                    if n >= 2:
                        sp.wait_ge(s_free, n - 1)
                    sp.dma_start(stage[:, n % 2, 0:w], split_in[:, a:a + w]).then_inc(s_stage[n % 2], 16)
                    if n == 0:
                        sp.wait_ge(s_one, 1)
                        sp.wait_ge(s_zero, 3)
                        for g in range(GH):
                            r = 32 * g + 3
                            sp.dma_start(kp[r:r + 1, g:NH:GH, :], kc[0:1, :, :]).then_inc(s_rows, 16)
                sp.wait_ge(s_rows, 16 * GH)
                sp.wait_ge(sem("spread0"), 16 * NSPREAD)

            @block.scalar
            def _(act):
                take_x(act, 0)
                act.wait_ge(s_in, 8 * 16)
                open_act_lat(act)
                act.wait_ge(s_zero, 4)
                open_act_v(act)
                for n, (a, w) in enumerate(LOADS):
                    if n == 2:
                        open_act_gates(act)
                    act.wait_ge(s_stage[n % 2], 16 * (n // 2 + 1))
                    nc.scalar.activation(w_hi[:, a:a + w], stage[:, n % 2, 0:w], ACT.Copy).then_inc(s_split, 1)
                    if n == 3:
                        spread_main(act, 0, 0)
                    if n:
                        first_relu(act, n - 1, 0)
                for n in range(len(LOADS) - 1, FIRST):
                    first_relu(act, n, 0)

            @block.vector
            def _(dve):
                nc.vector.memset(ones[:, :], 1.0)
                nc.vector.memset(neghalf[:, :], -0.5).then_inc(s_half, 1)
                nc.vector.memset(qs, 0.0)
                nc.vector.memset(kc, 1.0).then_inc(s_one, 1)
                dve.wait_ge(s_in, 8 * 16)
                nc.vector.tensor_copy(ident16[:, :], C("ident"))
                nc.vector.tensor_copy(identb[:, :], C("ident"))
                nc.vector.tensor_copy(maskb[:, :], C("mask"))
                nc.vector.tensor_copy(maskTb[:, :], C("maskT"))
                nc.vector.tensor_scalar(ca_bo7[:, :], V("ca_bo"), CAUSAL_W, None, ALU.mult)
                nc.vector.tensor_scalar(half_s1[:, :], cols[:, COLS_AT["s1"][0]:COLS_AT["s1"][1]], 0.5, None, ALU.mult)
                nc.vector.scalar_tensor_tensor(out=s12[:, :], in0=cols[:, COLS_AT["s1"][0]:COLS_AT["s1"][1]], scalar=0.5,
                                               in1=cols[:, COLS_AT["s2"][0]:COLS_AT["s2"][1]], op0=ALU.mult, op1=ALU.mult)
                nc.vector.tensor_scalar(mc_bo15[:, :], V("mc_bo"), META_W, None, ALU.mult)
                nc.vector.tensor_tensor(out=t_a[:, 0:1], in0=V("cg_b"), in1=V("am_b"), op=ALU.add).then_inc(s_set, 1)
                dve.wait_ge(s_set, 1)
                dve.wait_ge(s_am, 1)
                nc.vector.tensor_tensor(out=t_b[:, 0:1], in0=psum[:, 0, 0:1], in1=t_a[:, 0:1], op=ALU.add).then_inc(s_set, 1)
                dve.wait_ge(s_set, 2)
                nc.vector.tensor_scalar(mod_bias[:, :], t_b[:, 0:1], 0.5, None, ALU.mult).then_inc(s_set, 1)
                dve.wait_ge(s_set, 3)
                link = chain_of(dve)
                open_dve_x(dve, link)
                open_dve_lat(dve, link)
                open_dve_k(dve, link)
                for n, (a, w) in enumerate(LOADS):
                    if n == 2:
                        open_dve_rank(dve, link)
                        open_dve_gates(dve, link)
                    dve.wait_ge(s_split, n + 1)
                    nc.vector.tensor_tensor(out=w_lo[:, a:a + w], in0=stage[:, n % 2, 0:w], in1=w_hi[:, a:a + w],
                                            op=ALU.subtract).then_inc(s_free, 1)
                    if n:
                        first_hi(dve, n - 1, 0)
                for n in range(len(LOADS) - 1, FIRST):
                    first_hi(dve, n, 0)

            @block.tensor
            def _(pe):
                pe.wait_ge(s_in, 8 * 16)
                nc.tensor.matmul(psum[:, 0, 0:1], am[:, :], cons[:, :], start=True, stop=True).then_inc(s_am, 1)
                open_pe_x(pe)
                open_pe_lat(pe)
                open_pe_kv(pe)
                pe.wait_ge(s_free, 1)
                pe.wait_ge(sem("xsplit0"), 1)
                for n in range(FIRST):
                    first_up(pe, n, 0)

            @block.gpsimd
            def _(pool):
                nc.gpsimd.memset(vp[:, :, :, :], 0.0).then_inc(s_zero, 1)
                nc.gpsimd.memset(qm, 0.0).then_inc(s_zero, 1)
                nc.gpsimd.memset(kp[:, :, :], 0.0).then_inc(s_zero, 1)
                pool.wait_ge(s_zero, 3)
                nc.gpsimd.memset(vp[:, :, :, HD:HD + 1], 1.0).then_inc(s_zero, 1)
                pool.wait_ge(s_half, 1)
                inverse_root(pool, "x0")
                inverse_root(pool, "lat")
                for n in range(FIRST):
                    first_lo(pool, n, 0)

        restart()

        def main(st, gr):
            return st < 2 and gr < NG

        def width(st, c):
            return (P * (c + 1), P * c) if st == 0 else (T, 0)

        with nc.Fori(0, B) as i:
            with nc.Block() as block:
                @block.tensor
                def _(pe):
                    def score_unit(st, u):
                        gr, c, pair = u // U, (u % U) // 2, u % 2
                        if st == 1 and u == U * NG:
                            pe.wait_ge(sem("spread3"), 16 * NMIX)
                        kw, _ = width(st, c)
                        for s in range(2):
                            g = 2 * pair + s
                            if u:
                                pe.wait_ge(sem(f"max{st}"), 2 * u + s - 1)
                            if main(st, gr):
                                lhsT, rhs = qs[:, gr, c * P:(c + 1) * P], kp[:, GH * gr + g, 0:kw]
                            else:
                                lhsT, rhs = qc[0:96, g, c * P:(c + 1) * P], kc[0:96, g, 0:kw]
                            last = mm(SCO + s, slice(0, kw), lhsT, rhs, True, st != 0)
                            if st == 0:
                                last = mm(SCO + s, slice(kw - P, kw), identb[:, :], maskb[:, :], False, True)
                            last.then_inc(sem(f"score{st}"), 1)

                    def max_rows(st, gr):
                        pe.wait_ge(sem(f"max{st}"), 2 * U * (gr + 1))
                        if gr:
                            pe.wait_ge(sem(f"mrow{st}"), gr)
                        elif st == 2:
                            pe.wait_ge(sem("vp0"), 1)
                        for c in range(NC):
                            last = mm(MIS, slice(c * P, (c + 1) * P), negmax[:, gr, c, :], ident16[:, :], True, True,
                                      rows_=slice(0, GH))
                        last.then_inc(sem(f"mrow_ps{st}"), 1)

                    def trans_unit(st, u):
                        gr, c, pair = u // U, (u % U) // 2, u % 2
                        if st == 2 and u == 0:
                            for name in ("vc2", "rope_k"):
                                pe.wait_ge(sem(name), 1)
                        if u % U == 0:
                            pe.wait_ge(sem(f"qm{st}_{gr}"), 16 * (1 if main(st, gr) else MH))
                        _, q0 = width(st, c)
                        for s in range(2):
                            g = 2 * pair + s
                            if u:
                                pe.wait_ge(sem(f"exp{st}"), 2 * u + s - 1)
                            if main(st, gr):
                                lhsT, rhs = kp[:, GH * gr + g, c * P:(c + 1) * P], qm[:, gr, q0:T]
                            else:
                                lhsT, rhs = kc[0:97, g, c * P:(c + 1) * P], qc[0:97, g, q0:T]
                            last = mm(TRA + s, slice(q0, T), lhsT, rhs, True, st != 0)
                            if st == 0:
                                last = mm(TRA + s, slice(q0, q0 + P), identb[:, :], maskTb[:, :], False, True)
                            last.then_inc(sem(f"trans{st}"), 1)

                    def value_step(st, kk):
                        gr, c = kk // NC, kk % NC
                        pe.wait_ge(sem(f"exp{st}"), GH * (kk + 1))
                        if c == 0:
                            if gr:
                                pe.wait_ge(sem(f"osb{st}"), gr)
                            if st == 1 and gr == NG:
                                pe.wait_ge(sem("h32_1"), HC)
                        _, q0 = width(st, c)
                        for g in range(GH):
                            r = slice(32 * g, 32 * g + 32)
                            if main(st, gr):
                                lhsT = vp[:, c, GH * gr + g, :]
                            else:
                                lhsT = vc[:, c, MD * g:MD * (g + 1)]
                            last = mm(OUT, slice(q0, T), lhsT, probs[:, kk % 2, g, q0:T], c == 0, c == NC - 1, rows_=r)
                        if not main(st, gr):
                            for g in range(GH):
                                r = slice(32 * g, 32 * g + 32)
                                last = mm(DN, slice(q0, T), ones[:, :], probs[:, kk % 2, g, q0:T], c == 0, c == NC - 1, rows_=r)
                        last.then_inc(sem(f"pv{st}"), 1)

                    def attention(st, pieces, at={}):
                        n = NS[st]
                        slots = n + LAG + 3
                        done = 0
                        span = SPAN.get(st, slots)
                        for s in range(slots):
                            if st == 1 and s in TAIL:
                                for what, c in TAIL[s]:
                                    (heads_out if what else heads_back)(1, c)
                            if s < n:
                                score_unit(st, s)
                            want = -(-len(pieces) * min(s + 1, span) // span)
                            while done < (done + want + 1) // 2:
                                pieces[done][0](*pieces[done][1])
                                done += 1
                            if s % U == 1 and U < s <= n + 1:
                                max_rows(st, s // U - 1)
                            if s in at:
                                at[s]()
                            if LAG <= s < n + LAG:
                                trans_unit(st, s - LAG)
                            while done < want:
                                pieces[done][0](*pieces[done][1])
                                done += 1
                            k = s - LAG - 2
                            if k > 0 and k % 2 == 1 and k // 2 < n // 2:
                                value_step(st, k // 2)

                    def up0(e, hc):
                        n = e * HC + hc
                        if n > FIRST:
                            pe.wait_ge(sem("relu"), n - FIRST)
                        three(UP, slice(0, T), [(part(w_hi, "W1", n, P), part(w_lo, "W1", n, P), xh[:, :], xl[:, :])]) \
                            .then_inc(sem("up0"), 1)

                    def down0(e, c):
                        if c == 0:
                            if e >= 2:
                                pe.wait_ge(sem("h_lo0"), HC * (e - 1))
                            if e:
                                pe.wait_ge(sem("acc0"), e)
                        t = slice(c * P, (c + 1) * P)
                        last = three(DN, t, [(h_hi[:, e % 2, hc, t], h_lo[:, e % 2, hc, t],
                                              part(w_hi, "W2", e * HC + hc, P), part(w_lo, "W2", e * HC + hc, P))
                                             for hc in range(HC)])
                        if c == NC - 1:
                            last.then_inc(sem("down0"), 1)

                    pieces = []
                    for e in range(E + 1):
                        for hc in range(HC):
                            if 2 <= e < E:
                                pieces.append((up0, (e, hc)))
                            if e:
                                pieces.append((down0, (e - 1, hc)))
                    for f, a in pieces[:PRO]:
                        f(*a)
                    attention(0, pieces[PRO:-POST])

                    def heads_out(L, c):
                        pe.wait_ge(sem(f"osb{L}"), NG)
                        pe.wait_ge(sem(f"max{L}"), 2 * NS[L])
                        if c >= 2:
                            pe.wait_ge(sem(f"onorm{L}"), c - 1)
                        for gr in range(NG):
                            last = nc.tensor.transpose(psum[:, SCO + c % 2, gr * P:(gr + 1) * P],
                                                       osb[:, gr, c * P:(c + 1) * P], C("ident"))
                        last.then_inc(sem(f"oq_ps{L}"), 1)

                    def heads_back(L, c):
                        pe.wait_ge(sem(f"onorm{L}"), c + 1)
                        if c == 0:
                            pe.wait_ge(sem(f"mrow{L}"), NS[L] // U)
                        last = nc.tensor.transpose(psum[:, MIS, c * P:(c + 1) * P],
                                                   onorm[:, c, :, :].rearrange("p h d -> p (h d)"), C("ident"))
                        if c == NC - 1:
                            last.then_inc(sem(f"oT_ps{L}"), 1)

                    post = pieces[-POST:]
                    for c in range(NC):
                        heads_out(0, c)
                        if c:
                            post[c - 1][0](*post[c - 1][1])
                            heads_back(0, c - 1)
                    for f, a in post[3:5]:
                        f(*a)
                    heads_back(0, NC - 1)
                    for f, a in post[5:]:
                        f(*a)
                    pe.wait_ge(sem("oT0"), 1)
                    for c in range(NC):
                        last = nc.tensor.transpose(psum[0:E, UP, c * P:(c + 1) * P], gates[:, c, :], C("ident"))
                    last.then_inc(sem("gT_ps"), 1)
                    pe.wait_ge(sem("gT"), 1)
                    pe.wait_ge(sem("onorm0"), NC)
                    for c in range(NC):
                        t = slice(c * P, (c + 1) * P)
                        mm(0, t, oT[:, t], W("l0_o"), True, False)
                        last = mm(0, t, gT[:, t], b2[:, :], False, True)
                    last.then_inc(sem("attn0"), 1)

                    transpose_x(pe, 1)
                    pe.wait_ge(sem("xin1"), 1)
                    project(0, W("l1_q"), xT[:, :], "q_ps1")
                    project(1, W("cg"), xT[:, :], "mod_ps")
                    project(2, W("l1_k"), xT[:, :], "k_ps1")
                    project(3, W("ca_q"), xT[:, :], "caq_ps")
                    project(4, W("ca_k"), xT[:, :], "cak_ps")
                    pe.wait_ge(sem("xh1"), 1)
                    values(5, xT, W("l1_v"), "v_ps1")
                    values(7, xT, W("ca_v"), "cav_ps")

                    def gate1(o):
                        if o == 0:
                            pe.wait_ge(sem("xsplit1"), 1)
                            pe.wait_ge(sem("vc1"), 1)
                        else:
                            pe.wait_ge(sem("h32_1"), o)
                        three(UP, slice(0, T), [(part(w_hi, "F1", o, P), part(w_lo, "F1", o, P), xh[:, :], xl[:, :])]) \
                            .then_inc(sem("g1a"), 1)
                        three(DN, slice(0, T), [(part(w_hi, "F2", o, P), part(w_lo, "F2", o, P), xh[:, :], xl[:, :])]) \
                            .then_inc(sem("g1b"), 1)

                    def hidden(n, o, ic, name, src):
                        if ic == 0:
                            if o == 0:
                                pe.wait_ge(sem(f"hsplit{n}"), 1)
                            if n == 1 and o == 0:
                                pe.wait_ge(sem("h32_1"), HC)
                            else:
                                pe.wait_ge(sem("up_free"), HC * (n - 1) + o)
                        for j, (a, b) in enumerate(((w_hi, h_hi), (w_hi, h_lo), (w_lo, h_hi))):
                            wa, _ = SPLIT_AT[name]
                            last = mm(UP, slice(0, T), a[:, wa + ic * 512 + o * P:wa + ic * 512 + (o + 1) * P],
                                      b[:, src, ic, :], ic == 0 and j == 0, ic == HC - 1 and j == 2)
                        if ic == HC - 1:
                            last.then_inc(sem(f"hid{n}"), 1)

                    for o in range(HC):
                        gate1(o)
                    pieces = [(o, ic) for o in range(HC) for ic in range(HC)]
                    for o, ic in pieces[:PRO1]:
                        hidden(1, o, ic, "G1", 0)
                    pe.wait_ge(sem("spread1"), 16 * NSPREAD)
                    for name in ("q_out1", "mod_e", "k32_1", "caq32", "cak32", "vp1"):
                        pe.wait_ge(sem(name), 1)
                    attention(1, [(hidden, (1, o, ic, "G1", 0)) for o, ic in pieces[PRO1:]])

                    def hidden2(o):
                        for ic in range(HC):
                            hidden(2, o, ic, "G2", 1)

                    hidden2(0)
                    pe.wait_ge(sem("oc1"), 1)
                    project(OUT, W("ca_o"), oc[:, :], "mix_ps1")
                    hidden2(1)
                    pe.wait_ge(sem("ctx"), 1)
                    pe.wait_ge(sem("onorm1"), NC)
                    project(0, W("mc_q"), ctxT[:, :], "mcq_ps")
                    project(1, W("mc_k"), ctxT[:, :], "mck_ps")
                    values(2, ctxT, W("mc_v"), "mcv_ps")
                    open_pe_x(pe)
                    hidden2(2)
                    open_pe_lat(pe)
                    open_pe_kv(pe)
                    hidden2(3)
                    pe.wait_ge(sem("spread2"), 16 * NMIX)
                    for name in ("mcq32", "mck32"):
                        pe.wait_ge(sem(name), 1)

                    def third():
                        pe.wait_ge(sem("hsplit3"), 1)
                        for c in range(NC):
                            t = slice(c * P, (c + 1) * P)
                            last = three(UP, t, [(h_hi[:, 0, hc, t], h_lo[:, 0, hc, t], part(w_hi, "F3", hc, P),
                                                  part(w_lo, "F3", hc, P)) for hc in range(HC)])
                        last.then_inc(sem("y3"), 1)

                    def first(n):
                        if n == 0:
                            pe.wait_ge(sem("y3_out"), 1)
                        first_up(pe, n, REST)

                    attention(2, [], at={U + 1: third, **{U + 5 + n: (lambda n=n: first(n)) for n in range(FIRST)}})
                    pe.wait_ge(sem("oc2"), 1)
                    project(0, W("mc_o"), oc[:, :], "mix_ps2")
                    pe.wait_ge(sem("ctx2"), 1)
                    for c in range(NC):
                        t = slice(c * P, (c + 1) * P)
                        last = mm(1, t, ctxT[:, t], W("l1_o"), True, True)
                    last.then_inc(sem("attn1"), 1)

                @block.vector
                def _(dve):
                    link = chain_of(dve)
                    v = nc.vector

                    def reduce_unit(st, u):
                        gr, c, pair = u // U, (u % U) // 2, u % 2
                        kw, _ = width(st, c)
                        for s in range(2):
                            dve.wait_ge(sem(f"score{st}"), 2 * u + s + 1)
                            g = 2 * pair + s
                            v.tensor_reduce(negmax[:, gr, c, g:g + 1], psum[:, SCO + s, 0:kw],
                                            AX.X, ALU.max, negate=True).then_inc(sem(f"max{st}"), 1)

                    def max_out(st, gr):
                        dve.wait_ge(sem(f"mrow_ps{st}"), gr + 1)
                        if gr >= 2:
                            dve.wait_ge(sem(f"qm{st}_{gr - 2}"), 16)
                        v.tensor_copy(mrow[:, gr % 2, :], psum[0:GH, MIS, :]).then_inc(sem(f"mrow{st}"), 1)

                    def mixing_out(st):
                        dve.wait_ge(sem(f"pv{st}"), NS[st] // 2)
                        link(v.reciprocal(t_b[:, :], psum[:, DN, :]))
                        v.tensor_tensor(out=oc[:, :], in0=psum[:, OUT, :], in1=t_b[:, :], op=ALU.mult) \
                            .then_inc(sem(f"oc{st}"), 1)

                    def heads_norm(L, c):
                        dve.wait_ge(sem(f"oq_ps{L}"), c + 1)
                        bank = psum[:, SCO + c % 2, :].rearrange("p (h r) -> p h r", r=32)
                        link(v.reciprocal(rden[:, c, :], bank[:, :, HD]))
                        v.tensor_tensor(out=onorm[:, c, :, :], in0=bank[:, :, 0:HD],
                                        in1=rden[:, c, :].unsqueeze(2).broadcast_to([P, NH, HD]),
                                        op=ALU.mult).then_inc(sem(f"onorm{L}"), 1)

                    v.tensor_copy(x[:, :, :], x_next[:, :, :]).then_inc(sem("x_taken"), 1)
                    dve.wait_ge(sem("x_taken"), 1)

                    def hidden_hi(e, hc):
                        dve.wait_ge(sem("relu"), (e - 2) * HC + hc + 1)
                        if hc == 0:
                            dve.wait_ge(sem("down0"), e - 1)
                        v.tensor_copy(h_hi[:, e % 2, hc, :], h32[:, hc, :]).then_inc(sem("h_hi0"), 1)

                    def add_expert(e):
                        dve.wait_ge(sem("down0"), e + 1)
                        for c in range(NC):
                            ins = v.scalar_tensor_tensor(out=x[:, c, :], in0=psum[:, DN, c * P:(c + 1) * P],
                                                         scalar=gates[:, c, e:e + 1], in1=x[:, c, :],
                                                         op0=ALU.mult, op1=ALU.add)
                        ins.then_inc(sem("acc0"), 1)
                        dve.wait_ge(sem("acc0"), e + 1)

                    pieces = []
                    for e in range(E + 1):
                        for hc in range(HC):
                            if 2 <= e < E:
                                pieces.append((hidden_hi, (e, hc)))
                            if e:
                                pieces.append((add_expert, (e - 1,)) if hc == HC - 1 else None)

                    def attention(st, pieces, at={}):
                        n = NS[st]
                        slots = n + LAG + 3
                        done = 0
                        span = SPAN.get(st, slots)
                        for s in range(slots):
                            if st == 1 and s in TAIL:
                                for what, c in TAIL[s]:
                                    if what:
                                        heads_norm(1, c)
                            if s < n:
                                reduce_unit(st, s)
                            if s in at:
                                at[s](dve, link)
                            if st == 2 and 0 <= s - U - 5 < FIRST:
                                first_hi(dve, s - U - 5, REST)
                            want = -(-len(pieces) * min(s + 1, span) // span)
                            if s % U == 1 and U <= s <= n + 1:
                                max_out(st, s // U - 1)
                            while done < want:
                                if pieces[done] is not None:
                                    pieces[done][0](*pieces[done][1])
                                done += 1

                    for piece in pieces[:PRO]:
                        if piece is not None:
                            piece[0](*piece[1])
                    attention(0, pieces[PRO:-POST])
                    post = pieces[-POST:]
                    for c in range(NC):
                        heads_norm(0, c)
                        if c and post[c - 1] is not None:
                            post[c - 1][0](*post[c - 1][1])
                    for piece in post[3:]:
                        if piece is not None:
                            piece[0](*piece[1])
                    dve.wait_ge(sem("attn0"), 1)
                    xf = x[:, :, :].rearrange("p c d -> p (c d)")
                    v.tensor_tensor(out=xf, in0=xf, in1=psum[:, 0, :], op=ALU.add).then_inc(sem("xin1"), 1)
                    dve.wait_ge(sem("xin1"), 1)

                    normalise(dve, link, x, 1)
                    split_x(dve, 1)
                    dve.wait_ge(sem("mod_e"), 1)
                    link(v.tensor_scalar(t_a[:, :], t_a[:, :], 0.5, 0.5, ALU.mult, ALU.add))
                    dve.wait_ge(sem("q_ps1"), 1)
                    v.scalar_tensor_tensor(out=q32[:, :], in0=psum[:, 0, :], scalar=V("bq"), in1=t_a[:, :],
                                           op0=ALU.add, op1=ALU.mult).then_inc(sem("q_out1"), 1)
                    dve.wait_ge(sem("q_out1"), 1)
                    halves(link, q32, 0, 0, "qsplit1")
                    dve.wait_ge(sem("v_ps1"), 1)
                    for c in range(NC):
                        ins = v.tensor_tensor(out=vp[:, c, :, 0:HD],
                                              in0=psum[:, 5, c * P:(c + 1) * P].rearrange("p (h d) -> p h d", d=HD),
                                              in1=R("bv").rearrange("p (h d) -> p h d", d=HD), op=ALU.add)
                    ins.then_inc(sem("vp1"), 1)
                    dve.wait_ge(sem("cav_ps"), 1)
                    v.tensor_tensor(out=vc[:, :, :], in0=psum[:, 7, :].rearrange("p (c d) -> p c d", d=D),
                                    in1=R("ca_bv").unsqueeze(1).broadcast_to([P, NC, D]), op=ALU.add) \
                        .then_inc(sem("vc1"), 1)

                    def gate_out(o):
                        dve.wait_ge(sem("silu_e"), o + 1)
                        link(v.scalar_tensor_tensor(out=t_b[:, :], in0=t_b[:, :], scalar=1.0, in1=psum[:, UP, :],
                                                    op0=ALU.add, op1=ALU.mult))
                        dve.wait_ge(sem("g1b"), o + 1)
                        v.scalar_tensor_tensor(out=h32[:, o, :], in0=psum[:, DN, :], scalar=s12[:, o:o + 1], in1=t_b[:, :],
                                               op0=ALU.mult, op1=ALU.mult).then_inc(sem("h32_1"), 1)

                    def hidden_out(n, o):
                        dve.wait_ge(sem(f"hid{n}"), o + 1)
                        if n == 1 and o == 0:
                            dve.wait_ge(sem("hsplit1"), 1)
                        if n == 2 and o == 0:
                            dve.wait_ge(sem("hsplit2"), 1)
                        v.tensor_scalar(h32[:, o, :], psum[:, UP, :], V(f"hs{n}", o), None, ALU.mult) \
                            .then_inc(sem("up_free"), 1)

                    for o in range(HC):
                        gate_out(o)
                    pieces = [((hidden_out, (1, o)) if ic == HC - 1 else None) for o in range(HC) for ic in range(HC)]
                    for piece in pieces[:PRO1]:
                        if piece is not None:
                            piece[0](*piece[1])
                    attention(1, pieces[PRO1:], at={43: open_dve_x})
                    mixing_out(1)
                    hidden_out(2, 0)
                    dve.wait_ge(sem("mix1"), 1)
                    dve.wait_ge(sem("oT1"), 1)
                    v.scalar_tensor_tensor(out=ctxT[:, :], in0=oT[:, :], scalar=1.0 - CAUSAL_W, in1=t_a[:, :],
                                           op0=ALU.mult, op1=ALU.add).then_inc(sem("ctx"), 1)
                    for name, tmp, at, split in (("mcq32", 0, 0, "qsplit2"), ("mck32", 1, 2, "ksplit2")):
                        dve.wait_ge(sem(name), 1)
                        v.tensor_tensor(out=parts[:, 1, at + 1, :], in0=osb[:, tmp, :], in1=parts[:, 1, at, :],
                                        op=ALU.subtract).then_inc(sem(split), 1)
                    dve.wait_ge(sem("mcv_ps"), 1)
                    v.tensor_tensor(out=vc[:, :, :], in0=psum[:, 2, :].rearrange("p (c d) -> p c d", d=D),
                                    in1=R("mc_bv").unsqueeze(1).broadcast_to([P, NC, D]), op=ALU.add) \
                        .then_inc(sem("vc2"), 1)
                    hidden_out(2, 1)
                    open_dve_lat(dve, link)
                    hidden_out(2, 2)
                    hidden_out(2, 3)

                    def third_out(dve, link):
                        dve.wait_ge(sem("y3"), 1)
                        t4 = t_b[:, :].rearrange("p (c d) -> p c d", d=D)
                        v.tensor_tensor(out=t4, in0=psum[:, UP, :].rearrange("p (c d) -> p c d", d=D),
                                        in1=R("s3").unsqueeze(1).broadcast_to([P, NC, D]), op=ALU.mult) \
                            .then_inc(sem("y3_out"), 1)
                        dve.wait_ge(sem("y3_out"), 1)
                        link(v.tensor_tensor(out=xf, in0=xf, in1=t_b[:, :], op=ALU.add))
                        link(v.tensor_tensor(out=x[:, :, :], in0=x[:, :, :],
                                             in1=R("bo").unsqueeze(1).broadcast_to([P, NC, D]), op=ALU.add))

                    attention(2, [], at={2: open_dve_k, U + 2: open_dve_rank, U + 3: open_dve_gates, U + 4: third_out})
                    mixing_out(2)
                    dve.wait_ge(sem("mix2"), 1)
                    v.scalar_tensor_tensor(out=ctxT[:, :], in0=ctxT[:, :], scalar=1.0 - META_W, in1=t_a[:, :],
                                           op0=ALU.mult, op1=ALU.add).then_inc(sem("ctx2"), 1)
                    dve.wait_ge(sem("attn1"), 1)
                    v.tensor_tensor(out=xf, in0=xf, in1=psum[:, 1, :], op=ALU.add).then_inc(sem("x_out"), 1)

                @block.scalar
                def _(act):
                    a = nc.scalar

                    def exp_unit(st, u):
                        gr, c, pair = u // U, (u % U) // 2, u % 2
                        _, q0 = width(st, c)
                        kk = u // 2
                        if kk >= 2 and pair == 0:
                            act.wait_ge(sem(f"pv{st}"), kk - 1)
                        for s in range(2):
                            act.wait_ge(sem(f"trans{st}"), 2 * u + s + 1)
                            a.activation(probs[:, kk % 2, 2 * pair + s, q0:T], psum[:, TRA + s, q0:T],
                                         ACT.Exp, scale=SCALE[main(st, gr)]).then_inc(sem(f"exp{st}"), 1)

                    def out_group(st, gr):
                        act.wait_ge(sem(f"pv{st}"), NC * (gr + 1))
                        a.activation(osb[:, gr, :], psum[:, OUT, :], ACT.Copy).then_inc(sem(f"osb{st}"), 1)

                    def relu(e, hc):
                        act.wait_ge(sem("up0"), (e - 2) * HC + hc + 1)
                        if e > 2:
                            act.wait_ge(sem("h_lo0"), HC * (e - 3) + hc + 1)
                        a.activation(h32[:, hc, :], psum[:, UP, :], ACT.Relu, bias=V("b1", e * HC + hc)) \
                            .then_inc(sem("relu"), 1)

                    def attention(st, pieces, at={}):
                        n = NS[st]
                        slots = n + LAG + 3
                        done = 0
                        for s in range(slots):
                            if s in at:
                                at[s]()
                            want = -(-len(pieces) * (s + 1) // slots)
                            while done < (done + want + 1) // 2:
                                if pieces[done] is not None:
                                    pieces[done][0](*pieces[done][1])
                                done += 1
                            if LAG <= s < n + LAG:
                                exp_unit(st, s - LAG)
                            while done < want:
                                if pieces[done] is not None:
                                    pieces[done][0](*pieces[done][1])
                                done += 1
                            k = s - LAG - 2
                            if k > 0 and k % U == 7 and main(st, k // U) and k // U < n // U:
                                out_group(st, k // U)

                    pieces = []
                    for e in range(E + 1):
                        for hc in range(HC):
                            if 2 <= e < E:
                                pieces.append((relu, (e, hc)))
                            if e:
                                pieces.append(None)
                    for piece in pieces[:PRO]:
                        if piece is not None:
                            piece[0](*piece[1])
                    attention(0, pieces[PRO:-POST])
                    for piece in pieces[-POST:]:
                        if piece is not None:
                            piece[0](*piece[1])
                    move(act, oT[:, :], MIS, "oT0", wait="oT_ps0")
                    move(act, gT, UP, "gT", rows_=E, wait="gT_ps")

                    def take_projection(ps, bank, bias, tmp, w, at, name):
                        act.wait_ge(sem(ps), 1)
                        a.activation(osb[:, tmp, :], psum[:, bank, :], ACT.Identity, bias=V(bias))
                        a.activation(parts[:, w, at, :], psum[:, bank, :], ACT.Identity, bias=V(bias)).then_inc(sem(name), 1)

                    take_x(act, 1)
                    act.wait_ge(sem("mod_ps"), 1)
                    a.activation(t_a[:, :], psum[:, 1, :], ACT.Tanh, scale=0.5, bias=mod_bias[:, :]).then_inc(sem("mod_e"), 1)
                    act.wait_ge(sem("mod_e"), 1)
                    take_projection("k_ps1", 2, "bk", 2, 0, 2, "k32_1")
                    take_projection("caq_ps", 3, "ca_bq", 0, 1, 0, "caq32")
                    take_projection("cak_ps", 4, "ca_bk", 1, 1, 2, "cak32")

                    def silu_e(o):
                        act.wait_ge(sem("g1a"), o + 1)
                        if o:
                            act.wait_ge(sem("h32_1"), o)
                        a.activation(t_b[:, :], psum[:, UP, :], ACT.Tanh, scale=half_s1[:, o:o + 1]).then_inc(sem("silu_e"), 1)

                    for o in range(HC):
                        silu_e(o)
                        act.wait_ge(sem("h32_1"), o + 1)
                        a.activation(h_hi[:, 0, o, :], h32[:, o, :], ACT.Copy).then_inc(sem("g_hi"), 1)

                    def gelu(n):
                        act.wait_ge(sem("up_free"), HC * n)
                        a.activation(h32[:, :, :], h32[:, :, :], ACT.Gelu).then_inc(sem("gelu"), 1)

                    def gelu_hi(n, o, dst):
                        act.wait_ge(sem("gelu"), n)
                        a.activation(h_hi[:, dst, o, :], h32[:, o, :], ACT.Copy).then_inc(sem("gelu_hi"), 1)

                    gelu(1)
                    attention(1, [], at={LAG + 2 * o + 1: (lambda o=o: gelu_hi(1, o, 1)) for o in range(HC)})
                    move(act, oT[:, :], MIS, "oT1", wait="oT_ps1")
                    act.wait_ge(sem("mix_ps1"), 1)
                    a.activation(t_a[:, :], psum[:, OUT, :], ACT.Identity, scale=CAUSAL_W, bias=ca_bo7[:, :]).then_inc(sem("mix1"), 1)
                    take_projection("mcq_ps", 0, "mc_bq", 0, 1, 0, "mcq32")
                    take_projection("mck_ps", 1, "mc_bk", 1, 1, 2, "mck32")
                    take_x(act, 0)
                    open_act_lat(act)
                    open_act_v(act)
                    gelu(2)
                    for o in range(HC):
                        gelu_hi(2, o, 0)
                    open_act_gates(act)
                    attention(2, [], at={U + 5 + n: (lambda n=n: first_relu(act, n, REST)) for n in range(FIRST)})
                    act.wait_ge(sem("mix_ps2"), 1)
                    a.activation(t_a[:, :], psum[:, 0, :], ACT.Identity, scale=META_W, bias=mc_bo15[:, :]).then_inc(sem("mix2"), 1)

                @block.gpsimd
                def _(pool):
                    for n in range(FIRST, E * HC):
                        e, hc = n // HC, n % HC
                        pool.wait_ge(sem("h_hi0"), n - FIRST + 1)
                        nc.gpsimd.tensor_tensor(out=h_lo[:, e % 2, hc, :], in0=h32[:, hc, :], in1=h_hi[:, e % 2, hc, :],
                                                op=ALU.subtract).then_inc(sem("h_lo0"), 1)
                    inverse_root(pool, "x1")
                    for name, tmp, w, at, split in (("k32_1", 2, 0, 2, "ksplit1"), ("caq32", 0, 1, 0, "qsplit3"),
                                                    ("cak32", 1, 1, 2, "ksplit3")):
                        pool.wait_ge(sem(name), 1)
                        nc.gpsimd.tensor_tensor(out=parts[:, w, at + 1, :], in0=osb[:, tmp, :], in1=parts[:, w, at, :],
                                                op=ALU.subtract).then_inc(sem(split), 1)
                    for o in range(HC):
                        pool.wait_ge(sem("g_hi"), o + 1)
                        ins = nc.gpsimd.tensor_tensor(out=h_lo[:, 0, o, :], in0=h32[:, o, :], in1=h_hi[:, 0, o, :],
                                                      op=ALU.subtract)
                    ins.then_inc(sem("hsplit1"), 1)

                    def gelu_lo(n, dst):
                        for o in range(HC):
                            pool.wait_ge(sem("gelu_hi"), HC * (n - 1) + o + 1)
                            ins = nc.gpsimd.tensor_tensor(out=h_lo[:, dst, o, :], in0=h32[:, o, :], in1=h_hi[:, dst, o, :],
                                                          op=ALU.subtract)
                        ins.then_inc(sem(f"hsplit{n + 1}"), 1)

                    gelu_lo(1, 1)
                    inverse_root(pool, "x0")
                    inverse_root(pool, "lat")
                    gelu_lo(2, 0)
                    for n in range(FIRST):
                        first_lo(pool, n, REST)

                @block.sync
                def _(sp):
                    def spread_mixing(n, st):
                        sp.wait_ge(sem(f"qsplit{n}"), 1)
                        sp.wait_ge(sem(f"ksplit{n}"), 1)
                        relayed(sp, 1, 0)
                        relayed(sp, 1, 2)
                        if st == 2:
                            sp.wait_ge(sem("trans1"), 2 * NS[1])
                        sp.wait_ge(sem("relay1"), 32 * st)
                        for j, (a, b) in enumerate(((0, 2), (0, 3), (1, 2))):
                            for w, part_ in ((0, a), (1, b)):
                                sp.dma_start(qkc[32 * j:32 * j + 32, w, :, :],
                                             relay[1, part_].rearrange("(h d) t -> d h t", d=MD)).then_inc(sem(f"spread{n}"), 16)

                    def max_rows(st, gr):
                        sp.wait_ge(sem(f"mrow{st}"), gr + 1)
                        if main(st, gr):
                            sp.dma_start(qm[3:P:32, gr, :], mrow[:, gr % 2, :]).then_inc(sem(f"qm{st}_{gr}"), 16)
                        else:
                            for h in range(MH):
                                sp.dma_start(qc[96:97, h, :], mrow[h:h + 1, gr % 2, :]).then_inc(sem(f"qm{st}_{gr}"), 16)

                    sp.wait_ge(sem("x_taken"), 1)
                    load_x(sp, bass.ds(i + 1, 1))
                    for gr in range(NG):
                        max_rows(0, gr)
                    spread_main(sp, 1, 0)
                    spread_mixing(3, 1)
                    for gr in range(NG + 1):
                        max_rows(1, gr)
                    spread_mixing(2, 2)
                    max_rows(2, 0)
                    spread_main(sp, 0, 1)
                    sp.wait_ge(sem("x_out"), 1)
                    sp.dma_start(out[bass.ds(i, 1)].rearrange("b (c p) d -> p (b c) d", p=P), x[:, :, :]).then_inc(sem("stored"), 16)
                    sp.wait_ge(sem("spread0"), 16 * NSPREAD)
                    sp.wait_ge(sem("stored"), 16)

            restart()

def kernel(**inputs):
    import numpy as _np
    import concourse.bacc as _bacc
    from concourse import mybir as _mybir
    from concourse.bass_utils import run_bass_kernel_spmd as _run

    a = {n: _np.asarray(v) for n, v in inputs.items()}
    f32 = _np.float32

    def swapped(w):
        return w.reshape(w.shape[0], NH, 2, HD // 2)[:, :, ::-1].reshape(w.shape[0], 128)

    ca, mc = a["L1_attn_ca_Win"], a["L1_attn_mc_Win"]
    cab, mcb = a["L1_attn_ca_bin"], a["L1_attn_mc_bin"]
    wide = _np.concatenate([
        a["L0_attn_W_q"], swapped(a["L0_attn_W_q"]), a["L0_attn_W_o"], a["L1_attn_Wq"], a["L1_attn_Wk"], a["L1_attn_Wv"],
        _np.repeat(a["L1_attn_cg_W"], HD, axis=1), a["L1_attn_Wo"], ca, a["L1_attn_ca_Wout"], mc, a["L1_attn_mc_Wout"],
        a["L0_attn_W_dkv"], a["L0_ffn_Wg"]], axis=1)
    latw = _np.concatenate([a["L0_attn_W_uk"], swapped(a["L0_attn_W_uk"]), a["L0_attn_W_uv"]], axis=1)

    def column(v):
        return v.reshape(-1, 128).T

    def padded(v):
        z = _np.zeros((128, 1), f32)
        z[:v.shape[0], 0] = v
        return z

    cols = _np.concatenate([
        column(a["L1_attn_bq"]), column(a["L1_attn_bk"]), column(cab[:128]), column(cab[128:256]),
        column(mcb[:128]), column(mcb[128:256]), column(a["L1_attn_ca_bout"]), column(a["L1_attn_mc_bout"]),
        column(_np.repeat(a["L1_attn_cg_b"], HD)), column(_np.repeat(a["L1_attn_am_b"], HD)),
        padded(a["L0_attn_ln_gamma"]), padded(a["L0_attn_ln_beta"]), column(a["L0_ffn_b1"]),
        column(a["L1_ffn_w1_s"]), column(a["L1_ffn_w2_s"]), column(a["L1_ffn_h1_s"]), column(a["L1_ffn_h2_s"])], axis=1)
    rows = _np.concatenate([a["L1_attn_bv"], cab[256:], mcb[256:], a["L1_attn_bo"], a["L1_ffn_w3_s"], a["L0_ffn_bg"]])[None]

    def chunks(w):
        return w.reshape(-1, 128, w.shape[-1]).transpose(1, 0, 2).reshape(128, -1)

    split = _np.concatenate([
        a["L0_ffn_W1"].transpose(1, 0, 2).reshape(128, -1), chunks(a["L0_ffn_W2"].reshape(-1, 128)),
        a["L1_ffn_w1_w"].T, a["L1_ffn_w2_w"].T, chunks(a["L1_ffn_h1_w"].T), chunks(a["L1_ffn_h2_w"].T),
        chunks(a["L1_ffn_w3_w"].T)], axis=1)
    x_in = _np.concatenate([a["L0_attn_x"], a["L0_attn_x"][:1]])
    arrays = dict(x_in=x_in, wide_in=wide, lat_in=latw, cols_in=cols, rows_in=rows, const_in=constants(),
                  split_in=split, am_in=_np.repeat(a["L1_attn_am_W"], HD, axis=1), cons_in=a["L1_attn_cons_vec"][:, None],
                  b2_in=a["L0_ffn_b2"])
    arrays = {n: _np.ascontiguousarray(v) for n, v in arrays.items()}
    nc = _bacc.Bacc("TRN2", target_bir_lowering=False, num_devices=1)
    args = {n: nc.dram_tensor(n, v.shape, _mybir.dt.from_np(v.dtype), kind="ExternalInput").ap() for n, v in arrays.items()}
    out = nc.dram_tensor("out", (B, T, D), F32, kind="ExternalOutput").ap()
    build(nc, out=out, **args)
    r = _run(nc, [arrays], core_ids=[0])
    return r.results[0]["out"]
```
